# Optimizing a Trainium2 kernel written in Bass

```python
import numpy as np
import jax
import jax.numpy as jnp

def _softmax(x, axis=-1):
    return jax.nn.softmax(x, axis=axis)

def _gelu(x):
    return jax.nn.gelu(x, approximate=True)

def _silu(x):
    return jax.nn.silu(x)

def _sigmoid(x):
    return jax.nn.sigmoid(x)

def _layernorm(x, axis=-1, eps=1e-05):
    m = jnp.mean(x, axis=axis, keepdims=True)
    v = jnp.var(x, axis=axis, keepdims=True)
    return (x - m) / jnp.sqrt(v + eps)

def _scatter_add(tgt, idx, src, axis=0):
    return tgt.at[idx].add(src)

def _segment_sum(src, seg, n):
    return jax.ops.segment_sum(src, seg, n)
kernel_name = 'mk_perceiver_d2_seqx_r4_4034c3'

def setup_inputs(seed: int=0):
    np.random.seed(seed)
    _w = jnp.asarray

    def _rec_inputs():
        import jax
        import jax.numpy as jnp
        _rk = jax.random.key(seed)
        x = -0.0005146 + 1 * jax.random.normal(jax.random.fold_in(_rk, 1), (2, 64, 1024), jnp.float32)
        _lenS = 64 - jax.random.randint(jax.random.fold_in(_rk, 7), (2,), 0, max(1, 64 // 4) + 1, jnp.int32)
        _lenS2 = 1024 - jax.random.randint(jax.random.fold_in(_rk, 8), (2,), 0, max(1, 1024 // 4) + 1, jnp.int32)
        _ctx_4096P = jax.random.normal(jax.random.fold_in(_rk, 11), (2, 16, 1024), jnp.float32)
        _ctx_4096c = jax.random.dirichlet(jax.random.fold_in(_rk, 511), 0.3 * jnp.ones((16,), jnp.float32), (2, 1024))
        _ctx_4096t = jnp.einsum('bsk,bkd->bsd', _ctx_4096c, _ctx_4096P)
        _ctx_4096t = _ctx_4096t * jax.lax.rsqrt(jnp.mean(jnp.square(_ctx_4096t)) + 1e-12) * 0.953939
        ctx_4096 = -0.0142356 + 1.00583 * (_ctx_4096t + 0.3 * jax.random.normal(jax.random.fold_in(_rk, 611), (2, 1024, 1024), jnp.float32))
        return (x, ctx_4096)
    x, ctx_4096 = _rec_inputs()

    def _L0_xattn_setup():
        import jax, jax.numpy as jnp
        import numpy as np
        K = 10
        NUM_BITS = 10
        M_METHODS = 4

        def _quantize(coords, num_bits=NUM_BITS):
            cmin = coords.min(axis=1, keepdims=True)
            cmax = coords.max(axis=1, keepdims=True)
            scale = (2 ** num_bits - 1) / (cmax - cmin + 1e-06)
            q = jnp.floor((coords - cmin) * scale)
            return jnp.clip(q, 0, 2 ** num_bits - 1).astype(jnp.int32)

        def _morton_key(q):
            x, y, z = (q[..., 0], q[..., 1], q[..., 2])
            key = jnp.zeros(x.shape, dtype=jnp.int32)
            for b in range(NUM_BITS):
                key = key | (x >> b & 1) << 3 * b + 2 | (y >> b & 1) << 3 * b + 1 | (z >> b & 1) << 3 * b
            return key

        def _hilbert_key(q, num_bits=NUM_BITS):
            n = 3
            X = [q[..., i] for i in range(n)]
            M = 1 << num_bits - 1
            Q = M
            while Q > 1:
                P = Q - 1
                for i in range(n):
                    cond = X[i] & Q > 0
                    t = (X[0] ^ X[i]) & P
                    new_X0 = jnp.where(cond, X[0] ^ P, X[0] ^ t)
                    if i != 0:
                        X[i] = jnp.where(cond, X[i], X[i] ^ t)
                    X[0] = new_X0
                Q >>= 1
            for i in range(1, n):
                X[i] = X[i] ^ X[i - 1]
            t = jnp.zeros_like(X[0])
            Q = M
            while Q > 1:
                t = jnp.where(X[n - 1] & Q > 0, t ^ Q - 1, t)
                Q >>= 1
            X = [xi ^ t for xi in X]
            key = jnp.zeros(X[0].shape, dtype=jnp.int32)
            for b in range(num_bits - 1, -1, -1):
                for i in range(n):
                    key = key << 1 | X[i] >> b & 1
            return key

        def _sorted_indices(coords_bn3):
            q = _quantize(coords_bn3)
            qt = q[..., jnp.array([1, 0, 2])]
            keys = [_morton_key(q), _morton_key(qt), _hilbert_key(q), _hilbert_key(qt)]
            return [jnp.argsort(kk, axis=1) for kk in keys]

        def _window_inds(sorted_idx, k=K):
            B, N = sorted_idx.shape
            i = jnp.arange(N)
            start = jnp.maximum(0, i - k // 2)
            end = jnp.minimum(N, i + k // 2 + 1)
            pos = jnp.minimum(start[:, None] + jnp.arange(k)[None, :], (end - 1)[:, None])
            return jnp.take(sorted_idx, pos, axis=1)

        def _get_graph_features(feats, inds_list, perm, W_lin, b_lin, k=K):
            B, N, C = feats.shape
            center = feats[:, :, None, :]
            gather = jax.vmap(lambda f, idx: f[idx])
            per_method = []
            for inds in inds_list:
                neigh = gather(feats, inds)
                gf = jnp.concatenate([jnp.broadcast_to(center, (B, N, k, C)), neigh - center], axis=-1)
                per_method.append(gf)
            allf = jnp.stack(per_method, axis=-1)
            allf = allf[..., perm]
            total = 2 * C * M_METHODS
            x = allf.reshape(B * N, k, total)
            x16 = x.astype(jnp.float16).astype(jnp.float32)
            headdim = min(64, total)
            nheads = total // headdim
            qh = x16.reshape(B * N, k, nheads, headdim)
            scores = jnp.einsum('bihd,bjhd->bhij', qh, qh) / np.float32(np.sqrt(headdim))
            attn = jax.nn.softmax(scores, axis=-1)
            out = jnp.einsum('bhij,bjhd->bihd', attn, qh).reshape(B * N, k, total)
            fused = out @ W_lin.T + b_lin
            return fused.reshape(B, N, k, 128)

        def _instance_norm(x, axes):
            mu = x.mean(axis=axes, keepdims=True)
            var = x.var(axis=axes, keepdims=True)
            return (x - mu) / jnp.sqrt(var + 1e-05)

        def _lrelu(x):
            return jnp.where(x > 0, x, 0.2 * x)
        key = jax.random.key(seed)
        ks = jax.random.split(key, 8)
        B, N, C = (2, 1024, 64)
        tot = M_METHODS * 2 * C
        s = 0.02
        return {'coords': jax.random.normal(ks[0], (B, 3, N), jnp.float32), 'feats': jax.random.normal(ks[1], (B, C, N), jnp.float32), 'W_lin1': jax.random.normal(ks[2], (128, tot), jnp.float32) * s, 'b_lin1': jnp.zeros((128,), jnp.float32), 'W_lin2': jax.random.normal(ks[3], (128, tot), jnp.float32) * s, 'b_lin2': jnp.zeros((128,), jnp.float32), 'W_conv1': jax.random.normal(ks[4], (C, 2 * C), jnp.float32) * s, 'W_conv2': jax.random.normal(ks[5], (2 * C, 2 * C), jnp.float32) * s, 'W_conv3': jax.random.normal(ks[6], (C, 4 * C), jnp.float32) * s}
    _L0_xattn_all = _L0_xattn_setup()
    _L0_xattn_in = {k: v for k, v in _L0_xattn_all.items() if k in ('W_lin1', 'b_lin1', 'W_lin2', 'b_lin2', 'W_conv1', 'W_conv2', 'W_conv3')}
    del _L0_xattn_all

    def _L0_attn_setup():
        import jax, jax.numpy as jnp
        import numpy as np
        N_HEADS = 16
        HEAD_DIM = 64
        ROTARY_DIM = 64
        MASKED_BIAS = -1000000000.0

        def _rotate_every_two(x):
            x1 = x[..., ::2]
            x2 = x[..., 1::2]
            return jnp.stack((-x2, x1), axis=-1).reshape(x.shape)

        def _sincos(seq_len, dim, dtype):
            inv_freq = 1.0 / 10000.0 ** (jnp.arange(0, dim, 2, dtype=jnp.float32) / dim)
            ang = jnp.einsum('i,j->ij', jnp.arange(seq_len, dtype=jnp.float32), inv_freq)
            sin = jnp.repeat(jnp.sin(ang), 2, axis=-1).astype(dtype)
            cos = jnp.repeat(jnp.cos(ang), 2, axis=-1).astype(dtype)
            return (sin[None, :, None, :], cos[None, :, None, :])
        key = jax.random.key(seed)
        ks = jax.random.split(key, 5)
        B, S, D = (2, 512, 1024)
        sc = 0.02
        return {'hidden_states': jax.random.normal(ks[0], (B, S, D), jnp.float32), 'wq': jax.random.normal(ks[1], (D, D), jnp.float32) * sc, 'wk': jax.random.normal(ks[2], (D, D), jnp.float32) * sc, 'wv': jax.random.normal(ks[3], (D, D), jnp.float32) * sc, 'wo': jax.random.normal(ks[4], (D, D), jnp.float32) * sc}
    _L0_attn_all = _L0_attn_setup()
    _L0_attn_in = {k: v for k, v in _L0_attn_all.items() if k in ('wq', 'wk', 'wv', 'wo')}
    del _L0_attn_all

    def _L0_ffn_setup():
        import jax, jax.numpy as jnp
        import numpy as np
        B, S, D, O, E, R = (4, 512, 1024, 1024, 8, 16)
        SCALING = 32.0 / 16.0
        MAX_THRESHOLD = 0.125
        key = jax.random.key(seed)
        ks = jax.random.split(key, 8)
        return {'x': jax.random.normal(ks[0], (B, S, D), jnp.float32), 'W_base': jax.random.normal(ks[1], (O, D), jnp.float32) * (1.0 / np.sqrt(D)), 'b_base': jax.random.normal(ks[2], (O,), jnp.float32) * 0.02, 'W_gate': jax.random.normal(ks[3], (E, D), jnp.float32) * (1.0 / np.sqrt(D)), 'W_thr': jax.random.normal(ks[4], (D,), jnp.float32) * (1.0 / np.sqrt(D)), 'b_thr': jax.random.normal(ks[5], (1,), jnp.float32) * 0.02, 'A_w': jax.random.normal(ks[6], (E, R, D), jnp.float32) * (1.0 / np.sqrt(D)), 'B_w': jax.random.normal(ks[7], (E, O, R), jnp.float32) * (1.0 / np.sqrt(R))}
    _L0_ffn_all = _L0_ffn_setup()
    _L0_ffn_in = {k: v for k, v in _L0_ffn_all.items() if k in ('W_base', 'b_base', 'W_gate', 'W_thr', 'b_thr', 'A_w', 'B_w')}
    del _L0_ffn_all

    def _L1_xattn_setup():
        import jax, jax.numpy as jnp
        import numpy as np
        import math
        HIDDEN = 1024
        N_HEADS = 32
        HEAD_DIM = 128
        N_KV_HEADS = 4
        N_GROUPS = N_HEADS // N_KV_HEADS
        key = jax.random.key(seed)
        ks = jax.random.split(key, 6)
        B, NL, S = (8, 64, 1024)
        latents = jax.random.normal(ks[0], (B, NL, HIDDEN), dtype=jnp.float32)
        context = jax.random.normal(ks[1], (B, S, HIDDEN), dtype=jnp.float32)
        scale = 1.0 / math.sqrt(HIDDEN)
        Wq = jax.random.normal(ks[2], (HIDDEN, N_HEADS * HEAD_DIM), dtype=jnp.float32) * scale
        Wk = jax.random.normal(ks[3], (HIDDEN, N_KV_HEADS * HEAD_DIM), dtype=jnp.float32) * scale
        Wv = jax.random.normal(ks[4], (HIDDEN, N_KV_HEADS * HEAD_DIM), dtype=jnp.float32) * scale
        Wo = jax.random.normal(ks[5], (N_HEADS * HEAD_DIM, HIDDEN), dtype=jnp.float32) * scale
        return {'latents': latents, 'context': context, 'Wq': Wq, 'Wk': Wk, 'Wv': Wv, 'Wo': Wo}
    _L1_xattn_all = _L1_xattn_setup()
    _L1_xattn_in = {k: v for k, v in _L1_xattn_all.items() if k in ('Wq', 'Wk', 'Wv', 'Wo')}
    del _L1_xattn_all

    def _L1_attn_setup():
        import jax, jax.numpy as jnp
        import numpy as np
        NUM_HEADS = 32
        NUM_KV_HEADS = 8
        HEAD_DIM = 128
        key = jax.random.key(seed)
        ks = jax.random.split(key, 5)
        B, S, H = (2, 512, 1024)
        scale = 0.02
        return {'x': jax.random.normal(ks[0], (B, S, H), dtype=jnp.float32), 'wq': jax.random.normal(ks[1], (NUM_HEADS * HEAD_DIM, H), dtype=jnp.float32) * scale, 'wk': jax.random.normal(ks[2], (NUM_KV_HEADS * HEAD_DIM, H), dtype=jnp.float32) * scale, 'wv': jax.random.normal(ks[3], (NUM_KV_HEADS * HEAD_DIM, H), dtype=jnp.float32) * scale, 'wo': jax.random.normal(ks[4], (H, NUM_HEADS * HEAD_DIM), dtype=jnp.float32) * scale}
    _L1_attn_all = _L1_attn_setup()
    _L1_attn_in = {k: v for k, v in _L1_attn_all.items() if k in ('wq', 'wk', 'wv', 'wo')}
    del _L1_attn_all

    def _L1_ffn_setup():
        import jax, jax.numpy as jnp
        import numpy as np
        K_TOP = 8
        key = jax.random.key(seed)
        k1, k2, k3 = jax.random.split(key, 3)
        B, S, H, E = (4, 1024, 1024, 64)
        hidden_states = jax.random.normal(k1, (B, S, H), dtype=jnp.float32)
        router_weight = jax.random.normal(k2, (E, H), dtype=jnp.float32)
        router_bias = jnp.zeros((E,), dtype=jnp.float32)
        expert_bias = jax.random.normal(k3, (E, H), dtype=jnp.float32) * 0.1
        return {'hidden_states': hidden_states, 'router_weight': router_weight, 'router_bias': router_bias, 'expert_bias': expert_bias}
    _L1_ffn_all = _L1_ffn_setup()
    _L1_ffn_in = {k: v for k, v in _L1_ffn_all.items() if k in ('router_weight', 'router_bias', 'expert_bias')}
    del _L1_ffn_all
    return {'x': x, 'ctx_4096': ctx_4096, 'L0_xattn_W_lin1': _L0_xattn_in['W_lin1'], 'L0_xattn_b_lin1': _L0_xattn_in['b_lin1'], 'L0_xattn_W_lin2': _L0_xattn_in['W_lin2'], 'L0_xattn_b_lin2': _L0_xattn_in['b_lin2'], 'L0_xattn_W_conv1': _L0_xattn_in['W_conv1'], 'L0_xattn_W_conv2': _L0_xattn_in['W_conv2'], 'L0_xattn_W_conv3': _L0_xattn_in['W_conv3'], 'L0_attn_wq': _L0_attn_in['wq'], 'L0_attn_wk': _L0_attn_in['wk'], 'L0_attn_wv': _L0_attn_in['wv'], 'L0_attn_wo': _L0_attn_in['wo'], 'L0_ffn_W_base': _L0_ffn_in['W_base'], 'L0_ffn_b_base': _L0_ffn_in['b_base'], 'L0_ffn_W_gate': _L0_ffn_in['W_gate'], 'L0_ffn_W_thr': _L0_ffn_in['W_thr'], 'L0_ffn_b_thr': _L0_ffn_in['b_thr'], 'L0_ffn_A_w': _L0_ffn_in['A_w'], 'L0_ffn_B_w': _L0_ffn_in['B_w'], 'L1_xattn_Wq': _L1_xattn_in['Wq'], 'L1_xattn_Wk': _L1_xattn_in['Wk'], 'L1_xattn_Wv': _L1_xattn_in['Wv'], 'L1_xattn_Wo': _L1_xattn_in['Wo'], 'L1_attn_wq': _L1_attn_in['wq'], 'L1_attn_wk': _L1_attn_in['wk'], 'L1_attn_wv': _L1_attn_in['wv'], 'L1_attn_wo': _L1_attn_in['wo'], 'L1_ffn_router_weight': _L1_ffn_in['router_weight'], 'L1_ffn_router_bias': _L1_ffn_in['router_bias'], 'L1_ffn_expert_bias': _L1_ffn_in['expert_bias']}

def reference(x, ctx_4096, L0_xattn_W_lin1, L0_xattn_b_lin1, L0_xattn_W_lin2, L0_xattn_b_lin2, L0_xattn_W_conv1, L0_xattn_W_conv2, L0_xattn_W_conv3, L0_attn_wq, L0_attn_wk, L0_attn_wv, L0_attn_wo, L0_ffn_W_base, L0_ffn_b_base, L0_ffn_W_gate, L0_ffn_W_thr, L0_ffn_b_thr, L0_ffn_A_w, L0_ffn_B_w, L1_xattn_Wq, L1_xattn_Wk, L1_xattn_Wv, L1_xattn_Wo, L1_attn_wq, L1_attn_wk, L1_attn_wv, L1_attn_wo, L1_ffn_router_weight, L1_ffn_router_bias, L1_ffn_expert_bias):
    import jax
    import jax.numpy as jnp

    def _L0_xattn_ref(coords, feats, W_lin1, b_lin1, W_lin2, b_lin2, W_conv1, W_conv2, W_conv3):
        import jax, jax.numpy as jnp
        import numpy as np
        K = 10
        NUM_BITS = 10
        M_METHODS = 4

        def _quantize(coords, num_bits=NUM_BITS):
            cmin = coords.min(axis=1, keepdims=True)
            cmax = coords.max(axis=1, keepdims=True)
            scale = (2 ** num_bits - 1) / (cmax - cmin + 1e-06)
            q = jnp.floor((coords - cmin) * scale)
            return jnp.clip(q, 0, 2 ** num_bits - 1).astype(jnp.int32)

        def _morton_key(q):
            x, y, z = (q[..., 0], q[..., 1], q[..., 2])
            key = jnp.zeros(x.shape, dtype=jnp.int32)
            for b in range(NUM_BITS):
                key = key | (x >> b & 1) << 3 * b + 2 | (y >> b & 1) << 3 * b + 1 | (z >> b & 1) << 3 * b
            return key

        def _hilbert_key(q, num_bits=NUM_BITS):
            n = 3
            X = [q[..., i] for i in range(n)]
            M = 1 << num_bits - 1
            Q = M
            while Q > 1:
                P = Q - 1
                for i in range(n):
                    cond = X[i] & Q > 0
                    t = (X[0] ^ X[i]) & P
                    new_X0 = jnp.where(cond, X[0] ^ P, X[0] ^ t)
                    if i != 0:
                        X[i] = jnp.where(cond, X[i], X[i] ^ t)
                    X[0] = new_X0
                Q >>= 1
            for i in range(1, n):
                X[i] = X[i] ^ X[i - 1]
            t = jnp.zeros_like(X[0])
            Q = M
            while Q > 1:
                t = jnp.where(X[n - 1] & Q > 0, t ^ Q - 1, t)
                Q >>= 1
            X = [xi ^ t for xi in X]
            key = jnp.zeros(X[0].shape, dtype=jnp.int32)
            for b in range(num_bits - 1, -1, -1):
                for i in range(n):
                    key = key << 1 | X[i] >> b & 1
            return key

        def _sorted_indices(coords_bn3):
            q = _quantize(coords_bn3)
            qt = q[..., jnp.array([1, 0, 2])]
            keys = [_morton_key(q), _morton_key(qt), _hilbert_key(q), _hilbert_key(qt)]
            return [jnp.argsort(kk, axis=1) for kk in keys]

        def _window_inds(sorted_idx, k=K):
            B, N = sorted_idx.shape
            i = jnp.arange(N)
            start = jnp.maximum(0, i - k // 2)
            end = jnp.minimum(N, i + k // 2 + 1)
            pos = jnp.minimum(start[:, None] + jnp.arange(k)[None, :], (end - 1)[:, None])
            return jnp.take(sorted_idx, pos, axis=1)

        def _get_graph_features(feats, inds_list, perm, W_lin, b_lin, k=K):
            B, N, C = feats.shape
            center = feats[:, :, None, :]
            gather = jax.vmap(lambda f, idx: f[idx])
            per_method = []
            for inds in inds_list:
                neigh = gather(feats, inds)
                gf = jnp.concatenate([jnp.broadcast_to(center, (B, N, k, C)), neigh - center], axis=-1)
                per_method.append(gf)
            allf = jnp.stack(per_method, axis=-1)
            allf = allf[..., perm]
            total = 2 * C * M_METHODS
            x = allf.reshape(B * N, k, total)
            x16 = x.astype(jnp.float16).astype(jnp.float32)
            headdim = min(64, total)
            nheads = total // headdim
            qh = x16.reshape(B * N, k, nheads, headdim)
            scores = jnp.einsum('bihd,bjhd->bhij', qh, qh) / np.float32(np.sqrt(headdim))
            attn = jax.nn.softmax(scores, axis=-1)
            out = jnp.einsum('bhij,bjhd->bihd', attn, qh).reshape(B * N, k, total)
            fused = out @ W_lin.T + b_lin
            return fused.reshape(B, N, k, 128)

        def _instance_norm(x, axes):
            mu = x.mean(axis=axes, keepdims=True)
            var = x.var(axis=axes, keepdims=True)
            return (x - mu) / jnp.sqrt(var + 1e-05)

        def _lrelu(x):
            return jnp.where(x > 0, x, 0.2 * x)
        inds_sorted = _sorted_indices(coords.transpose(0, 2, 1))
        inds_list = [_window_inds(s) for s in inds_sorted]
        perm1 = jnp.array([2, 0, 3, 1])
        perm2 = jnp.array([1, 3, 0, 2])
        f0 = feats.transpose(0, 2, 1)
        g1 = _get_graph_features(f0, inds_list, perm1, W_lin1, b_lin1)
        h1 = jnp.einsum('oc,bnkc->bonk', W_conv1, g1)
        h1 = _lrelu(_instance_norm(h1, (2, 3)))
        feats1 = h1.max(axis=-1)
        g2 = _get_graph_features(feats1.transpose(0, 2, 1), inds_list, perm2, W_lin2, b_lin2)
        h2 = jnp.einsum('oc,bnkc->bonk', W_conv2, g2)
        h2 = _lrelu(_instance_norm(h2, (2, 3)))
        feats2 = h2.max(axis=-1)
        f3 = jnp.concatenate([feats, feats1, feats2], axis=1)
        h3 = jnp.einsum('oc,bcn->bon', W_conv3, f3)
        return _lrelu(_instance_norm(h3, (2,)))

    def _L0_attn_ref(hidden_states, wq, wk, wv, wo):
        import jax, jax.numpy as jnp
        import numpy as np
        N_HEADS = 16
        HEAD_DIM = 64
        ROTARY_DIM = 64
        MASKED_BIAS = -1000000000.0

        def _rotate_every_two(x):
            x1 = x[..., ::2]
            x2 = x[..., 1::2]
            return jnp.stack((-x2, x1), axis=-1).reshape(x.shape)

        def _sincos(seq_len, dim, dtype):
            inv_freq = 1.0 / 10000.0 ** (jnp.arange(0, dim, 2, dtype=jnp.float32) / dim)
            ang = jnp.einsum('i,j->ij', jnp.arange(seq_len, dtype=jnp.float32), inv_freq)
            sin = jnp.repeat(jnp.sin(ang), 2, axis=-1).astype(dtype)
            cos = jnp.repeat(jnp.cos(ang), 2, axis=-1).astype(dtype)
            return (sin[None, :, None, :], cos[None, :, None, :])
        B, S, D = hidden_states.shape
        H, hd, rd = (N_HEADS, HEAD_DIM, ROTARY_DIM)
        q = (hidden_states @ wq.T).reshape(B, S, H, hd)
        k = (hidden_states @ wk.T).reshape(B, S, H, hd)
        v = (hidden_states @ wv.T).reshape(B, S, H, hd)
        sin, cos = _sincos(S, rd, hidden_states.dtype)
        q_rot, q_pass = (q[..., :rd], q[..., rd:])
        k_rot, k_pass = (k[..., :rd], k[..., rd:])
        q_rot = q_rot * cos + _rotate_every_two(q_rot) * sin
        k_rot = k_rot * cos + _rotate_every_two(k_rot) * sin
        q = jnp.concatenate([q_rot, q_pass], axis=-1)
        k = jnp.concatenate([k_rot, k_pass], axis=-1)
        q = q.transpose(0, 2, 1, 3).astype(jnp.float32)
        k = k.transpose(0, 2, 1, 3).astype(jnp.float32)
        v = v.transpose(0, 2, 1, 3)
        aw = jnp.einsum('bhqd,bhkd->bhqk', q, k)
        causal = jnp.tril(jnp.ones((S, S), dtype=bool))[None, None]
        aw = jnp.where(causal, aw, jnp.float32(MASKED_BIAS))
        aw = aw / jnp.sqrt(jnp.float32(hd))
        aw = jax.nn.softmax(aw, axis=-1).astype(v.dtype)
        out = jnp.einsum('bhqk,bhkd->bhqd', aw, v)
        out = out.transpose(0, 2, 1, 3).reshape(B, S, D)
        return out @ wo.T

    def _L0_ffn_ref(x, W_base, b_base, W_gate, W_thr, b_thr, A_w, B_w):
        import jax, jax.numpy as jnp
        import numpy as np
        B, S, D, O, E, R = (4, 512, 1024, 1024, 8, 16)
        SCALING = 32.0 / 16.0
        MAX_THRESHOLD = 0.125
        base = jnp.einsum('bsd,od->bso', x, W_base) + b_base
        xf = x.reshape(-1, D)
        gate = jax.nn.softmax(xf @ W_gate.T, axis=-1)
        thr = jax.nn.sigmoid(xf @ W_thr + b_thr[0]) * MAX_THRESHOLD
        adapted = gate - thr[:, None]
        selected = (adapted >= 0).astype(x.dtype)
        w = adapted * selected
        wsum = jnp.sum(w, axis=-1, keepdims=True)
        wsum = jnp.where(wsum == 0, jnp.ones_like(wsum), wsum)
        w = w / wsum
        h = jnp.einsum('nd,erd->ner', xf, A_w)
        moe = jnp.einsum('ner,ne,eor->no', h, w, B_w) * SCALING
        return base + moe.reshape(base.shape)

    def _L1_xattn_ref(latents, context, Wq, Wk, Wv, Wo):
        import jax, jax.numpy as jnp
        import numpy as np
        import math
        HIDDEN = 1024
        N_HEADS = 32
        HEAD_DIM = 128
        N_KV_HEADS = 4
        N_GROUPS = N_HEADS // N_KV_HEADS
        b, q_len, _ = latents.shape
        kv_len = q_len + context.shape[1]
        hidden_states = jnp.concatenate([context, latents], axis=1)
        q = (latents @ Wq).reshape(b, q_len, N_KV_HEADS, N_GROUPS, HEAD_DIM)
        k = (hidden_states @ Wk).reshape(b, kv_len, N_KV_HEADS, HEAD_DIM)
        v = (hidden_states @ Wv).reshape(b, kv_len, N_KV_HEADS, HEAD_DIM)
        scale = 1.0 / math.sqrt(HEAD_DIM)
        scores = jnp.einsum('bqhgd,bkhd->bhgqk', q, k) * scale
        attn = jax.nn.softmax(scores.astype(jnp.float32), axis=-1).astype(q.dtype)
        out = jnp.einsum('bhgqk,bkhd->bqhgd', attn, v)
        out = out.reshape(b, q_len, N_HEADS * HEAD_DIM)
        return out @ Wo

    def _L1_attn_ref(x, wq, wk, wv, wo):
        import jax, jax.numpy as jnp
        import numpy as np
        NUM_HEADS = 32
        NUM_KV_HEADS = 8
        HEAD_DIM = 128
        B, S, H = x.shape
        g = NUM_HEADS // NUM_KV_HEADS
        q = (x @ wq.T).reshape(B, S, NUM_KV_HEADS, g, HEAD_DIM)
        k = (x @ wk.T).reshape(B, S, NUM_KV_HEADS, HEAD_DIM)
        v = (x @ wv.T).reshape(B, S, NUM_KV_HEADS, HEAD_DIM)
        scores = jnp.einsum('bqgrd,bkgd->bgrqk', q, k) / np.float32(np.sqrt(HEAD_DIM))
        probs = jax.nn.softmax(scores.astype(jnp.float32), axis=-1).astype(q.dtype)
        out = jnp.einsum('bgrqk,bkgd->bqgrd', probs, v).reshape(B, S, NUM_HEADS * HEAD_DIM)
        return out @ wo.T

    def _L1_ffn_ref(hidden_states, router_weight, router_bias, expert_bias):
        import jax, jax.numpy as jnp
        import numpy as np
        K_TOP = 8
        B, S, H = hidden_states.shape
        E = router_weight.shape[0]
        T = B * S
        flat = hidden_states.reshape(T, H)
        logits = jnp.einsum('th,eh->te', flat, router_weight) + router_bias
        scores = jax.nn.softmax(logits, axis=-1)
        topk_w, topk_idx = jax.lax.top_k(scores, K_TOP)
        w_sum = topk_w.sum(axis=-1, keepdims=True)
        w_dense = jnp.zeros((T, E), dtype=scores.dtype).at[jnp.arange(T)[:, None], topk_idx].add(topk_w)
        bias_mix = jnp.einsum('te,eh->th', w_dense, expert_bias)
        out = flat * w_sum + bias_mix
        return out.reshape(B, S, H)
    x = x + _L0_xattn_ref(ctx_4096, _layernorm(x, axis=-1), L0_xattn_W_lin1, L0_xattn_b_lin1, L0_xattn_W_lin2, L0_xattn_b_lin2, L0_xattn_W_conv1, L0_xattn_W_conv2, L0_xattn_W_conv3)
    x = x + _L0_attn_ref(_layernorm(x, axis=-1), L0_attn_wq, L0_attn_wk, L0_attn_wv, L0_attn_wo)
    x = x + _L0_ffn_ref(_layernorm(x, axis=-1), L0_ffn_W_base, L0_ffn_b_base, L0_ffn_W_gate, L0_ffn_W_thr, L0_ffn_b_thr, L0_ffn_A_w, L0_ffn_B_w)
    x = x + _L1_xattn_ref(_layernorm(x, axis=-1), ctx_4096, L1_xattn_Wq, L1_xattn_Wk, L1_xattn_Wv, L1_xattn_Wo)
    x = x + _L1_attn_ref(_layernorm(x, axis=-1), L1_attn_wq, L1_attn_wk, L1_attn_wv, L1_attn_wo)
    x = x + _L1_ffn_ref(_layernorm(x, axis=-1), L1_ffn_router_weight, L1_ffn_router_bias, L1_ffn_expert_bias)
    return x

_drawn_inputs = setup_inputs


def setup_inputs(seed=0):
    import zlib

    import numpy as np

    out = dict(_drawn_inputs(seed))
    spreads = {'L0_xattn_b_lin1': (0.0, 0.8),
     'L0_xattn_b_lin2': (0.0, 0.8),
     'L1_ffn_router_bias': (0.0, 0.8)}
    factors = {'L0_ffn_b_base': 6.4, 'L1_attn_wq': 3.203, 'L1_attn_wk': 3.166}
    for name, (base, spread) in spreads.items():
        noise = np.random.default_rng([zlib.crc32(name.encode()), seed]).standard_normal(out[name].shape)
        drawn = base * np.exp(spread * noise) if base else spread * noise
        out[name] = jnp.asarray(drawn.astype(out[name].dtype))
    for name, factor in factors.items():
        out[name] = (out[name] * factor).astype(out[name].dtype)
    return out
```

```python
from contextlib import ExitStack

import concourse.bass as bass
from concourse import mybir

F32 = mybir.dt.float32
F16 = mybir.dt.float16
I32 = mybir.dt.int32
U32 = mybir.dt.uint32
ALU = mybir.AluOpType
ACT = mybir.ActivationFunctionType
AX = mybir.AxisListType

P = 128
B, C, N = 2, 64, 1024
NBLK = N // P
METHODS = 4
KW = 10
GP = 12
GROWS = GP * KW
BP = 2 * GP
BCOLS = BP * KW
BODIES = -(-N // BP)
TAIL_NEW = N - (BODIES - 1) * BP
RUNS = 2 * B
OUTC = (64, 128)
BIG = 2.0 ** 30
EPS = 1e-5
KT = N // P
KV = N + C
CHUNK = 4096
SLOTS = 3
ARENA = 18960


WEIGHTS = (["aq0", "aq1", "ak0", "ak1", "av0", "av1", "ao0", "ao1", "base0", "base1"]
           + [f"xq{i}" for i in range(8)] + ["xk", "xv"] + [f"xo{i}" for i in range(8)]
           + [f"sq{i}" for i in range(8)] + ["sk0", "sk1", "sv0", "sv1"] + [f"so{i}" for i in range(8)])
PROJ = (["aq0", "aq1", "ak0", "ak1", "av0", "av1", "gates"] + [f"xq{i}" for i in range(8)] + ["xk", "xv_b0", "xv_b1"]
        + [f"sq{i}" for i in range(8)] + ["sk0", "sk1", "sv0", "sv1", "route"])
GATES = 128 + 8 + 1
TURNS = (["aq0", "aq1", "ak0", "ak1"] + [f"xq{i}" for i in range(8)] + [f"sq{i}" for i in range(8)] + ["sk0", "sk1"])
AGROUPS = 4
SGROUPS = 8
XTILES = 32
KVT = 9


def build(nc, a, out):
    ctx = ExitStack()
    with ctx:
        def sb(name, shape, dt):
            return ctx.enter_context(nc.sbuf_tensor(name, shape, dt))

        def sem(name):
            return ctx.enter_context(nc.semaphore(name))

        def dram(name, shape, dt=F32):
            return nc.dram_tensor(name, shape, dt, kind="Internal").ap()

        x = sb("x", [P, N], F32)
        ident = sb("ident", [P, P], F32)
        identh = sb("identh", [P, P], F16)
        ring = sb("ring", [P, SLOTS, CHUNK], F32)
        keysT = sb("keysT", [P, 4, B * KV], F32)
        vals = sb("vals", [P, B * NBLK, 512], F32)
        small = sb("small", [P, 64], F32)
        bstat = sb("bstat", [P, BODIES, 6], F32)
        arena = sb("arena", [P, ARENA], F32)
        used = [0]

        def take(n, dt=F32):
            lo = used[0]
            used[0] += n
            assert used[0] <= ARENA, used[0]
            return arena[:, lo:lo + n]

        FSW = N + 12
        p_all = take(2 * 8 * GROWS)
        pt_all = take(2 * 8 * GROWS)
        vs_all = take(2 * 2 * 256)
        keyrow = arena[:, 0:4 * N].rearrange("p (m n) -> p m n", m=4)
        p_sb = p_all.rearrange("p (k g n) -> p k g n", k=2, g=8)
        pt_sb = pt_all.rearrange("p (k g n) -> p k g n", k=2, g=8)
        vs_sb = vs_all.rearrange("p (k g n) -> p k g n", k=2, g=2)
        o_off = used[0]
        o_sb = take(2 * 2 * BCOLS).rearrange("p (k t n) -> p k t n", k=2, t=2)
        hs = take(2 * BCOLS).rearrange("p (k n) -> p k n", k=2)
        xt = take(2 * BCOLS).bitcast(F16).rearrange("p (k t n) -> p k t n", k=2, t=2)
        fs_off = used[0]
        fs = take(2 * FSW).rearrange("p (t n) -> p t n", t=2)
        fc_off = used[0]
        fc = take(2 * N).rearrange("p (t n) -> p t n", t=2)
        fsr_off = used[0]
        fsr = take(NBLK * METHODS * C).rearrange("p (k c) -> p k c", c=C)
        fn = take(NBLK * P).rearrange("p (k c) -> p k c", k=NBLK)
        f0 = take(N)
        hc_off = used[0]
        hc = take(N)
        mx_off = used[0]
        mx = take(N)
        fsp = arena[:, hc_off:hc_off + 2 * N].rearrange("p (k n) -> p k n", k=NBLK)
        c16 = take(256).bitcast(F16)
        c32 = take(512)
        fh = take(2 * 5 * KW).rearrange("p (t n k) -> p t n k", t=2, n=5)
        junk = take(N).bitcast(F16).rearrange("p (k n) -> p k n", k=2)
        f2 = fsr.rearrange("p k c -> p (k c)")[:, 0:N]
        g01 = fsr.rearrange("p k c -> p (k c)")[:, N:2 * N]

        def scratch(lo, n, dt=F32):
            return arena[:, o_off + lo:o_off + lo + n].bitcast(dt)

        spot = [0]

        def place(n, *dims):
            lo = spot[0]
            spot[0] += n
            assert spot[0] <= ARENA, spot[0]
            return arena[:, lo:lo + n]

        def heads(ap, n):
            return ap.rearrange("p (h n) -> p h n", n=n)

        hn = place(N)
        hT = heads(place(N), P)
        common = spot[0]
        aq, ak, av, rot = place(N), place(N), place(N), place(N)
        aqT, akT, aoT = heads(place(N), P), heads(place(N), P), heads(place(N), P)
        gp = place(2 * 512).rearrange("p (k h n) -> p k h n", k=2, h=4)
        gpT = place(2 * 512).rearrange("p (k h n) -> p k h n", k=2, h=4)
        cosn, sinn, causal = place(64), place(64), place(P)
        wgate = place(KT * GATES).rearrange("p (k n) -> p k n", k=KT)
        lora_b, bbase = place(N), place(N)
        gates, lora, loraT, bthr = place(GATES + 1), place(P), place(P), place(1)
        spot[0] = common
        sq = place(4 * N)
        soT = heads(sq, P)
        xqT = place(4 * N).rearrange("p (b h n) -> p b h n", b=B, h=32)
        sqT = heads(arena[:, common + 4 * N:common + 8 * N], P)
        shared = spot[0]
        vlat = place(2 * 512).rearrange("p (b n) -> p b n", b=B)
        xp = place(2 * KV).rearrange("p (k n) -> p k n", k=2)
        xpT = place(2 * KVT * P).rearrange("p (k t n) -> p k t n", k=2, t=KVT)
        spot[0] = shared
        sk, sv, skT = place(N), place(N), heads(place(N), P)
        sp_ = place(2 * 512).rearrange("p (k h n) -> p k h n", k=2, h=4)
        spT = place(2 * 512).rearrange("p (k h n) -> p k h n", k=2, h=4)
        samebatch = place(P)
        wroute = place(KT * 64).rearrange("p (k n) -> p k n", k=KT)
        ebias, rbias = place(N), place(64)
        route = place(5 * 64).rearrange("p (k n) -> p k n", k=5)
        rT = place(P)
        gsum = sb("gsum", [P, 2, 4, 4], F32)
        xsum = sb("xsum", [P, 2, 8], F32)
        tiny = sb("tiny", [P, 40], F32)

        coord, quant, qtmp = (scratch(48 * i, 48).rearrange("p (i n) -> p i n", i=3) for i in range(3))
        qint = scratch(144, 48, I32).rearrange("p (i n) -> p i n", i=3)
        bits = scratch(192, 192, I32).rearrange("p (i m n) -> p i m n", i=3, m=METHODS)
        spread = scratch(384, 192, I32).rearrange("p (i m n) -> p i m n", i=3, m=METHODS)
        bt = scratch(576, 160, I32).rearrange("p (i n) -> p i n", i=5)
        key = sb("key", [P, 64], I32)
        expo = sb("expo", [P, 64], I32)
        ext = sb("ext", [P, 4, 6], F32)
        keycol = sb("keycol", [64, P], F32)
        cnt = sb("cnt", [P, 3, 64], F32)
        ranks = sb("ranks", [P, 64], F32)
        rankoff = sb("rankoff", [P, 64], F32)
        rowidx = sb("rowidx", [P, 64], U32)
        lower = sb("lower", [P, P], F32)
        maskl = sb("maskl", [P, GROWS], F16)
        maskr = sb("maskr", [P, 4 * GROWS], F16)
        wlin_n = sb("wlin_n", [P, 2, 256], F32)
        wlin_c = sb("wlin_c", [P, 2, 256], F32)
        blin = sb("blin", [P, 2], F32)
        wconv = [sb(f"wconv{l}", [P, OUTC[l]], F32) for l in range(2)]
        wconv3 = sb("wconv3", [P, 2, 64], F32)
        wp = [sb(f"wp{l}", [P, 2, OUTC[l]], F32) for l in range(2)]
        wc = [sb(f"wc{l}", [P, 2, OUTC[l]], F32) for l in range(2)]
        cb = sb("cb", [P, 2], F32)
        negmax = sb("negmax", [P, 2, 2, 8], F32)
        rsum = sb("rsum", [P, 2, 2, 8], F32)

        ps_s = ctx.enter_context(nc.psum_tensor("ps_s", [P, 2, 512], F32))
        ps_pt = ctx.enter_context(nc.psum_tensor("ps_pt", [P, 2, 512], F32))
        ps_v = ctx.enter_context(nc.psum_tensor("ps_v", [P, 2, 512], F16))
        ps_o = ctx.enter_context(nc.psum_tensor("ps_o", [P, 512], F32))
        ps_h = ctx.enter_context(nc.psum_tensor("ps_h", [P, 512], F32))
        ps_f = ctx.enter_context(nc.psum_tensor("ps_f", [P, 512], F32))

        y_ps = (ps_v[:].rearrange("p g n -> p (g n)").bitcast(F32), ps_f[:])
        proj_bank = (ps_o, ps_h)

        keys_d = dram("keys_d", (64, P))
        feat_d = [dram(f"feat_d{l}", (P, N)) for l in range(2)]
        sorted_d = [dram(f"sorted_d{r}", (METHODS * N, C)) for r in range(RUNS)]

        names = ("x_in coord_in const_in vchain minmax_ready minmax_all pow_ready pow_done ln_ready feat_out0 "
                 "keyT_ps keycol_ready keys_out keyrow_in keyrow_free rank_ready fnT_ps fnT_ev "
                 "fsr_in fsT_ps fsT_ev fc_in fh_ready wp_ps wp_ev c16_ready hc_ps hc_ready "
                 "counted key_ready fsp_ready stats_ready h3_out ctx_ps ctx_ev "
                 "xt_ready s_done v_done t_done pv_done w_done rowmax negmax_ready exp_done recip_ready norm_done "
                 "v_ev pt_ev o_ev h_read feat_ready feat_out g01_in h3_ps x1_ready x_ready out_done "
                 "late_in late2_in hn_ready hT_ps hT_ev w_used proj_ps proj_ev rope_ready turn_ps turn_ev "
                 "g_s g_masked g_max g_negmax g_exp g_recip g_norm g_t g_tev g_pv g_oev "
                 "t_s t_max t_exp t_norm t_t t_tev t_pv t_oev y_ps gate_max gate_exp gate_ready gateT_ps gateT_ev "
                 "route_max route_exp route_ready routeT_ps routeT_ev dchain").split()
        S = {n: sem(n) for n in names}
        scattered = [sem(f"scattered{r}") for r in range(RUNS)]
        slot_in = [sem(f"slot_in{i}") for i in range(SLOTS)]

        plan = [("xk", 0, 0), ("xv", 1, 0), ("ctx0", 2, 0), ("ctx1", 2, 1), ("ctx2", 2, 2), ("ctx3", 2, 3)]
        loads = {}
        nctx = len(plan)
        stream_row = {nm: i for i, nm in enumerate(["xk", "xv", "ctx0", "ctx1", "ctx2", "ctx3"]
                                                   + [n for n in WEIGHTS if n not in ("xk", "xv")])}
        plan = plan + [(nm, i % SLOTS, None) for i, nm in enumerate(WEIGHTS)]
        count = [0] * SLOTS
        for i, (nm, s, after) in enumerate(plan):
            count[s] += 16
            loads[(nm, i >= nctx)] = (s, count[s])

        summed = [nm for nm in WEIGHTS if nm[:2] in ("ao", "ba", "xo", "so") and nm not in ("ao1", "xo7", "so7")]

        def used_at(nm):
            if nm in summed:
                return S["w_used"], summed.index(nm) + 1
            if nm in ("ao1", "xo7", "so7"):
                return S["y_ps"], {"ao1": 1, "xo7": 3, "so7": 4}[nm]
            return S["proj_ps"], PROJ.index("xv_b1" if nm == "xv" else nm) + 1

        def chunk(eng, nm):
            s, v = loads[(nm, True)]
            eng.wait_ge(slot_in[s], v)
            return ring[:, s, :].rearrange("p (k n) -> p k n", n=N if nm[:2] in ("ao", "xo", "so") else 512)

        block = ctx.enter_context(nc.Block())

        def run_of(layer, b):
            return 2 * layer + b

        @block.sync
        def _(sp):
            sp.dma_start(coord, a["coords"]).then_inc(S["coord_in"], 16)
            sp.dma_start(x[:], a["x"]).then_inc(S["x_in"], 16)
            for dst, src in ((ident[:], "ident"), (identh[:], "identh"), (lower[:], "lower"),
                             (rankoff[:], "rankoff"), (maskl[:], "maskl"), (maskr[:], "maskr"),
                             (wlin_n[:], "wlin_n"), (wlin_c[:], "wlin_c"), (blin[:], "blin"),
                             (wconv[0][:], "wconv0"), (wconv[1][:], "wconv1"), (wconv3[:], "wconv3")):
                sp.dma_start(dst, a[src]).then_inc(S["const_in"], 16)
            def stream(lo, hi):
                for i in range(lo, hi):
                    nm, s, after = plan[i]
                    w = i - nctx
                    if w >= SLOTS:
                        sp.wait_ge(*used_at(WEIGHTS[w - SLOTS]))
                    elif w >= 0:
                        sp.wait_ge(S["ctx_ps"], 32)
                    elif after:
                        sp.wait_ge(S["ctx_ps"], 8 * after)
                    sp.dma_start(ring[:, s, :], a["wstream"][stream_row[nm]]).then_inc(slot_in[s], 16)

            stream(0, nctx + SLOTS)
            for b in range(B):
                sp.wait_ge(S["fsT_ps"], 4 * (run_of(1, b) + 1))
                sp.wait_ge(S["feat_out"], 32)
                for l in range(2):
                    sp.dma_start(g01[64 * l:64 * l + 64, :], feat_d[l][64 * b:64 * b + 64, :]).then_inc(S["g01_in"], 16)
            sp.wait_ge(S["x1_ready"], 1)
            for dst, src in ((cosn, a["cosn"]), (sinn, a["sinn"]), (causal, a["causal"]), (wgate, a["wgate"]),
                             (lora_b, a["lora_b"]), (bbase, a["bbase"].partition_broadcast(P)),
                             (bthr, a["bthr"].partition_broadcast(P))):
                sp.dma_start(dst, src).then_inc(S["late_in"], 16)
            stream(nctx + SLOTS, nctx + WEIGHTS.index("sq0") + 3)
            sp.wait_ge(S["x_ready"], 3)
            for dst, src in ((samebatch, a["samebatch"]), (wroute, a["wroute"]), (ebias[0:64, :], a["ebias"]),
                             (rbias, a["rbias"].partition_broadcast(P))):
                sp.dma_start(dst, src).then_inc(S["late2_in"], 16)
            stream(nctx + WEIGHTS.index("sq0") + 3, len(plan))
            sp.wait_ge(S["x_ready"], 5)
            sp.dma_start(out, x[:]).then_inc(S["out_done"], 16)
            sp.wait_ge(S["out_done"], 16)

        CONSTS = 16 * 12
        LATE, LATE2 = 16 * 7, 16 * 4

        def step_last(pool, base):
            par = (base + BODIES - 2) % 2
            xt_body(pool, base, BODIES - 1, 1 - par)
            norm_body(pool, base, BODIES - 2, par)
            norm_body(pool, base, BODIES - 1, 1 - par)

        def scatter(pool, r):
            layer, b = divmod(r, B)
            if layer == 0:
                pool.wait_ge(S["rank_ready"], b + 1)
                pool.wait_ge(S["fnT_ev"], 2)
            else:
                pool.wait_ge(S["fnT_ev"], 3 + b)
            for m in range(METHODS):
                for k in range(NBLK):
                    col = (m * B + b) * NBLK + k
                    src = fn[:, k, 64 * b:64 * b + 64]
                    pool.indirect_dma_start(
                        out=sorted_d[r], out_offset=bass.IndirectOffsetOnAxis(ap=rowidx[:, col:col + 1], axis=0),
                        in_=src, in_offset=None).then_inc(scattered[r], 16)

        def front_loads(pool, r):
            layer, b = divmod(r, B)
            pool.wait_ge(scattered[r], 16 * METHODS * NBLK)
            if r:
                pool.wait_ge(S["fsT_ps"], 4 * r)
            if r == RUNS - 1:
                pool.wait_ge(S["h3_ps"], 1)
            pool.dma_start(fsr, sorted_d[r].rearrange("(k q) c -> q k c", q=P))\
                .then_inc(S["fsr_in"], 16)
            if layer == 0:
                pool.wait_ge(S["feat_out0"], 16)
            else:
                pool.wait_ge(S["feat_out"], 16 * 2)
            if r:
                pool.wait_ge(S["xt_ready"], BODIES * r)
                pool.wait_ge(S["c16_ready"], 4 * r)
            src = feat_d[layer]
            for t in range(2):
                for h in range(2):
                    pool.dma_start(fc[64 * h:64 * h + 64, t, :],
                                   bass.AP(tensor=src.tensor, offset=(64 * b + 32 * t + 16 * h) * N,
                                           ap=[[0, METHODS], [N, 16], [1, N]])).then_inc(S["fc_in"], 16)

        def n0_of(t):
            return t * BP if not isinstance(t, int) or t < BODIES - 1 else N - BP

        def win(t, lo, cnt):
            return bass.AP(tensor=arena, offset=fs_off + lo, ap=[[ARENA, P], [FSW, 2], [1, cnt], [1, KW]])

        def centre(lo, cnt):
            return bass.AP(tensor=arena, offset=fc_off + lo, ap=[[ARENA, P], [N, 2], [1, cnt], [0, KW]])

        def xt_body(pool, base, t, par):
            u = base + t
            par = par if not isinstance(t, int) else u % 2
            if not isinstance(t, int) or u >= 2:
                pool.wait_ge(S["v_done"], u - 1)
            dst = xt[:, par, :, :].rearrange("p t (n k) -> p t n k", k=KW)
            if isinstance(t, int) and t == 0:
                nc.gpsimd.tensor_tensor(dst[:, :, 0:5, :], fh, centre(0, 5), ALU.subtract)
                nc.gpsimd.tensor_tensor(dst[:, :, 5:BP, :], win(t, 5, BP - 5), centre(5, BP - 5), ALU.subtract)\
                    .then_inc(S["xt_ready"], 1)
            else:
                n0 = n0_of(t)
                nc.gpsimd.tensor_tensor(dst, win(t, n0, BP), centre(n0, BP), ALU.subtract).then_inc(S["xt_ready"], 1)

        def norm_body(pool, base, t, par):
            u = base + t
            par = par if not isinstance(t, int) else u % 2
            pool.wait_ge(S["recip_ready"], u + 1)
            pr = p_sb[0:GROWS, par, :, :]
            nc.gpsimd.tensor_tensor(pr, pr, rsum[0:GROWS, par, 1, :].unsqueeze(2).broadcast_to([GROWS, 8, GROWS]),
                                    ALU.mult).then_inc(S["norm_done"], 1)

        @block.gpsimd
        def _(pool):
            pool.wait_ge(S["minmax_ready"], 1)
            nc.gpsimd.partition_all_reduce(ext[:, 2:4, :], ext[:, 0:2, :], P, bass.bass_isa.ReduceOp.max)\
                .then_inc(S["minmax_all"], 1)

            def powers(n, rows=P):
                pool.wait_ge(S["pow_ready"], n)
                nc.gpsimd.tensor_tensor(small[0:rows, 2:3], small[0:rows, 1:2], small[0:rows, 8:9], ALU.pow)\
                    .then_inc(S["pow_done"], 1)

            powers(1)
            pool.wait_ge(S["ln_ready"], 1)
            pool.dma_start(feat_d[0], f0).then_inc(S["feat_out0"], 16)
            pool.wait_ge(S["keycol_ready"], 1)
            pool.dma_start(keys_d, keycol[:]).then_inc(S["keys_out"], 16)
            pool.wait_ge(S["keys_out"], 16)
            kd = keys_d.rearrange("(m b k) q -> b m (k q)", m=METHODS, b=B)
            for b in range(B):
                if b:
                    pool.wait_ge(S["keyrow_free"], 1)
                pool.dma_start(keyrow, kd[b].partition_broadcast(P)).then_inc(S["keyrow_in"], 16)
                if b:
                    scatter(pool, 0)
            scatter(pool, 1)
            front_loads(pool, 0)
            nbody = 0
            for r in range(RUNS):
                layer, b = divmod(r, B)
                pool.wait_ge(S["fsT_ev"], 4 * (r + 1))
                pool.wait_ge(S["fh_ready"], r + 1)
                pool.wait_ge(S["fc_in"], 64 * (r + 1))
                base = BODIES * r
                xt_body(pool, base, 0, 0)

                def step(t, par):
                    xt_body(pool, base, t + 1, 1 - par)
                    norm_body(pool, base, t, par)

                step(0, base % 2)
                with pool.Fori(1, BODIES - 2, 2) as t:
                    step(t, (base + 1) % 2)
                    step(t + 1, base % 2)
                step_last(pool, base)
                powers(2 + r, OUTC[layer])
                if layer == 0:
                    pool.wait_ge(S["feat_ready"], r + 1)
                    pool.dma_start(feat_d[1][64 * b:64 * b + 64, :], f0[0:64, :]).then_inc(S["feat_out"], 16)
                    scatter(pool, 2 + b)
                if r + 1 < RUNS:
                    front_loads(pool, r + 1)
            powers(2 + RUNS)
            def normalise(n):
                pool.wait_ge(S["g_recip"], n + 1)
                pr = (gp if n < AGROUPS else sp_)[:, n % 2]
                nc.gpsimd.tensor_tensor(pr, pr, gsum[:, n % 2, 3, :].unsqueeze(2).broadcast_to([P, 4, P]), ALU.mult)\
                    .then_inc(S["g_norm"], 1)

            powers(3 + RUNS)
            for n in range(AGROUPS):
                normalise(n)
            powers(4 + RUNS)
            powers(5 + RUNS)
            powers(6 + RUNS)
            for n in range(AGROUPS, AGROUPS + SGROUPS):
                normalise(n)
            powers(7 + RUNS)

        def ctx_chunk(pe, c):
            s, v = loads[(f"ctx{c}", False)]
            pe.wait_ge(slot_in[s], v)
            if c == 0:
                pe.wait_ge(slot_in[0], 16)
                pe.wait_ge(slot_in[1], 16)
            cx = ring[:, s, :].rearrange("p (k n) -> p k n", k=KT)
            wk = ring[:, 0, :].rearrange("p (k n) -> p k n", k=KT)
            wv = ring[:, 1, :].rearrange("p (k n) -> p k n", k=KT)
            for j in range(8):
                g = 8 * c + j
                if g >= 2:
                    pe.wait_ge(S["ctx_ev"], g - 1)
                bank = (ps_o, ps_h)[g % 2]
                q = j % 4
                for k in range(KT):
                    if j < 4:
                        mm = nc.tensor.matmul(bank[:], wk[:, k, q * P:(q + 1) * P], cx[:, k, :], start=k == 0, stop=k == KT - 1)
                    else:
                        mm = nc.tensor.matmul(bank[:], cx[:, k, q * P:(q + 1) * P], wv[:, k, :], start=k == 0, stop=k == KT - 1)
                mm.then_inc(S["ctx_ps"], 1)

        def front_transposes(pe, r):
            pe.wait_ge(S["fsp_ready"], r + 1)
            if r:
                pe.wait_ge(S["hc_ready"], 2 * r)
                pe.wait_ge(S["fnT_ev"], min(2 + r, 4))
            for t in range(2):
                for h in range(2):
                    n = 4 * r + 2 * t + h
                    if n:
                        pe.wait_ge(S["fsT_ev"], n)
                    for k in range(4):
                        src = fsp[:, 4 * h + k, 128 * t:128 * t + 128]
                        mm = nc.tensor.transpose(ps_f[:, k * P:(k + 1) * P], src, ident[:])
                    mm.then_inc(S["fsT_ps"], 1)

        @block.tensor
        def _(pe):
            pe.wait_ge(S["const_in"], CONSTS)
            pe.wait_ge(S["ln_ready"], 1)
            for h in range(2):
                if h:
                    pe.wait_ge(S["fnT_ev"], h)
                for k in range(4):
                    mm = nc.tensor.transpose(ps_f[:, k * P:(k + 1) * P], f0[:, (4 * h + k) * P:(4 * h + k + 1) * P], ident[:])
                mm.then_inc(S["fnT_ps"], 1)
            ctx_chunk(pe, 0)
            pe.wait_ge(S["key_ready"], 1)
            pe.wait_ge(S["fnT_ev"], 2)
            nc.tensor.transpose(ps_f[0:64, 0:P], key[:].bitcast(F32), ident[:]).then_inc(S["keyT_ps"], 1)
            for c in range(1, 4):
                ctx_chunk(pe, c)
            for l in range(2):
                O = OUTC[l]
                bank = (ps_s[:, 0], ps_s[:, 1])[l]
                for t in range(2):
                    nc.tensor.matmul(bank[:, t * P:t * P + O], wlin_n[:, l, t * P:(t + 1) * P], wconv[l][:], start=True, stop=True)
                bank = (ps_pt[:, 0], ps_pt[:, 1])[l]
                for t in range(2):
                    nc.tensor.matmul(bank[:, t * P:t * P + O], wlin_c[:, l, t * P:(t + 1) * P], wconv[l][:], start=True, stop=True)
                mm = nc.tensor.matmul(bank[0:O, 256:257], wconv[l][:], blin[:, l:l + 1], start=True, stop=True)
            mm.then_inc(S["wp_ps"], 1)
            pe.wait_ge(S["wp_ev"], 1)
            pe.wait_ge(S["keycol_ready"], 1)
            for r in range(RUNS):
                layer, b = divmod(r, B)
                O = OUTC[layer]
                base = BODIES * r
                front_transposes(pe, r)
                pe.wait_ge(S["fsT_ev"], 4 * (r + 1))
                for h in range(2):
                    for t in range(2):
                        n = 4 * r + 2 * h + t
                        pe.wait_ge(S["c16_ready"], n + 1)
                        if t == 0:
                            pe.wait_ge(S["hc_ready"], 2 * r + h)
                        mm = nc.tensor.matmul(ps_f[0:O, :], wc[layer][:, t, :], c32, start=t == 0, stop=t == 1)
                        mm.then_inc(S["hc_ps"], 1)

                def scores(t, par):
                    u = base + t
                    st = isinstance(t, int)
                    pe.wait_ge(S["xt_ready"], u + 1)
                    if not st or u >= 1:
                        pe.wait_ge(S["exp_done"], u)
                    for half in range(2):
                        q = slice(64 * half, 64 * half + 64)
                        nc.tensor.matmul(ps_s[0:GROWS, half, 0:4 * GROWS], maskl[q, :], maskr[q, :], start=True, stop=False,
                                         skip_group_check=True)
                        for g in range(2):
                            for k in range(2):
                                c0 = (2 * g + k) * GROWS
                                xs = xt[q, par, k, g * GROWS:(g + 1) * GROWS]
                                mm = nc.tensor.matmul(ps_s[0:GROWS, half, c0:c0 + GROWS], xs, xs, start=False,
                                                      stop=(g, k) == (1, 1), skip_group_check=True)
                    mm.then_inc(S["s_done"], 1)
                    if not st or u >= 1:
                        pe.wait_ge(S["v_ev"], u)
                    for g in range(2):
                        for k in range(2):
                            mm = nc.tensor.transpose(ps_v[0:GROWS, g, k * P:(k + 1) * P],
                                                     xt[:, par, k, g * GROWS:(g + 1) * GROWS], identh[:])
                    mm.then_inc(S["v_done"], 1)

                def attend(t, par):
                    u = base + t
                    st = isinstance(t, int)
                    pe.wait_ge(S["norm_done"], u + 1)
                    if st and t == 0 and r == RUNS - 1:
                        pe.wait_ge(S["h3_out"], 1)
                    if not st or u >= 1:
                        pe.wait_ge(S["pt_ev"], 2 * u)
                    for g in range(2):
                        for h in range(4):
                            mm = nc.tensor.transpose(ps_pt[0:GROWS, g, h * GROWS:(h + 1) * GROWS],
                                                     p_sb[0:GROWS, par, 4 * (h % 2) + 2 * g + h // 2, :],
                                                     ident[0:GROWS, 0:GROWS])
                        mm.then_inc(S["t_done"], 1)
                    pe.wait_ge(S["v_ev"], u + 1)
                    if not st or u >= 1:
                        pe.wait_ge(S["o_ev"], u)
                    for g in range(2):
                        pe.wait_ge(S["pt_ev"], 2 * u + g + 1)
                        for h in range(4):
                            q = 64 * (h % 2)
                            c0 = (h // 2) * BCOLS + g * GROWS
                            mm = nc.tensor.matmul(ps_o[q:q + 64, c0:c0 + GROWS], vs_sb[0:GROWS, par, g, 64 * h:64 * h + 64],
                                                  pt_sb[0:GROWS, par, 4 * g + h, :], start=True, stop=True)
                    mm.then_inc(S["pv_done"], 1)

                def project(t, par):
                    u = base + t
                    st = isinstance(t, int)
                    pe.wait_ge(S["o_ev"], u + 1)
                    if not st or u >= 1:
                        pe.wait_ge(S["h_read"], u)
                    for k in range(2):
                        mm = nc.tensor.matmul(ps_h[0:O, 0:BCOLS], wp[layer][:, k, :], o_sb[:, par, k, :],
                                              start=k == 0, stop=k == 1)
                    mm.then_inc(S["w_done"], 1)

                p0 = base % 2
                p1 = 1 - p0
                scores(0, p0)
                scores(1, p1)
                attend(0, p0)
                with pe.Fori(2, BODIES - 1, 2) as t:
                    scores(t, p0)
                    project(t - 2, p0)
                    attend(t - 1, p1)
                    scores(t + 1, p1)
                    project(t - 1, p1)
                    attend(t, p0)
                scores(BODIES - 1, p0)
                project(BODIES - 3, p0)
                attend(BODIES - 2, p1)
                attend(BODIES - 1, p0)
                project(BODIES - 2, p1)
                project(BODIES - 1, p0)
                if layer == 0:
                    pe.wait_ge(S["feat_ready"], r + 1)
                    pe.wait_ge(S["hc_ready"], 2 * r + 2)
                    for k in range(NBLK):
                        mm = nc.tensor.transpose(ps_f[:, k * 64:(k + 1) * 64], f0[0:64, k * P:(k + 1) * P], ident[0:64, 0:64])
                    mm.then_inc(S["fnT_ps"], 1)
                else:
                    pe.wait_ge(S["feat_ready"], r + 1)
                    pe.wait_ge(S["g01_in"], 32 * (b + 1))
                    for h in range(2):
                        cols = slice(512 * h, 512 * h + 512)
                        nc.tensor.matmul(ps_pt[64 * b:64 * b + 64, h, :], wconv3[:, 0, :], g01[:, cols], start=True, stop=False)
                        mm = nc.tensor.matmul(ps_pt[64 * b:64 * b + 64, h, :], wconv3[:, 1, :], f2[:, cols], start=False, stop=True)
                    mm.then_inc(S["h3_ps"], 1)

            def transpose_tokens(n):
                pe.wait_ge(S["hn_ready"], n + 1)
                for h in range(2):
                    for k in range(4):
                        mm = nc.tensor.transpose(ps_pt[:, h, k * P:(k + 1) * P], hn[:, (4 * h + k) * P:(4 * h + k + 1) * P], ident[:])
                    mm.then_inc(S["hT_ps"], 1)
                pe.wait_ge(S["hT_ev"], 2 * n + 2)

            def bank_for(nm):
                g = PROJ.index(nm)
                if g >= 2:
                    pe.wait_ge(S["proj_ev"], g - 1)
                return proj_bank[g % 2]

            def project_tokens(nm):
                w = chunk(pe, nm)
                bank = bank_for(nm)
                for k in range(KT):
                    mm = nc.tensor.matmul(bank[:], hT[:, k, :], w[:, k, :], start=k == 0, stop=k == KT - 1)
                mm.then_inc(S["proj_ps"], 1)

            def small_product(nm, w, cols):
                bank = bank_for(nm)
                for k in range(KT):
                    mm = nc.tensor.matmul(bank[:, 0:cols], hT[:, k, :], w[:, k, :], start=k == 0, stop=k == KT - 1)
                mm.then_inc(S["proj_ps"], 1)

            def turn(nm, src):
                n = TURNS.index(nm)
                pe.wait_ge(S["proj_ev"] if nm[0] != "a" else S["rope_ready"],
                           PROJ.index(nm) + 1 if nm[0] != "a" else 1 + ("ak" in nm))
                if n >= 2:
                    pe.wait_ge(S["turn_ev"], n - 1)
                for k in range(4):
                    mm = nc.tensor.transpose(ps_pt[:, n % 2, k * P:(k + 1) * P], src[:, k * P:(k + 1) * P], ident[:])
                mm.then_inc(S["turn_ps"], 1)

            def group_scores(n):
                if n >= 2:
                    pe.wait_ge(S["g_masked"], n - 1)
                bank = ps_s[:, n % 2]
                for i in range(4):
                    if n < AGROUPS:
                        q, t = slice(64 * (n % 2), 64 * (n % 2) + 64), 4 * (n // 2) + i
                        l, r = aqT[q, t, :], akT[q, t, :]
                    else:
                        l, r = sqT[:, 4 * (n - AGROUPS) + i, :], skT[:, n - AGROUPS, :]
                    mm = nc.tensor.matmul(bank[:, i * P:(i + 1) * P], l, r, start=True, stop=True)
                mm.then_inc(S["g_s"], 1)

            def group_turn(n):
                pe.wait_ge(S["g_norm"], n + 1)
                if n >= 2:
                    pe.wait_ge(S["g_tev"], n - 1)
                pr = (gp if n < AGROUPS else sp_)[:, n % 2]
                for i in range(4):
                    mm = nc.tensor.transpose(ps_pt[:, n % 2, i * P:(i + 1) * P], pr[:, i, :], ident[:])
                mm.then_inc(S["g_t"], 1)

            def group_outputs(n):
                pe.wait_ge(S["g_tev"], n + 1)
                if n >= 2:
                    pe.wait_ge(S["g_oev"], n - 1)
                bank = proj_bank[n % 2]
                if n < AGROUPS:
                    q = 64 * (n % 2)
                    for i in range(4):
                        c = (4 * (n // 2) + i) * P + q
                        mm = nc.tensor.matmul(bank[q:q + 64, i * P:(i + 1) * P], av[:, c:c + 64], gpT[:, n % 2, i, :],
                                              start=True, stop=True)
                else:
                    c = (n - AGROUPS) * P
                    mm = nc.tensor.matmul(bank[:], sv[:, c:c + P], spT[:, n % 2].rearrange("p h n -> p (h n)"), start=True, stop=True)
                mm.then_inc(S["g_pv"], 1)

            def groups(lo, hi):
                group_scores(lo)
                group_scores(lo + 1)
                for n in range(lo, hi):
                    group_turn(n)
                    if n + 2 < hi:
                        group_scores(n + 2)
                    group_outputs(n)

            def output_map(names, oT):
                for j, nm in enumerate(names):
                    w = chunk(pe, nm)
                    for k in range(4):
                        for h in range(2):
                            mm = nc.tensor.matmul(y_ps[h], oT[:, 4 * j + k, :], w[:, k, 512 * h:512 * h + 512],
                                                  start=(j, k) == (0, 0), stop=(j, k) == (len(names) - 1, 3),
                                                  skip_group_check=True)
                    mm.then_inc(S["y_ps"] if j == len(names) - 1 else S["w_used"], 1)

            transpose_tokens(0)
            for nm in ("aq0", "aq1", "ak0", "ak1", "av0", "av1"):
                project_tokens(nm)
            for nm, src in (("aq0", aq[:, 0:512]), ("aq1", aq[:, 512:N]), ("ak0", ak[:, 0:512]), ("ak1", ak[:, 512:N])):
                turn(nm, src)
            pe.wait_ge(S["turn_ev"], 4)
            pe.wait_ge(S["proj_ev"], 6)
            groups(0, AGROUPS)
            pe.wait_ge(S["g_oev"], AGROUPS)
            output_map(["ao0", "ao1"], aoT)
            transpose_tokens(1)
            pe.wait_ge(S["late_in"], LATE)
            small_product("gates", wgate, GATES)
            for h in range(2):
                w = chunk(pe, f"base{h}")
                for k in range(KT):
                    mm = nc.tensor.matmul(y_ps[h], hT[:, k, :], w[:, k, :], start=k == 0, stop=False, skip_group_check=True)
                mm.then_inc(S["w_used"], 1)
            pe.wait_ge(S["gate_ready"], 1)
            nc.tensor.transpose(ps_pt[:, 0, 0:P], lora, ident[:]).then_inc(S["gateT_ps"], 1)
            pe.wait_ge(S["gateT_ev"], 1)
            for h in range(2):
                mm = nc.tensor.matmul(y_ps[h], loraT, lora_b[:, 512 * h:512 * h + 512], start=False, stop=True, skip_group_check=True)
            mm.then_inc(S["y_ps"], 1)
            transpose_tokens(2)
            for i in range(8):
                project_tokens(f"xq{i}")
                if i:
                    turn(f"xq{i - 1}", sq[:, 512 * (i - 1):512 * i])
            turn("xq7", sq[:, 512 * 7:512 * 8])
            w = chunk(pe, "xk")
            bank = bank_for("xk")
            for h in range(4):
                for k in range(KT):
                    mm = nc.tensor.matmul(bank[:, h * P:(h + 1) * P], w[:, k, h * P:(h + 1) * P], hT[:, k, :], start=k == 0, stop=k == KT - 1)
            mm.then_inc(S["proj_ps"], 1)
            w = chunk(pe, "xv")
            for b in range(B):
                bank = bank_for(f"xv_b{b}")
                for k in range(KT):
                    mm = nc.tensor.matmul(bank[0:64, :], hT[:, k, 64 * b:64 * b + 64], w[:, k, :], start=k == 0, stop=k == KT - 1)
                mm.then_inc(S["proj_ps"], 1)
            pe.wait_ge(S["proj_ev"], PROJ.index("xv_b1") + 1)
            pe.wait_ge(S["turn_ev"], TURNS.index("xq7") + 1)

            def x_scores(n):
                b, h, g = n // 16, n // 4 % 4, n % 4
                if n:
                    pe.wait_ge(S["t_exp"], n)
                else:
                    pe.wait_ge(S["x_ready"], 2)
                l = xqT[:, b, 8 * h + 2 * g:8 * h + 2 * g + 2, :].rearrange("p h n -> p (h n)")
                for o, (c, w) in ((ps_s[:, 0], (0, 512)), (ps_s[:, 1], (512, 512)), (y_ps[0][:, 0:64], (N, 64))):
                    mm = nc.tensor.matmul(o, l, keysT[:, h, b * KV + c:b * KV + c + w], start=True, stop=True)
                mm.then_inc(S["t_s"], 1)

            def x_turn(n):
                pe.wait_ge(S["t_norm"], n + 1)
                for j in range(3):
                    m = 3 * n + j
                    if m >= 2:
                        pe.wait_ge(S["t_tev"], m - 1)
                    for k in range(4 * j, min(4 * j + 4, KVT)):
                        w = P if k < KVT - 1 else 64
                        mm = nc.tensor.transpose(ps_pt[0:w, m % 2, (k % 4) * P:(k % 4 + 1) * P], xp[:, n % 2, k * P:k * P + w], ident[:])
                    mm.then_inc(S["t_t"], 1)

            def x_outputs(n):
                b, h, g = n // 16, n // 4 % 4, n % 4
                pe.wait_ge(S["t_tev"], 3 * n + 3)
                if n >= 2:
                    pe.wait_ge(S["t_oev"], n - 1)
                bank = proj_bank[n % 2]
                for k in range(KVT):
                    if k < KVT - 1:
                        l, r = vals[:, NBLK * b + k, h * P:(h + 1) * P], xpT[:, n % 2, k, :]
                    else:
                        l, r = vlat[0:64, b, h * P:(h + 1) * P], xpT[0:64, n % 2, k, :]
                    mm = nc.tensor.matmul(bank[:, 0:P], l, r, start=k == 0, stop=k == KVT - 1)
                mm.then_inc(S["t_pv"], 1)

            x_scores(0)
            for n in range(XTILES):
                if n + 1 < XTILES:
                    x_scores(n + 1)
                x_turn(n)
                x_outputs(n)
            pe.wait_ge(S["t_oev"], XTILES)
            output_map([f"xo{i}" for i in range(8)], soT)
            transpose_tokens(3)
            for i in range(8):
                project_tokens(f"sq{i}")
                if i:
                    turn(f"sq{i - 1}", sq[:, 512 * (i - 1):512 * i])
            turn("sq7", sq[:, 512 * 7:512 * 8])
            for nm in ("sk0", "sk1", "sv0", "sv1"):
                project_tokens(nm)
            turn("sk0", sk[:, 0:512])
            turn("sk1", sk[:, 512:N])
            pe.wait_ge(S["turn_ev"], len(TURNS))
            pe.wait_ge(S["proj_ev"], PROJ.index("sv1") + 1)
            groups(AGROUPS, AGROUPS + SGROUPS)
            pe.wait_ge(S["g_oev"], AGROUPS + SGROUPS)
            output_map([f"so{i}" for i in range(8)], soT)
            transpose_tokens(4)
            pe.wait_ge(S["late2_in"], LATE2)
            small_product("route", wroute, 64)
            pe.wait_ge(S["route_ready"], 1)
            nc.tensor.transpose(ps_pt[0:64, 0, 0:P], route[:, 4, :], ident[:]).then_inc(S["routeT_ps"], 1)
            pe.wait_ge(S["routeT_ev"], 1)
            for h in range(2):
                mm = nc.tensor.matmul(y_ps[h], rT[0:64, :], ebias[0:64, 512 * h:512 * h + 512], start=True, stop=True)
            mm.then_inc(S["y_ps"], 1)

        @block.scalar
        def _(act):
            for h in range(2):
                act.wait_ge(S["fnT_ps"], h + 1)
                nc.scalar.copy(fn[:, 4 * h:4 * h + 4, :], ps_f[:].rearrange("p (k c) -> p k c", k=4)).then_inc(S["fnT_ev"], 1)
            for g in range(32):
                c, j = divmod(g, 8)
                if g == 8:
                    act.wait_ge(S["keyT_ps"], 1)
                    nc.scalar.copy(keycol[:], ps_f[0:64, 0:P]).then_inc(S["keycol_ready"], 1)
                act.wait_ge(S["ctx_ps"], g + 1)
                bank = (ps_o, ps_h)[g % 2]
                if j < 4:
                    lo = (c // 2) * KV + (c % 2) * 512
                    dst = keysT[:, j, lo:lo + 512]
                else:
                    dst = vals[:, 4 * c + j - 4, :]
                nc.scalar.copy(dst, bank[:]).then_inc(S["ctx_ev"], 1)
            act.wait_ge(S["wp_ps"], 1)
            for l in range(2):
                O = OUTC[l]
                for t in range(2):
                    nc.scalar.copy(wp[l][:, t, :], ps_s[:, l, t * P:t * P + O])
                    nc.scalar.copy(wc[l][:, t, :], ps_pt[:, l, t * P:t * P + O])
                cp = nc.scalar.copy(cb[0:O, l:l + 1], ps_pt[0:O, l, 256:257])
            cp.then_inc(S["wp_ev"], 1)
            for r in range(RUNS):
                layer, b = divmod(r, B)
                O = OUTC[layer]
                base = BODIES * r
                act.wait_ge(S["fsr_in"], 16 * (r + 1))
                if r:
                    act.wait_ge(S["feat_ready"], r)
                for m in range(METHODS):
                    cp = nc.scalar.copy(fsp.rearrange("p k (h m c) -> p m k h c", h=4, m=METHODS)[:, m],
                                        fsr.rearrange("p (m k) (h c) -> p m k h c", m=METHODS, h=4)[:, m])
                cp.then_inc(S["fsp_ready"], 1)
                for t in range(2):
                    for h in range(2):
                        n = 4 * r + 2 * t + h
                        act.wait_ge(S["fsT_ps"], n + 1)
                        if r and n == 4 * r:
                            act.wait_ge(S["xt_ready"], base)
                        nc.scalar.copy(fs[:, t, 5 + 512 * h:5 + 512 * h + 512], ps_f[:]).then_inc(S["fsT_ev"], 1)
                for h in range(2):
                    act.wait_ge(S["hc_ps"], 4 * r + 2 * h + 2)
                    if r and h == 0:
                        act.wait_ge(S["h_read"], base)
                    nc.scalar.activation(hc[0:O, 512 * h:512 * h + 512], ps_f[0:O, :], ACT.Identity,
                                         bias=cb[0:O, layer:layer + 1]).then_inc(S["hc_ready"], 1)

                def values_out(t, par):
                    u = base + t
                    st = isinstance(t, int)
                    act.wait_ge(S["v_done"], u + 1)
                    if not st or u >= 2:
                        act.wait_ge(S["pv_done"], u - 1)
                    nc.scalar.copy(vs_sb[0:GROWS, par, :, :], ps_v[0:GROWS, :, 0:256]).then_inc(S["v_ev"], 1)

                def exponentials(t, par):
                    u = base + t
                    st = isinstance(t, int)
                    act.wait_ge(S["negmax_ready"], u + 1)
                    if not st or u >= 2:
                        act.wait_ge(S["t_done"], 2 * u - 2)
                    for g in range(8):
                        e = nc.scalar.activation(p_sb[0:GROWS, par, g, :],
                                                 ps_s[0:GROWS, g // 4, (g % 4) * GROWS:(g % 4 + 1) * GROWS], ACT.Exp,
                                                 bias=negmax[0:GROWS, par, 1, g:g + 1], scale=0.125,
                                                 accum_out=rsum[0:GROWS, par, 0, g:g + 1])
                    e.then_inc(S["exp_done"], 1)

                def outputs_out(t, par):
                    u = base + t
                    st = isinstance(t, int)
                    act.wait_ge(S["pv_done"], u + 1)
                    if not st or u >= 2:
                        act.wait_ge(S["w_done"], u - 1)
                    nc.scalar.copy(o_sb[:, par, :, :], ps_o[:, 0:2 * BCOLS].rearrange("p (t n) -> p t n", t=2))\
                        .then_inc(S["o_ev"], 1)

                p0 = base % 2
                p1 = 1 - p0
                values_out(0, p0)
                exponentials(0, p0)

                def two(t):
                    values_out(t, p1)
                    exponentials(t, p1)
                    outputs_out(t - 1, p0)
                    values_out(t + 1, p0)
                    exponentials(t + 1, p0)
                    outputs_out(t, p1)

                two(1)
                with act.Fori(3, BODIES - 1, 2) as t:
                    two(t)
                outputs_out(BODIES - 1, p0)

            def tokens_out(n):
                for h in range(2):
                    act.wait_ge(S["hT_ps"], 2 * n + h + 1)
                    nc.scalar.copy(hT[:, 4 * h:4 * h + 4, :], heads(ps_pt[:, h], P)).then_inc(S["hT_ev"], 1)

            def proj_out(nm, dst, rows=P):
                g = PROJ.index(nm)
                act.wait_ge(S["proj_ps"], g + 1)
                w = dst.shape[-1] if len(dst.shape) == 2 else 512
                src = proj_bank[g % 2][0:rows, 0:w]
                if len(dst.shape) == 4:
                    src = src.rearrange("p (h b n) -> p h b n", h=dst.shape[1], b=dst.shape[2])
                nc.scalar.copy(dst, src).then_inc(S["proj_ev"], 1)

            def turn_out(nm, dst):
                n = TURNS.index(nm)
                act.wait_ge(S["turn_ps"], n + 1)
                src = ps_pt[:, n % 2]
                src = src.rearrange("p (h b n) -> p h b n", h=4, b=B) if len(dst.shape) == 4 else heads(src, P)
                nc.scalar.copy(dst, src).then_inc(S["turn_ev"], 1)

            def group_exp(n, scale):
                act.wait_ge(S["g_negmax"], n + 1)
                pr = (gp if n < AGROUPS else sp_)[:, n % 2]
                for i in range(4):
                    act_ = nc.scalar.activation(pr[:, i, :], pr[:, i, :], ACT.Exp, bias=gsum[:, n % 2, 1, i:i + 1], scale=scale,
                                                accum_out=gsum[:, n % 2, 2, i:i + 1])
                act_.then_inc(S["g_exp"], 1)

            def group_turn_out(n):
                act.wait_ge(S["g_t"], n + 1)
                if n >= 2:
                    act.wait_ge(S["g_pv"], n - 1)
                nc.scalar.copy((gpT if n < AGROUPS else spT)[:, n % 2], heads(ps_pt[:, n % 2], P)).then_inc(S["g_tev"], 1)

            def group_out(n):
                act.wait_ge(S["g_pv"], n + 1)
                if n < AGROUPS:
                    q = slice(64 * (n % 2), 64 * (n % 2) + 64)
                    dst = aoT[q, 4 * (n // 2):4 * (n // 2) + 4, :]
                    src = heads(proj_bank[n % 2][q, :], P)
                else:
                    dst = soT[:, 4 * (n - AGROUPS):4 * (n - AGROUPS) + 4, :]
                    src = heads(proj_bank[n % 2][:], P)
                nc.scalar.copy(dst, src).then_inc(S["g_oev"], 1)

            def groups(lo, hi, scale):
                group_exp(lo, scale)
                for n in range(lo, hi):
                    if n + 1 < hi:
                        group_exp(n + 1, scale)
                    group_turn_out(n)
                    group_out(n)

            tokens_out(0)
            for nm, dst in (("aq", aq), ("ak", ak), ("av", av)):
                proj_out(nm + "0", dst[:, 0:512])
                proj_out(nm + "1", dst[:, 512:N])
            for nm, dst in (("aq", aqT), ("ak", akT)):
                turn_out(nm + "0", dst[:, 0:4, :])
                turn_out(nm + "1", dst[:, 4:8, :])
            groups(0, AGROUPS, 0.125)
            tokens_out(1)
            proj_out("gates", gates[:, 0:GATES])
            act.wait_ge(S["gate_max"], 1)
            nc.scalar.activation(tiny[:, 8:16], gates[:, 128:136], ACT.Exp, bias=tiny[:, 1:2], accum_out=tiny[:, 2:3])
            nc.scalar.activation(tiny[:, 4:5], tiny[:, 3:4], ACT.Exp, scale=-1.0).then_inc(S["gate_exp"], 1)
            act.wait_ge(S["gateT_ps"], 1)
            nc.scalar.copy(loraT, ps_pt[:, 0, 0:P]).then_inc(S["gateT_ev"], 1)
            tokens_out(2)
            for i in range(8):
                proj_out(f"xq{i}", sq[:, 512 * i:512 * i + 512])
                if i:
                    turn_out(f"xq{i - 1}", xqT[:, :, 4 * (i - 1):4 * i, :].rearrange("p b h n -> p h b n"))
            turn_out("xq7", xqT[:, :, 28:32, :].rearrange("p b h n -> p h b n"))
            proj_out("xk", keysT[:].rearrange("p h (b n) -> p h b n", b=B)[:, :, :, N:KV])
            for b in range(B):
                proj_out(f"xv_b{b}", vlat[0:64, b, :], 64)
            root = float(P) ** -0.5

            def x_exp(n):
                act.wait_ge(S["t_max"], n + 1)
                if n >= 2:
                    act.wait_ge(S["t_t"], 3 * n - 3)
                k = n % 2
                nc.scalar.activation(xp[:, k, 0:N], ps_s[:].rearrange("p g n -> p (g n)"), ACT.Exp, bias=xsum[:, k, 3:4],
                                     scale=root, accum_out=xsum[:, k, 4:5])
                nc.scalar.activation(xp[:, k, N:KV], y_ps[0][:, 0:64], ACT.Exp, bias=xsum[:, k, 3:4],
                                     scale=root, accum_out=xsum[:, k, 5:6]).then_inc(S["t_exp"], 1)

            def x_turn_out(n):
                for j in range(3):
                    m = 3 * n + j
                    if j == 0 and n >= 2:
                        act.wait_ge(S["t_pv"], n - 1)
                    act.wait_ge(S["t_t"], m + 1)
                    if j < 2:
                        nc.scalar.copy(xpT[:, n % 2, 4 * j:4 * j + 4, :], heads(ps_pt[:, m % 2], P)).then_inc(S["t_tev"], 1)
                    else:
                        nc.scalar.copy(xpT[0:64, n % 2, 8, :], ps_pt[0:64, m % 2, 0:P]).then_inc(S["t_tev"], 1)

            def x_out(n):
                b, h, g = n // 16, n // 4 % 4, n % 4
                act.wait_ge(S["t_pv"], n + 1)
                h0 = 8 * h + 2 * g
                nc.scalar.copy(soT[:, h0:h0 + 2, 64 * b:64 * b + 64], heads(proj_bank[n % 2][:, 0:P], 64)).then_inc(S["t_oev"], 1)

            x_exp(0)
            for n in range(XTILES):
                if n + 1 < XTILES:
                    x_exp(n + 1)
                x_turn_out(n)
                x_out(n)
            tokens_out(3)
            for i in range(8):
                proj_out(f"sq{i}", sq[:, 512 * i:512 * i + 512])
                if i:
                    turn_out(f"sq{i - 1}", sqT[:, 4 * (i - 1):4 * i, :])
            turn_out("sq7", sqT[:, 28:32, :])
            for nm, dst in (("sk", sk), ("sv", sv)):
                proj_out(nm + "0", dst[:, 0:512])
                proj_out(nm + "1", dst[:, 512:N])
            turn_out("sk0", skT[:, 0:4, :])
            turn_out("sk1", skT[:, 4:8, :])
            groups(AGROUPS, AGROUPS + SGROUPS, root)
            tokens_out(4)
            proj_out("route", route[:, 0, :])
            act.wait_ge(S["route_max"], 1)
            nc.scalar.activation(route[:, 1, :], route[:, 1, :], ACT.Exp, bias=tiny[:, 1:2], accum_out=tiny[:, 2:3])\
                .then_inc(S["route_exp"], 1)
            act.wait_ge(S["routeT_ps"], 1)
            nc.scalar.copy(rT[0:64, :], ps_pt[0:64, 0, 0:P]).then_inc(S["routeT_ev"], 1)

        @block.vector
        def _(dve):
            chain = [0]

            def link(ins):
                chain[0] += 1
                ins.then_inc(S["vchain"], 1)
                dve.wait_ge(S["vchain"], chain[0])

            V = nc.vector

            pows = [0]

            def norm_stats(rows, stats):
                pows[0] += 1
                link(V.bn_aggr(small[0:rows, 0:2], stats))
                V.tensor_scalar(small[0:rows, 1:2], small[0:rows, 1:2], EPS, None, ALU.add).then_inc(S["pow_ready"], 1)
                dve.wait_ge(S["pow_done"], pows[0])

            V.memset(small[:, 8:9], -0.5)
            V.memset(small[:, 9:10], 0.0)
            V.memset(cnt[:], 0.0)
            link(V.memset(expo[:], 0x20000000))
            dve.wait_ge(S["coord_in"], 16)
            cv = coord.rearrange("p i (b k) -> p (i b) k", b=B)
            link(V.tensor_reduce(ext[:, 0, :], cv, AX.X, ALU.max))
            V.tensor_reduce(ext[:, 1, :], cv, AX.X, ALU.min, negate=True).then_inc(S["minmax_ready"], 1)
            dve.wait_ge(S["x_in"], 16)
            link(V.bn_stats(bstat[:, 0, :], x[:, 0:512]))
            link(V.bn_stats(bstat[:, 1, :], x[:, 512:1024]))
            norm_stats(P, bstat[:, 0:2, :])
            V.tensor_scalar(f0, x[:], small[:, 0:1], small[:, 2:3], ALU.subtract, ALU.mult).then_inc(S["ln_ready"], 1)
            dve.wait_ge(S["minmax_all"], 1)
            link(V.tensor_tensor(ext[:, 0, :], ext[:, 2, :], ext[:, 3, :], ALU.add))
            link(V.tensor_scalar(ext[:, 0, :], ext[:, 0, :], 1e-6, None, ALU.add))
            link(V.reciprocal(ext[:, 1, :], ext[:, 0, :]))
            link(V.tensor_scalar(ext[:, 1, :], ext[:, 1, :], 1023.0, None, ALU.mult))
            qv = quant.rearrange("p i (b k) -> p (i b) k", b=B)
            link(V.tensor_tensor(qv, cv, ext[:, 3, :].unsqueeze(2).broadcast_to([P, 6, NBLK]), ALU.add))
            link(V.tensor_tensor(qv, qv, ext[:, 1, :].unsqueeze(2).broadcast_to([P, 6, NBLK]), ALU.mult))
            link(V.tensor_copy(qint, quant))
            link(V.tensor_copy(qtmp, qint))
            link(V.tensor_tensor(coord, qtmp, quant, ALU.is_gt))
            link(V.tensor_tensor(qtmp, qtmp, coord, ALU.subtract))
            link(V.tensor_scalar(qtmp, qtmp, 0.0, 1023.0, ALU.max, ALU.min))
            link(V.tensor_copy(qint, qtmp))
            for m in range(METHODS):
                for i in range(3):
                    j = (0, 1, 2)[i] if m % 2 == 0 else (1, 0, 2)[i]
                    ins = V.tensor_copy(bits[:, i, m, :], qint[:, j, :])
            link(ins)
            h3 = [bits[:, i, 2:4, :].rearrange("p m n -> p (m n)") for i in range(3)]
            m_, t_, n_, s_, a_ = (bt[:, i, :] for i in range(5))
            for bit in range(9, 0, -1):
                low = (1 << bit) - 1
                for i in range(3):
                    if i:
                        V.tensor_tensor(t_, h3[0], h3[i], ALU.bitwise_xor)
                    link(V.tensor_scalar(m_, h3[i], 31 - bit, 31, ALU.logical_shift_left, ALU.arith_shift_right))
                    if i == 0:
                        link(V.scalar_tensor_tensor(h3[0], m_, low, h3[0], ALU.bitwise_and, ALU.bitwise_xor))
                        continue
                    V.scalar_tensor_tensor(a_, m_, low, h3[0], ALU.bitwise_and, ALU.bitwise_xor)
                    link(V.tensor_scalar(n_, m_, -1, None, ALU.bitwise_xor))
                    link(V.scalar_tensor_tensor(s_, t_, low, n_, ALU.bitwise_and, ALU.bitwise_and))
                    V.tensor_tensor(h3[0], a_, s_, ALU.bitwise_xor)
                    link(V.tensor_tensor(h3[i], h3[i], s_, ALU.bitwise_xor))
            link(V.tensor_tensor(h3[1], h3[1], h3[0], ALU.bitwise_xor))
            link(V.tensor_tensor(h3[2], h3[2], h3[1], ALU.bitwise_xor))
            link(V.tensor_scalar(t_, h3[2], 1, None, ALU.logical_shift_right))
            for sh in (1, 2, 4, 8):
                link(V.scalar_tensor_tensor(m_ if sh in (1, 4) else t_, t_ if sh in (1, 4) else m_, sh,
                                            t_ if sh in (1, 4) else m_, ALU.logical_shift_right, ALU.bitwise_xor))
            for i in range(3):
                ins = V.tensor_tensor(h3[i], h3[i], t_, ALU.bitwise_xor)
            link(ins)
            bv = bits.rearrange("p i m n -> p (i m n)")
            sv = spread.rearrange("p i m n -> p (i m n)")
            for sh, mask in ((16, 0x030000FF), (8, 0x0300F00F), (4, 0x030C30C3), (2, 0x09249249)):
                link(V.scalar_tensor_tensor(sv, bv, sh, bv, ALU.logical_shift_left, ALU.bitwise_or))
                link(V.tensor_scalar(bv, sv, mask, None, ALU.bitwise_and))
            b3 = [bits[:, i, :, :].rearrange("p m n -> p (m n)") for i in range(3)]
            link(V.scalar_tensor_tensor(key[:], b3[0], 1, b3[1], ALU.logical_shift_left, ALU.bitwise_or))
            link(V.scalar_tensor_tensor(spread[:, 0, :, :].rearrange("p m n -> p (m n)"), key[:], 1, b3[2],
                                        ALU.logical_shift_left, ALU.bitwise_or))
            V.tensor_tensor(key[:], spread[:, 0, :, :].rearrange("p m n -> p (m n)"), expo[:], ALU.add)\
                .then_inc(S["key_ready"], 1)
            dve.wait_ge(S["key_ready"], 1)
            keyf = key[:].bitcast(F32)
            dve.wait_ge(S["const_in"], CONSTS)
            ncount = [0]

            def spare(n):
                if ncount[0] >= 2:
                    dve.wait_ge(S["counted"], ncount[0] - 1)
                return junk[:, ncount[0] % 2, 0:n]

            def counted(ins):
                ncount[0] += 1
                ins.then_inc(S["counted"], 1)

            for b in range(B):
                dve.wait_ge(S["keyrow_in"], 16 * (b + 1))
                for m in range(METHODS):
                    for k in range(NBLK):
                        col = (m * B + b) * NBLK + k
                        mine = keyf[:, col:col + 1]
                        if k:
                            counted(V.tensor_scalar(spare(P * k), keyrow[:, m, 0:P * k], mine, 0.0, ALU.is_le, ALU.add,
                                                    accum_out=cnt[:, 0, col:col + 1]))
                        counted(V.tensor_scalar(spare(N - P * k), keyrow[:, m, P * k:N], mine, 0.0, ALU.is_lt, ALU.add,
                                                accum_out=cnt[:, 1, col:col + 1]))
                        counted(V.scalar_tensor_tensor(spare(P), keyrow[:, m, P * k:P * k + P], mine, lower[:],
                                                       ALU.is_equal, ALU.mult, accum_out=cnt[:, 2, col:col + 1]))
                dve.wait_ge(S["counted"], ncount[0])
                V.tensor_copy(small[:, 24:25], small[:, 8:9]).then_inc(S["keyrow_free"], 1)
                dve.wait_ge(S["keyrow_free"], b + 1)
                bc = [cnt[:, i, :].rearrange("p (m b k) -> p b m k", m=METHODS, b=B)[:, b] for i in range(3)]
                rk = ranks[:].rearrange("p (m b k) -> p b m k", m=METHODS, b=B)[:, b]
                ro = rankoff[:].rearrange("p (m b k) -> p b m k", m=METHODS, b=B)[:, b]
                ri = rowidx[:].rearrange("p (m b k) -> p b m k", m=METHODS, b=B)[:, b]
                link(V.tensor_tensor(rk, bc[0], bc[1], ALU.add))
                link(V.tensor_tensor(rk, rk, bc[2], ALU.add))
                link(V.tensor_tensor(rk, rk, ro, ALU.add))
                V.tensor_copy(ri, rk).then_inc(S["rank_ready"], 1)
            for r in range(RUNS):
                layer, b = divmod(r, B)
                O = OUTC[layer]
                base = BODIES * r
                for h in range(2):
                    for t in range(2):
                        n = 4 * r + 2 * h + t
                        dve.wait_ge(S["fc_in"], 64 * (r + 1))
                        if n:
                            dve.wait_ge(S["hc_ps"], n)
                        link(V.tensor_copy(c16, fc[:, t, 512 * h:512 * h + 512]))
                        V.tensor_copy(c32, c16).then_inc(S["c16_ready"], 1)
                dve.wait_ge(S["fsT_ev"], 4 * (r + 1))
                for n in range(5):
                    V.tensor_copy(fh[:, :, n, 0:n + 6], fs[:, :, 5:n + 11])
                    if n < 4:
                        V.tensor_copy(fh[:, :, n, n + 6:KW], fs[:, :, n + 10:n + 11].broadcast_to([P, 2, 4 - n]))
                V.tensor_copy(fs[:, :, N + 5:N + 9], fs[:, :, N + 4:N + 5].broadcast_to([P, 2, 4])).then_inc(S["fh_ready"], 1)

                def row_max(t, par):
                    u = base + t
                    st = isinstance(t, int)
                    dve.wait_ge(S["s_done"], u + 1)
                    if not st or u >= 2:
                        dve.wait_ge(S["exp_done"], u - 1)
                    V.tensor_reduce(negmax[0:GROWS, par, 0, :],
                                    ps_s[0:GROWS, :, 0:4 * GROWS].rearrange("p g (h n) -> p g h n", h=4),
                                    AX.X, ALU.max).then_inc(S["rowmax"], 1)
                    dve.wait_ge(S["rowmax"], u + 1)
                    V.tensor_scalar(negmax[0:GROWS, par, 1, :], negmax[0:GROWS, par, 0, :], -0.125, None, ALU.mult)\
                        .then_inc(S["negmax_ready"], 1)

                def sums(t, par):
                    u = base + t
                    st = isinstance(t, int)
                    dve.wait_ge(S["exp_done"], u + 1)
                    if not st or u >= 2:
                        dve.wait_ge(S["norm_done"], u - 1)
                    V.reciprocal(rsum[0:GROWS, par, 1, :], rsum[0:GROWS, par, 0, :]).then_inc(S["recip_ready"], 1)

                def probs_out(t, par):
                    u = base + t
                    st = isinstance(t, int)
                    if not st or u >= 2:
                        dve.wait_ge(S["pv_done"], u - 1)
                    for g in range(2):
                        dve.wait_ge(S["t_done"], 2 * u + g + 1)
                        V.tensor_copy(pt_sb[0:GROWS, par, 4 * g:4 * g + 4, :],
                                      ps_pt[0:GROWS, g, 0:4 * GROWS].rearrange("p (h n) -> p h n", h=4)).then_inc(S["pt_ev"], 1)

                def add_centre(t, par):
                    u = base + t
                    n0 = n0_of(t)
                    dve.wait_ge(S["w_done"], u + 1)
                    if isinstance(t, int) and t == 0:
                        dve.wait_ge(S["hc_ready"], 2 * r + 2)
                    hcw = bass.AP(tensor=arena, offset=hc_off + n0, ap=[[ARENA, O], [1, BP], [0, KW]])
                    hv = hs[0:O, par, :].rearrange("p (n k) -> p n k", k=KW)
                    V.tensor_tensor(hv, ps_h[0:O, 0:BCOLS].rearrange("p (n k) -> p n k", k=KW), hcw, ALU.add)\
                        .then_inc(S["h_read"], 1)
                    dve.wait_ge(S["h_read"], u + 1)
                    tail = isinstance(t, int) and t == BODIES - 1
                    lo = BCOLS - TAIL_NEW * KW if tail else 0
                    ti = t if isinstance(t, int) else t
                    V.bn_stats(bass.AP(tensor=bstat, offset=ti * 6, ap=[[BODIES * 6, O], [1, 6]]), hs[0:O, par, lo:BCOLS])
                    last = V.tensor_reduce(bass.AP(tensor=arena, offset=mx_off + n0, ap=[[ARENA, O], [1, BP]]), hv,
                                           AX.X, ALU.max)
                    if tail:
                        last.then_inc(S["stats_ready"], 1)

                p0 = base % 2
                p1 = 1 - p0
                row_max(0, p0)
                sums(0, p0)
                row_max(1, p1)
                probs_out(0, p0)
                sums(1, p1)
                with dve.Fori(2, BODIES - 1, 2) as t:
                    row_max(t, p0)
                    add_centre(t - 2, p0)
                    probs_out(t - 1, p1)
                    sums(t, p0)
                    row_max(t + 1, p1)
                    add_centre(t - 1, p1)
                    probs_out(t, p0)
                    sums(t + 1, p1)
                row_max(BODIES - 1, p0)
                add_centre(BODIES - 3, p0)
                probs_out(BODIES - 2, p1)
                sums(BODIES - 1, p0)
                probs_out(BODIES - 1, p0)
                add_centre(BODIES - 2, p1)
                add_centre(BODIES - 1, p0)
                dve.wait_ge(S["stats_ready"], r + 1)
                norm_stats(O, bstat[0:O, :, :])
                link(V.tensor_scalar(mx[0:O, :], mx[0:O, :], small[0:O, 0:1], small[0:O, 2:3], ALU.subtract, ALU.mult))
                if layer == 0:
                    if b:
                        dve.wait_ge(S["feat_out"], 16)
                    dve.wait_ge(S["fnT_ps"], 2 + b)
                    dve.wait_ge(S["feat_out0"], 16)
                    V.scalar_tensor_tensor(f0[0:64, :], mx[0:64, :], 0.2, mx[0:64, :], ALU.mult, ALU.max).then_inc(S["feat_ready"], 1)
                    dve.wait_ge(S["fnT_ps"], 3 + b)
                    dve.wait_ge(scattered[b], 16 * METHODS * NBLK)
                    V.tensor_copy(fn[:, :, 64 * b:64 * b + 64], ps_f[:].rearrange("p (k c) -> p k c", k=NBLK)).then_inc(S["fnT_ev"], 1)
                else:
                    if b:
                        dve.wait_ge(S["h3_ps"], b)
                    dve.wait_ge(S["fsT_ps"], 4 * (r + 1))
                    V.scalar_tensor_tensor(f2, mx, 0.2, mx, ALU.mult, ALU.max).then_inc(S["feat_ready"], 1)
                    dve.wait_ge(S["h3_ps"], b + 1)
                    dve.wait_ge(S["feat_out"], 32)
                    q = slice(64 * b, 64 * b + 64)
                    V.tensor_copy(f0[q, :], ps_pt[q].rearrange("p h n -> p (h n)")).then_inc(S["h3_out"], 1)
            dve.wait_ge(S["h3_out"], 2)
            for h in range(2):
                link(V.bn_stats(bstat[:, h, :], f0[:, 512 * h:512 * h + 512]))
            norm_stats(P, bstat[:, 0:2, :])
            link(V.tensor_scalar(mx, f0, small[:, 0:1], small[:, 2:3], ALU.subtract, ALU.mult))
            link(V.scalar_tensor_tensor(mx, mx, 0.2, mx, ALU.mult, ALU.max))
            V.tensor_tensor(x[:], x[:], mx, ALU.add).then_inc(S["x1_ready"], 1)
            def layer_norm(n):
                dve.wait_ge(S["x1_ready"] if n == 0 else S["x_ready"], max(n, 1))
                if n:
                    dve.wait_ge(S["hT_ps"], 2 * n)
                link(V.bn_stats(bstat[:, 0, :], x[:, 0:512]))
                link(V.bn_stats(bstat[:, 1, :], x[:, 512:N]))
                norm_stats(P, bstat[:, 0:2, :])
                V.tensor_scalar(hn, x[:], small[:, 0:1], small[:, 2:3], ALU.subtract, ALU.mult).then_inc(S["hn_ready"], 1)

            def group_max(n, mask, scale):
                k = n % 2
                pr = (gp if n < AGROUPS else sp_)[:, k]
                dve.wait_ge(S["g_s"], n + 1)
                if n >= 2:
                    dve.wait_ge(S["g_t"], n - 1)
                V.tensor_tensor(pr, heads(ps_s[:, k], P), mask.unsqueeze(1).broadcast_to([P, 4, P]), ALU.add)\
                    .then_inc(S["g_masked"], 1)
                dve.wait_ge(S["g_masked"], n + 1)
                V.tensor_reduce(gsum[:, k, 0, :], pr, AX.X, ALU.max).then_inc(S["g_max"], 1)
                dve.wait_ge(S["g_max"], n + 1)
                V.tensor_scalar(gsum[:, k, 1, :], gsum[:, k, 0, :], -scale, None, ALU.mult).then_inc(S["g_negmax"], 1)

            def group_recip(n):
                dve.wait_ge(S["g_exp"], n + 1)
                V.reciprocal(gsum[:, n % 2, 3, :], gsum[:, n % 2, 2, :]).then_inc(S["g_recip"], 1)

            def groups(lo, hi, mask, scale):
                group_max(lo, mask, scale)
                for n in range(lo, hi):
                    if n + 1 < hi:
                        group_max(n + 1, mask, scale)
                    group_recip(n)

            def residual(n):
                dve.wait_ge(S["y_ps"], n)
                V.tensor_tensor(x[:, 0:512], x[:, 0:512], y_ps[0], ALU.add)
                V.tensor_tensor(x[:, 512:N], x[:, 512:N], y_ps[1], ALU.add).then_inc(S["x_ready"], 1)

            layer_norm(0)
            dve.wait_ge(S["late_in"], LATE)
            for i, v in enumerate((aq, ak)):
                dve.wait_ge(S["proj_ev"], 2 * i + 2)
                v4 = v.rearrange("p (h n t) -> p h n t", h=16, t=2)
                r4 = rot.rearrange("p (h n t) -> p h n t", h=16, t=2)
                s4 = sinn.rearrange("p (n t) -> p n t", t=2)
                for e in range(2):
                    last = V.tensor_tensor(r4[:, :, :, e], v4[:, :, :, 1 - e], s4[:, :, e].unsqueeze(1).broadcast_to([P, 16, 32]), ALU.mult)
                link(last)
                v3, r3 = heads(v, 64), heads(rot, 64)
                link(V.tensor_tensor(v3, v3, cosn.unsqueeze(1).broadcast_to([P, 16, 64]), ALU.mult))
                V.tensor_tensor(v3, v3, r3, ALU.add).then_inc(S["rope_ready"], 1)
                dve.wait_ge(S["rope_ready"], i + 1)
            groups(0, AGROUPS, causal, 0.125)
            residual(1)
            layer_norm(1)
            link(V.tensor_tensor(x[:], x[:], bbase, ALU.add))
            dve.wait_ge(S["proj_ev"], PROJ.index("gates") + 1)
            link(V.tensor_reduce(tiny[:, 0:1], gates[:, 128:136], AX.X, ALU.max))
            link(V.tensor_scalar(tiny[:, 1:2], tiny[:, 0:1], -1.0, None, ALU.mult))
            V.tensor_tensor(tiny[:, 3:4], gates[:, 136:137], bthr, ALU.add).then_inc(S["gate_max"], 1)
            dve.wait_ge(S["gate_exp"], 1)
            link(V.reciprocal(tiny[:, 5:6], tiny[:, 2:3]))
            link(V.tensor_scalar(tiny[:, 6:7], tiny[:, 4:5], 1.0, None, ALU.add))
            link(V.reciprocal(tiny[:, 7:8], tiny[:, 6:7]))
            link(V.tensor_scalar(tiny[:, 7:8], tiny[:, 7:8], 0.125, None, ALU.mult))
            link(V.tensor_scalar(tiny[:, 8:16], tiny[:, 8:16], tiny[:, 5:6], tiny[:, 7:8], ALU.mult, ALU.subtract))
            link(V.tensor_scalar(tiny[:, 8:16], tiny[:, 8:16], 0.0, None, ALU.max))
            link(V.tensor_reduce(tiny[:, 16:17], tiny[:, 8:16], AX.X, ALU.add))
            link(V.tensor_scalar(tiny[:, 17:18], tiny[:, 16:17], 0.0, None, ALU.is_equal))
            link(V.tensor_tensor(tiny[:, 18:19], tiny[:, 16:17], tiny[:, 17:18], ALU.add))
            link(V.reciprocal(tiny[:, 19:20], tiny[:, 18:19]))
            link(V.tensor_scalar(tiny[:, 24:32], tiny[:, 8:16], tiny[:, 19:20], 2.0, ALU.mult, ALU.mult))
            V.tensor_tensor(heads(lora, 16), heads(gates[:, 0:128], 16), tiny[:, 24:32].unsqueeze(2).broadcast_to([P, 8, 16]),
                            ALU.mult).then_inc(S["gate_ready"], 1)
            residual(2)
            layer_norm(2)
            root = float(P) ** -0.5

            def x_max(n):
                k = n % 2
                dve.wait_ge(S["t_s"], n + 1)
                V.tensor_reduce(xsum[:, k, 0:1], ps_s[:].rearrange("p g n -> p (g n)"), AX.X, ALU.max)
                link(V.tensor_reduce(xsum[:, k, 1:2], y_ps[0][:, 0:64], AX.X, ALU.max))
                link(V.tensor_reduce(xsum[:, k, 2:3], xsum[:, k, 0:2], AX.X, ALU.max))
                V.tensor_scalar(xsum[:, k, 3:4], xsum[:, k, 2:3], -root, None, ALU.mult).then_inc(S["t_max"], 1)

            def x_norm(n):
                k = n % 2
                dve.wait_ge(S["t_exp"], n + 1)
                link(V.tensor_tensor(xsum[:, k, 6:7], xsum[:, k, 4:5], xsum[:, k, 5:6], ALU.add))
                link(V.reciprocal(xsum[:, k, 7:8], xsum[:, k, 6:7]))
                V.tensor_scalar(xp[:, k, :], xp[:, k, :], xsum[:, k, 7:8], None, ALU.mult).then_inc(S["t_norm"], 1)

            x_max(0)
            x_norm(0)
            for n in range(1, XTILES):
                x_max(n)
                x_norm(n)
            residual(3)
            layer_norm(3)
            dve.wait_ge(S["late2_in"], LATE2)
            groups(AGROUPS, AGROUPS + SGROUPS, samebatch, root)
            residual(4)
            layer_norm(4)
            dve.wait_ge(S["proj_ev"], PROJ.index("route") + 1)
            link(V.tensor_tensor(route[:, 1, :], route[:, 0, :], rbias, ALU.add))
            link(V.tensor_reduce(tiny[:, 0:1], route[:, 1, :], AX.X, ALU.max))
            V.tensor_scalar(tiny[:, 1:2], tiny[:, 0:1], -1.0, None, ALU.mult).then_inc(S["route_max"], 1)
            dve.wait_ge(S["route_exp"], 1)
            link(V.reciprocal(tiny[:, 3:4], tiny[:, 2:3]))
            link(V.tensor_scalar(route[:, 2, :], route[:, 1, :], tiny[:, 3:4], None, ALU.mult))
            link(V.max(tiny[:, 8:16], route[:, 2, :]))
            link(V.match_replace(route[:, 3, :], tiny[:, 8:16], route[:, 2, :], -1.0))
            link(V.tensor_reduce(tiny[:, 16:17], tiny[:, 8:16], AX.X, ALU.add))
            V.scalar_tensor_tensor(route[:, 4, :], route[:, 3, :], 0.0, route[:, 2, :], ALU.is_lt, ALU.mult)\
                .then_inc(S["route_ready"], 1)
            dve.wait_ge(S["y_ps"], 5)
            for h in range(2):
                c = slice(512 * h, 512 * h + 512)
                last = V.scalar_tensor_tensor(hn[:, c], hn[:, c], tiny[:, 16:17], y_ps[h], ALU.mult, ALU.add)
            link(last)
            V.tensor_tensor(x[:], x[:], hn, ALU.add).then_inc(S["x_ready"], 1)


def host(inputs):
    import numpy as np
    g = {k: np.asarray(v) for k, v in inputs.items()}
    a = {}
    a["x"] = g["x"].reshape(P, N)
    ctx = g["ctx_4096"]
    a["coords"] = ctx[:, 0:3, :].reshape(B, 3, NBLK, P).transpose(3, 1, 0, 2).reshape(P, 3, 16)
    a["ident"] = np.eye(P, dtype=np.float32)
    a["identh"] = np.eye(P, dtype=np.float16)
    a["lower"] = np.tril(np.ones((P, P), np.float32), -1)
    a["rankoff"] = np.tile(np.repeat(np.arange(METHODS) * N, 16)[None].astype(np.float32), (P, 1))
    own = np.arange(GROWS) // KW == np.arange(GP)[:, None]
    root = BIG ** 0.5
    ml = np.full((GP + 1, GROWS), root, np.float16)
    ml[:GP] = own * root
    mr = np.full((GP + 1, GROWS), -root, np.float16)
    mr[:GP] = own * root
    ml, mr = (np.tile(np.pad(m, ((0, 64 - GP - 1), (0, 0))), (2, 1)) for m in (ml, mr))
    a["maskl"] = ml
    a["maskr"] = np.tile(mr, (1, 4))
    perms = ([2, 0, 3, 1], [1, 3, 0, 2])

    def lin(w, perm, lo):
        w = w.reshape(P, 2 * C, METHODS)[:, lo:lo + C, :]
        w = w[:, :, [perm.index(m) for m in range(METHODS)]]
        return w.reshape(P, 2, 2, 16, METHODS).transpose(0, 1, 2, 4, 3).reshape(P, 256)

    ws = [g["L0_xattn_W_lin1"], g["L0_xattn_W_lin2"]]
    a["wlin_n"] = np.stack([lin(w, p, C) for w, p in zip(ws, perms)], 1)
    a["wlin_c"] = np.stack([lin(w, p, 0) for w, p in zip(ws, perms)], 1)
    a["blin"] = np.stack([g["L0_xattn_b_lin1"], g["L0_xattn_b_lin2"]], 1)
    a["wconv0"] = g["L0_xattn_W_conv1"].T
    a["wconv1"] = g["L0_xattn_W_conv2"].T
    a["wconv3"] = g["L0_xattn_W_conv3"].T.reshape(2, P, 64).transpose(1, 0, 2)

    def wide(w):
        n = w.shape[1]
        return w.reshape(KT, P, n // 512, 512).transpose(2, 1, 0, 3).reshape(n // 512, P, CHUNK)

    def tall(w):
        return w.reshape(-1, 4, P, N).transpose(0, 2, 1, 3).reshape(-1, P, CHUNK)

    cx = ctx.reshape(B * N, N)
    chunks = [wide(g["L1_xattn_Wk"]), wide(g["L1_xattn_Wv"]), wide(cx.T),
              wide(g["L0_attn_wq"].T), wide(g["L0_attn_wk"].T), wide(g["L0_attn_wv"].T), tall(g["L0_attn_wo"].T),
              wide(g["L0_ffn_W_base"].T), wide(g["L1_xattn_Wq"]), tall(g["L1_xattn_Wo"]),
              wide(g["L1_attn_wq"].T), wide(g["L1_attn_wk"].T), wide(g["L1_attn_wv"].T), tall(g["L1_attn_wo"].T)]
    freq = (1.0 / np.float32(10000.0) ** (np.arange(0, 64, 2, dtype=np.float32) / np.float32(64))).astype(np.float32)
    ang = np.arange(C, dtype=np.float32)[:, None] * freq[None]
    a["cosn"] = np.tile(np.repeat(np.cos(ang), 2, axis=1), (B, 1))
    a["sinn"] = np.tile(np.repeat(np.sin(ang), 2, axis=1) * np.tile(np.array([-1, 1], np.float32), 32), (B, 1))
    tok = np.arange(P)
    same = tok[:, None] // C == tok[None] // C
    a["samebatch"] = np.where(same, 0, -BIG).astype(np.float32)
    a["causal"] = np.where(same & (tok[:, None] >= tok[None]), 0, -BIG).astype(np.float32)
    wg = np.concatenate([g["L0_ffn_A_w"].reshape(P, N), g["L0_ffn_W_gate"], g["L0_ffn_W_thr"][None]], 0)
    a["wgate"] = wg.T.reshape(KT, P, GATES).transpose(1, 0, 2)
    a["lora_b"] = g["L0_ffn_B_w"].transpose(0, 2, 1).reshape(P, N)
    a["bbase"] = g["L0_ffn_b_base"]
    a["bthr"] = g["L0_ffn_b_thr"]
    a["wroute"] = g["L1_ffn_router_weight"].T.reshape(KT, P, 64).transpose(1, 0, 2)
    a["rbias"] = g["L1_ffn_router_bias"]
    a["ebias"] = g["L1_ffn_expert_bias"]
    a["wstream"] = np.concatenate(chunks, 0)
    return {k: np.ascontiguousarray(v) for k, v in a.items()}


def kernel(**inputs):
    import numpy as _np
    import concourse.bacc as _bacc
    from concourse.bass_utils import run_bass_kernel_spmd as _run

    nc = _bacc.Bacc("TRN2", target_bir_lowering=False, num_devices=1)
    arrays = host(inputs)
    args = {n: nc.dram_tensor(f"in_{n}", v.shape, mybir.dt.from_np(v.dtype), kind="ExternalInput").ap()
            for n, v in arrays.items()}
    out = nc.dram_tensor("out_0", (P, N), F32, kind="ExternalOutput").ap()
    build(nc, args, out)
    r = _run(nc, [{f"in_{n}": v for n, v in arrays.items()}], core_ids=[0])
    return r.results[0]["out_0"].reshape(B, C, N)
```

```python
from contextlib import ExitStack

import concourse.bass as bass
from concourse import mybir

F32 = mybir.dt.float32
F16 = mybir.dt.float16
I32 = mybir.dt.int32
U32 = mybir.dt.uint32
ALU = mybir.AluOpType
ACT = mybir.ActivationFunctionType
AX = mybir.AxisListType

P = 128
B, C, N = 2, 64, 1024
NBLK = N // P
METHODS = 4
KW = 10
GP = 12
GROWS = GP * KW
BP = 2 * GP
BCOLS = BP * KW
BODIES = -(-N // BP)
TAIL_NEW = N - (BODIES - 1) * BP
RUNS = 2 * B
OUTC = (64, 128)
BIG = 2.0 ** 30
EPS = 1e-5
KT = N // P
KV = N + C
CHUNK = 4096
SLOTS = 3
ARENA = 18960


WEIGHTS = (["aq0", "aq1", "ak0", "ak1", "av0", "av1", "ao0", "ao1", "base0", "base1"]
           + [f"xq{i}" for i in range(8)] + ["xk", "xv"] + [f"xo{i}" for i in range(8)]
           + [f"sq{i}" for i in range(8)] + ["sk0", "sk1", "sv0", "sv1"] + [f"so{i}" for i in range(8)])
PROJ = (["aq0", "aq1", "ak0", "ak1", "av0", "av1", "gates"] + [f"xq{i}" for i in range(8)] + ["xk", "xv_b0", "xv_b1"]
        + [f"sq{i}" for i in range(8)] + ["sk0", "sk1", "sv0", "sv1", "route"])
GATES = 128 + 8 + 1
TURNS = (["aq0", "aq1", "ak0", "ak1"] + [f"xq{i}" for i in range(8)] + [f"sq{i}" for i in range(8)] + ["sk0", "sk1"])
AGROUPS = 4
SGROUPS = 8
XTILES = 32
KVT = 9


def build(nc, a, out):
    ctx = ExitStack()
    with ctx:
        def sb(name, shape, dt):
            return ctx.enter_context(nc.sbuf_tensor(name, shape, dt))

        def sem(name):
            return ctx.enter_context(nc.semaphore(name))

        def dram(name, shape, dt=F32):
            return nc.dram_tensor(name, shape, dt, kind="Internal").ap()

        x = sb("x", [P, N], F32)
        ident = sb("ident", [P, P], F32)
        identh = sb("identh", [P, P], F16)
        ring = sb("ring", [P, SLOTS, CHUNK], F32)
        keysT = sb("keysT", [P, 4, B * KV], F32)
        vals = sb("vals", [P, B * NBLK, 512], F32)
        small = sb("small", [P, 64], F32)
        bstat = sb("bstat", [P, BODIES, 6], F32)
        arena = sb("arena", [P, ARENA], F32)
        used = [0]

        def take(n, dt=F32):
            lo = used[0]
            used[0] += n
            assert used[0] <= ARENA, used[0]
            return arena[:, lo:lo + n]

        FSW = N + 12
        p_all = take(2 * 8 * GROWS)
        pt_all = take(2 * 8 * GROWS)
        vs_all = take(2 * 2 * 256)
        keyrow = arena[:, 0:4 * N].rearrange("p (m n) -> p m n", m=4)
        p_sb = p_all.rearrange("p (k g n) -> p k g n", k=2, g=8)
        pt_sb = pt_all.rearrange("p (k g n) -> p k g n", k=2, g=8)
        vs_sb = vs_all.rearrange("p (k g n) -> p k g n", k=2, g=2)
        o_off = used[0]
        o_sb = take(2 * 2 * BCOLS).rearrange("p (k t n) -> p k t n", k=2, t=2)
        hs = take(2 * BCOLS).rearrange("p (k n) -> p k n", k=2)
        xt = take(2 * BCOLS).bitcast(F16).rearrange("p (k t n) -> p k t n", k=2, t=2)
        fs_off = used[0]
        fs = take(2 * FSW).rearrange("p (t n) -> p t n", t=2)
        fc_off = used[0]
        fc = take(2 * N).rearrange("p (t n) -> p t n", t=2)
        fsr_off = used[0]
        fsr = take(NBLK * METHODS * C).rearrange("p (k c) -> p k c", c=C)
        fn = take(NBLK * P).rearrange("p (k c) -> p k c", k=NBLK)
        f0 = take(N)
        hc_off = used[0]
        hc = take(N)
        mx_off = used[0]
        mx = take(N)
        fsp = ring[:, 2, 0:2 * N].rearrange("p (k n) -> p k n", k=NBLK)
        c16 = ring[:, 2, 2 * N:3 * N].bitcast(F16)
        c32 = ring[:, 1, 2 * N:4 * N]
        fh = take(2 * 5 * KW).rearrange("p (t n k) -> p t n k", t=2, n=5)
        junk = take(N).bitcast(F16).rearrange("p (k n) -> p k n", k=2)
        flat = fsr.rearrange("p k c -> p (k c)")
        f2 = (ring[:, 1, 0:N], flat[:, 0:N])
        g01 = (ring[:, 1, N:2 * N], flat[:, N:2 * N])

        def scratch(lo, n, dt=F32):
            return arena[:, o_off + lo:o_off + lo + n].bitcast(dt)

        spot = [0]

        def place(n, *dims):
            lo = spot[0]
            spot[0] += n
            assert spot[0] <= ARENA, spot[0]
            return arena[:, lo:lo + n]

        def heads(ap, n):
            return ap.rearrange("p (h n) -> p h n", n=n)

        hn = place(N)
        hT = heads(place(N), P)
        common = spot[0]
        aq, ak, av, rot = place(N), place(N), place(N), place(N)
        aqT, akT, aoT = heads(place(N), P), heads(place(N), P), heads(place(N), P)
        gp = place(2 * 512).rearrange("p (k h n) -> p k h n", k=2, h=4)
        gpT = place(2 * 512).rearrange("p (k h n) -> p k h n", k=2, h=4)
        cosn, sinn, causal = place(64), place(64), place(P)
        wgate = place(KT * GATES).rearrange("p (k n) -> p k n", k=KT)
        lora_b, bbase = place(N), place(N)
        gates, lora, loraT, bthr = place(GATES + 1), place(P), place(P), place(1)
        spot[0] = common
        sq = place(4 * N)
        soT = heads(sq, P)
        xqT = place(4 * N).rearrange("p (b h n) -> p b h n", b=B, h=32)
        sqT = heads(arena[:, common + 4 * N:common + 8 * N], P)
        shared = spot[0]
        vlat = place(2 * 512).rearrange("p (b n) -> p b n", b=B)
        xp = place(2 * KV).rearrange("p (k n) -> p k n", k=2)
        xpT = place(2 * KVT * P).rearrange("p (k t n) -> p k t n", k=2, t=KVT)
        xtail = heads(place(XTILES * 64), 64)
        tailmax = place(XTILES)
        spot[0] = shared
        sk, sv, skT = place(N), place(N), heads(place(N), P)
        sp_ = place(2 * 512).rearrange("p (k h n) -> p k h n", k=2, h=4)
        spT = place(2 * 512).rearrange("p (k h n) -> p k h n", k=2, h=4)
        samebatch = place(P)
        wroute = place(KT * 64).rearrange("p (k n) -> p k n", k=KT)
        ebias, rbias = place(N), place(64)
        route = place(5 * 64).rearrange("p (k n) -> p k n", k=5)
        rT = place(P)
        gsum = sb("gsum", [P, 2, 4, 4], F32)
        xsum = sb("xsum", [P, 2, 8], F32)
        tiny = sb("tiny", [P, 40], F32)

        coord, quant, qtmp = (scratch(48 * i, 48).rearrange("p (i n) -> p i n", i=3) for i in range(3))
        qint = scratch(144, 48, I32).rearrange("p (i n) -> p i n", i=3)
        bits = scratch(192, 192, I32).rearrange("p (i m n) -> p i m n", i=3, m=METHODS)
        spread = scratch(384, 192, I32).rearrange("p (i m n) -> p i m n", i=3, m=METHODS)
        bt = scratch(576, 160, I32).rearrange("p (i n) -> p i n", i=5)
        key = sb("key", [P, 64], I32)
        expo = sb("expo", [P, 64], I32)
        ext = sb("ext", [P, 4, 6], F32)
        keycol = sb("keycol", [64, P], F32)
        cnt = sb("cnt", [P, 3, 64], F32)
        ranks = sb("ranks", [P, 64], F32)
        rankoff = sb("rankoff", [P, 64], F32)
        rowidx = sb("rowidx", [P, 64], U32)
        lower = sb("lower", [P, P], F32)
        maskl = sb("maskl", [P, GROWS], F16)
        maskr = sb("maskr", [P, 4 * GROWS], F16)
        wlin_n = sb("wlin_n", [P, 2, 256], F32)
        wlin_c = sb("wlin_c", [P, 2, 256], F32)
        blin = sb("blin", [P, 2], F32)
        wconv = [sb(f"wconv{l}", [P, OUTC[l]], F32) for l in range(2)]
        wconv3 = sb("wconv3", [P, 2, 64], F32)
        wp = [sb(f"wp{l}", [P, 2, OUTC[l]], F32) for l in range(2)]
        wc = [sb(f"wc{l}", [P, 2, OUTC[l]], F32) for l in range(2)]
        cb = sb("cb", [P, 2], F32)
        negmax = sb("negmax", [P, 2, 2, 8], F32)
        rsum = sb("rsum", [P, 2, 2, 8], F32)

        ps_s = ctx.enter_context(nc.psum_tensor("ps_s", [P, 2, 2, 512], F32))
        ps_pt = ctx.enter_context(nc.psum_tensor("ps_pt", [P, 2, 512], F32))
        ps_o = ctx.enter_context(nc.psum_tensor("ps_o", [P, 512], F32))
        ps_vh = ctx.enter_context(nc.psum_tensor("ps_vh", [P, 512], F32))
        ps_v = ps_vh[:, 0:256].bitcast(F16).rearrange("p (g n) -> p g n", g=2)
        ps_hg = ps_vh[:, 256:256 + BCOLS]
        ps_h, ps_f = ps_s[:, 1, 0], ps_s[:, 1, 1]
        y_ps = (ps_vh[:], ps_f)
        x_bank = (ps_o, ps_vh)
        proj_bank = (ps_o[:], ps_h)

        keys_d = dram("keys_d", (64, P))
        feat_d = [dram(f"feat_d{l}", (P, N)) for l in range(2)]
        sorted_d = [dram(f"sorted_d{r}", (METHODS * N, C)) for r in range(RUNS)]

        names = ("xk_in xv_in ctx0_in ctx1_in ctx2_in ctx3_in x_in coord_in const_in vchain minmax_ready minmax_all pow_ready pow_done ln_ready feat_out0 "
                 "keyT_ps keycol_ready keys_out keyrow_in keyrow_free rank_ready fnT_ps fnT_ev "
                 "fsr_in fsT_ps fsT_ev fc_in fh_ready wp_ps wp_ev c16_ready c32_ready hc_ps hc_ready "
                 "counted key_ready fsp_ready stats_ready h3_out ctx_ps ctx_ev "
                 "xt_ready s_done v_done t_done pv_done w_done rowmax negmax_ready exp_done recip_ready norm_done "
                 "v_ev pt_ev o_ev h_read feat_ready feat_out h3_ps x1_ready x_ready out_done "
                 "late_in late2_in hn_ready hT_ps hT_ev w_used proj_ps proj_ev rope_ready turn_ps turn_ev "
                 "g_s g_masked g_max g_negmax g_exp g_recip g_norm g_t g_tev g_pv g_oev tail_ps tail_ev tail_max "
                 "t_s t_max t_exp t_norm t_t t_tev t_pv t_oev y_ps gate_max gate_exp gate_ready gateT_ps gateT_ev "
                 "route_max route_exp route_ready routeT_ps routeT_ev dchain").split()
        S = {n: sem(n) for n in names}
        scattered = [sem(f"scattered{r}") for r in range(RUNS)]
        g01_in = [sem(f"g01_in{b}") for b in range(B)]
        slot_in = [sem(f"slot_in{i}") for i in range(SLOTS)]

        ctx_place = {"xk": ring[:, 0, :], "ctx0": ring[:, 2, :], "xv": ring[:, 1, :],
                     "ctx1": vals[:, NBLK:2 * NBLK, :].rearrange("p k n -> p (k n)"),
                     "ctx2": arena[:, fs_off:fs_off + CHUNK], "ctx3": ring[:, 2, :]}
        FIRST = ["xk", "ctx0", "xv", "ctx1", "ctx2", "ctx3"]
        stream_row = {nm: i for i, nm in enumerate(["xk", "xv", "ctx0", "ctx1", "ctx2", "ctx3"]
                                                   + [n for n in WEIGHTS if n not in ("xk", "xv")])}
        loads = {nm: (i % SLOTS, 16 * (i // SLOTS + 1)) for i, nm in enumerate(WEIGHTS)}

        summed = [nm for nm in WEIGHTS if nm[:2] in ("ao", "ba", "xo", "so") and nm not in ("ao1", "xo7", "so7")]

        def used_at(nm):
            if nm in summed:
                return S["w_used"], summed.index(nm) + 1
            if nm in ("ao1", "xo7", "so7"):
                return S["y_ps"], {"ao1": 1, "xo7": 3, "so7": 4}[nm]
            return S["proj_ps"], PROJ.index("xv_b1" if nm == "xv" else nm) + 1

        def chunk(eng, nm):
            s, v = loads[nm]
            eng.wait_ge(slot_in[s], v)
            return ring[:, s, :].rearrange("p (k n) -> p k n", n=N if nm[:2] in ("ao", "xo", "so") else 512)

        block = ctx.enter_context(nc.Block())

        def run_of(layer, b):
            return 2 * layer + b

        @block.sync
        def _(sp):
            sp.dma_start(coord, a["coords"]).then_inc(S["coord_in"], 16)
            sp.dma_start(x[:], a["x"]).then_inc(S["x_in"], 16)
            for dst, src in ((ident[:], "ident"), (identh[:], "identh"), (lower[:], "lower"),
                             (rankoff[:], "rankoff"), (maskl[:], "maskl"), (maskr[:], "maskr"),
                             (wlin_n[:], "wlin_n"), (wlin_c[:], "wlin_c"), (blin[:], "blin"),
                             (wconv[0][:], "wconv0"), (wconv[1][:], "wconv1"), (wconv3[:], "wconv3")):
                sp.dma_start(dst, a[src]).then_inc(S["const_in"], 16)
            def stream(lo, hi):
                for i in range(lo, hi):
                    if i >= SLOTS:
                        sp.wait_ge(*used_at(WEIGHTS[i - SLOTS]))
                    else:
                        sp.wait_ge(S["ctx_ps"], 32)
                    sp.dma_start(ring[:, i % SLOTS, :], a["wstream"][stream_row[WEIGHTS[i]]]).then_inc(slot_in[i % SLOTS], 16)

            def sorted_in(r):
                sp.wait_ge(scattered[r], 16 * METHODS * NBLK)
                if r:
                    sp.wait_ge(S["fsp_ready"], r)
                sp.dma_start(fsr, sorted_d[r].rearrange("(k q) c -> q k c", q=P)).then_inc(S["fsr_in"], 16)

            def centres_in(r):
                layer, b = divmod(r, B)
                if layer == 0:
                    sp.wait_ge(S["feat_out0"], 16)
                else:
                    sp.wait_ge(S["feat_out"], 16 * (b + 1))
                if r:
                    sp.wait_ge(S["xt_ready"], BODIES * r)
                    sp.wait_ge(S["c16_ready"], r)
                for t in range(2):
                    for h in range(2):
                        src = feat_d[layer]
                        sp.dma_start(fc[64 * h:64 * h + 64, t, :],
                                     bass.AP(tensor=src.tensor, offset=(64 * b + 32 * t + 16 * h) * N,
                                             ap=[[0, METHODS], [N, 16], [1, N]])).then_inc(S["fc_in"], 16)

            def earlier_in(b):
                sp.wait_ge(S["feat_out"], 16 * (b + 1))
                if b:
                    sp.wait_ge(S["fsp_ready"], RUNS)
                for l in range(2):
                    sp.dma_start(g01[b][64 * l:64 * l + 64, :], feat_d[l][64 * b:64 * b + 64, :]).then_inc(g01_in[b], 16)

            for nm in FIRST:
                if nm == "ctx3":
                    sp.wait_ge(S["ctx_ps"], 8)
                sp.dma_start(ctx_place[nm], a["wstream"][stream_row[nm]]).then_inc(S[nm + "_in"], 16)
            sp.wait_ge(S["ctx_ps"], 24)
            centres_in(0)
            sorted_in(0)
            stream(0, 1)
            for r in range(1, RUNS):
                sorted_in(r)
                centres_in(r)
                if r - 1 < B:
                    sp.wait_ge(S["feat_ready"], r)
                    sp.dma_start(feat_d[1][64 * (r - 1):64 * r, :], f0[0:64, :]).then_inc(S["feat_out"], 16)
            earlier_in(0)
            earlier_in(1)
            sp.wait_ge(S["fsT_ps"], 4 * RUNS)
            sp.wait_ge(S["c32_ready"], RUNS)
            stream(2, 3)
            sp.wait_ge(S["h3_ps"], B)
            stream(1, 2)
            sp.wait_ge(S["x1_ready"], 1)
            for dst, src in ((cosn, a["cosn"]), (sinn, a["sinn"]), (causal, a["causal"]), (wgate, a["wgate"]),
                             (lora_b, a["lora_b"]), (bbase, a["bbase"].partition_broadcast(P)),
                             (bthr, a["bthr"].partition_broadcast(P))):
                sp.dma_start(dst, src).then_inc(S["late_in"], 16)
            stream(SLOTS, WEIGHTS.index("sq0") + 3)
            sp.wait_ge(S["x_ready"], 3)
            for dst, src in ((samebatch, a["samebatch"]), (wroute, a["wroute"]), (ebias[0:64, :], a["ebias"]),
                             (rbias, a["rbias"].partition_broadcast(P))):
                sp.dma_start(dst, src).then_inc(S["late2_in"], 16)
            stream(WEIGHTS.index("sq0") + 3, len(WEIGHTS))
            sp.wait_ge(S["x_ready"], 5)
            sp.dma_start(out, x[:]).then_inc(S["out_done"], 16)
            sp.wait_ge(S["out_done"], 16)

        CONSTS = 16 * 12
        LATE, LATE2 = 16 * 7, 16 * 4

        def scatter(pool, r, j):
            layer, b = divmod(r, B)
            m, k = divmod(j, NBLK)
            if j == 0 and layer == 0:
                pool.wait_ge(S["rank_ready"], b + 1)
                pool.wait_ge(S["fnT_ev"], 2)
            elif j == 0:
                pool.wait_ge(S["fnT_ev"], 3 + b)
            col = (m * B + b) * NBLK + k
            pool.indirect_dma_start(
                out=sorted_d[r], out_offset=bass.IndirectOffsetOnAxis(ap=rowidx[:, col:col + 1], axis=0),
                in_=fn[:, k, 64 * b:64 * b + 64], in_offset=None).then_inc(scattered[r], 16)

        def n0_of(t):
            return t * BP if not isinstance(t, int) or t < BODIES - 1 else N - BP

        def win(t, lo, cnt):
            return bass.AP(tensor=arena, offset=fs_off + lo, ap=[[ARENA, P], [FSW, 2], [1, cnt], [1, KW]])

        def centre(lo, cnt):
            return bass.AP(tensor=arena, offset=fc_off + lo, ap=[[ARENA, P], [N, 2], [1, cnt], [0, KW]])

        def xt_body(pool, base, t, par):
            u = base + t
            par = par if not isinstance(t, int) else u % 2
            if not isinstance(t, int) or u >= 2:
                pool.wait_ge(S["v_done"], u - 1)
            dst = xt[:, par, :, :].rearrange("p t (n k) -> p t n k", k=KW)
            if isinstance(t, int) and t == 0:
                nc.gpsimd.tensor_tensor(dst[:, :, 0:5, :], fh, centre(0, 5), ALU.subtract)
                nc.gpsimd.tensor_tensor(dst[:, :, 5:BP, :], win(t, 5, BP - 5), centre(5, BP - 5), ALU.subtract)\
                    .then_inc(S["xt_ready"], 1)
            else:
                n0 = n0_of(t)
                nc.gpsimd.tensor_tensor(dst, win(t, n0, BP), centre(n0, BP), ALU.subtract).then_inc(S["xt_ready"], 1)

        def norm_half(pool, base, t, par, g):
            u = base + t
            par = par if not isinstance(t, int) else u % 2
            if True:
                pool.wait_ge(S["recip_ready"], 2 * u + g + 1)
                pr = p_sb[0:GROWS, par].rearrange("p (f g k) n -> p f g k n", f=2, g=2)[:, :, g]
                sums = rsum[0:GROWS, par, 1].rearrange("p (f g k) -> p f g k", f=2, g=2)[:, :, g]
                nc.gpsimd.tensor_tensor(pr, pr, sums.unsqueeze(3).broadcast_to([GROWS, 2, 2, GROWS]), ALU.mult)\
                    .then_inc(S["norm_done"], 1)

        @block.gpsimd
        def _(pool):
            pool.wait_ge(S["minmax_ready"], 1)
            nc.gpsimd.partition_all_reduce(ext[:, 2:4, :], ext[:, 0:2, :], P, bass.bass_isa.ReduceOp.max)\
                .then_inc(S["minmax_all"], 1)

            def powers(n, rows=P):
                pool.wait_ge(S["pow_ready"], n)
                nc.gpsimd.tensor_tensor(small[0:rows, 2:3], small[0:rows, 1:2], small[0:rows, 8:9], ALU.pow)\
                    .then_inc(S["pow_done"], 1)

            powers(1)
            pool.wait_ge(S["ln_ready"], 1)
            pool.dma_start(feat_d[0], f0).then_inc(S["feat_out0"], 16)
            pool.wait_ge(S["keycol_ready"], 1)
            pool.dma_start(keys_d, keycol[:]).then_inc(S["keys_out"], 16)
            pool.wait_ge(S["keys_out"], 16)
            kd = keys_d.rearrange("(m b k) q -> b m (k q)", m=METHODS, b=B)
            pool.dma_start(keyrow, kd[0].partition_broadcast(P)).then_inc(S["keyrow_in"], 16)
            pool.wait_ge(S["keyrow_free"], 1)
            pool.dma_start(keyrow, kd[1].partition_broadcast(P)).then_inc(S["keyrow_in"], 16)
            for j in range(METHODS * NBLK):
                scatter(pool, 0, j)
            for r in range(RUNS):
                layer, b = divmod(r, B)
                pool.wait_ge(S["fsT_ev"], 4 * (r + 1))
                pool.wait_ge(S["fh_ready"], r + 1)
                pool.wait_ge(S["fc_in"], 64 * (r + 1))
                base = BODIES * r
                p0 = base % 2
                p1 = 1 - p0
                xt_body(pool, base, 0, p0)
                if r:
                    powers(1 + r, OUTC[(r - 1) // B])
                xt_body(pool, base, 1, p1)
                xt_body(pool, base, 2, p0)
                norm_half(pool, base, 0, p0, 0)

                def step(t, par):
                    norm_half(pool, base, t, par, 1)
                    if not isinstance(t, int) or t + 3 < BODIES:
                        xt_body(pool, base, t + 3, 1 - par)
                    if not isinstance(t, int) or t + 1 < BODIES:
                        norm_half(pool, base, t + 1, 1 - par, 0)

                if r + 1 < RUNS:
                    for t in range(BODIES):
                        step(t, (base + t) % 2)
                        if 0 <= t - 3 < METHODS * NBLK:
                            scatter(pool, r + 1, t - 3)
                else:
                    step(0, p0)
                    with pool.Fori(1, BODIES - 4, 2) as t:
                        step(t, p1)
                        step(t + 1, p0)
                    for t in range(BODIES - 4, BODIES):
                        step(t, (base + t) % 2)
            powers(1 + RUNS, OUTC[1])
            powers(2 + RUNS)
            def normalise(n):
                pool.wait_ge(S["g_recip"], n + 1)
                pr = (gp if n < AGROUPS else sp_)[:, n % 2]
                nc.gpsimd.tensor_tensor(pr, pr, gsum[:, n % 2, 3, :].unsqueeze(2).broadcast_to([P, 4, P]), ALU.mult)\
                    .then_inc(S["g_norm"], 1)

            powers(3 + RUNS)
            for n in range(AGROUPS):
                normalise(n)
            powers(4 + RUNS)
            powers(5 + RUNS)
            powers(6 + RUNS)
            for n in range(AGROUPS, AGROUPS + SGROUPS):
                normalise(n)
            powers(7 + RUNS)

        def ctx_chunk(pe, c):
            if c == 0:
                pe.wait_ge(S["xk_in"], 16)
            pe.wait_ge(S[f"ctx{c}_in"], 16)
            cx = ctx_place[f"ctx{c}"].rearrange("p (k n) -> p k n", k=KT)
            wk = ring[:, 0, :].rearrange("p (k n) -> p k n", k=KT)
            wv = ring[:, 1, :].rearrange("p (k n) -> p k n", k=KT)
            for j in range(8):
                g = 8 * c + j
                if g >= 2:
                    pe.wait_ge(S["ctx_ev"], g - 1)
                bank = (ps_o[:], ps_h)[g % 2]
                q = j % 4
                if g == 4:
                    pe.wait_ge(S["xv_in"], 16)
                for k in range(KT):
                    if j < 4:
                        mm = nc.tensor.matmul(bank, wk[:, k, q * P:(q + 1) * P], cx[:, k, :], start=k == 0, stop=k == KT - 1)
                    else:
                        mm = nc.tensor.matmul(bank, cx[:, k, q * P:(q + 1) * P], wv[:, k, :], start=k == 0, stop=k == KT - 1)
                mm.then_inc(S["ctx_ps"], 1)

        def sorted_transposes(pe, r, t):
            pe.wait_ge(S["fsp_ready"], r + 1)
            par = (BODIES * r + t) % 2
            if r:
                pe.wait_ge(S["exp_done"], 2 * (BODIES * r - 1 + t))
            for h in range(2):
                for k in range(4):
                    src = fsp[:, 4 * h + k, 128 * t:128 * t + 128]
                    mm = nc.tensor.transpose(ps_s[:, par, h, k * P:(k + 1) * P], src, ident[:])
                mm.then_inc(S["fsT_ps"], 1)

        @block.tensor
        def _(pe):
            pe.wait_ge(S["const_in"], CONSTS)
            pe.wait_ge(S["ln_ready"], 1)
            for h in range(2):
                if h:
                    pe.wait_ge(S["fnT_ev"], h)
                for k in range(4):
                    mm = nc.tensor.transpose(ps_f[:, k * P:(k + 1) * P], f0[:, (4 * h + k) * P:(4 * h + k + 1) * P], ident[:])
                mm.then_inc(S["fnT_ps"], 1)
            ctx_chunk(pe, 0)
            pe.wait_ge(S["key_ready"], 1)
            pe.wait_ge(S["fnT_ev"], 2)
            nc.tensor.transpose(ps_f[0:64, 0:P], key[:].bitcast(F32), ident[:]).then_inc(S["keyT_ps"], 1)
            for c in range(1, 4):
                ctx_chunk(pe, c)
            for l in range(2):
                O = OUTC[l]
                bank = ps_s[:, 0, l]
                for t in range(2):
                    nc.tensor.matmul(bank[:, t * P:t * P + O], wlin_n[:, l, t * P:(t + 1) * P], wconv[l][:], start=True, stop=True)
                bank = (ps_pt[:, 0], ps_pt[:, 1])[l]
                for t in range(2):
                    nc.tensor.matmul(bank[:, t * P:t * P + O], wlin_c[:, l, t * P:(t + 1) * P], wconv[l][:], start=True, stop=True)
                mm = nc.tensor.matmul(bank[0:O, 256:257], wconv[l][:], blin[:, l:l + 1], start=True, stop=True)
            mm.then_inc(S["wp_ps"], 1)
            pe.wait_ge(S["wp_ev"], 1)
            pe.wait_ge(S["keycol_ready"], 1)
            pe.wait_ge(S["ctx_ev"], 32)
            for t in range(2):
                sorted_transposes(pe, 0, t)
            for r in range(RUNS):
                layer, b = divmod(r, B)
                O = OUTC[layer]
                base = BODIES * r

                def centre_output(h):
                    pe.wait_ge(S["c32_ready"], r + 1)
                    if r:
                        pe.wait_ge(S["pt_ev"], 2 * base)
                    for t in range(2):
                        mm = nc.tensor.matmul(ps_pt[0:O, h, :], wc[layer][:, t, :], c32[:, N * t + 512 * h:N * t + 512 * h + 512],
                                              start=t == 0, stop=t == 1)
                    mm.then_inc(S["hc_ps"], 1)

                def scores(t, par):
                    u = base + t
                    st = isinstance(t, int)
                    pe.wait_ge(S["xt_ready"], u + 1)
                    if not st or u >= 2:
                        pe.wait_ge(S["exp_done"], 2 * u - 2)
                    for half in range(2):
                        q = slice(64 * half, 64 * half + 64)
                        nc.tensor.matmul(ps_s[0:GROWS, par, half, 0:4 * GROWS], maskl[q, :], maskr[q, :], start=True, stop=False,
                                         skip_group_check=True)
                        for g in range(2):
                            for k in range(2):
                                c0 = (2 * g + k) * GROWS
                                xs = xt[q, par, k, g * GROWS:(g + 1) * GROWS]
                                mm = nc.tensor.matmul(ps_s[0:GROWS, par, half, c0:c0 + GROWS], xs, xs, start=False,
                                                      stop=(g, k) == (1, 1), skip_group_check=True)
                    mm.then_inc(S["s_done"], 1)

                def values(t, par):
                    u = base + t
                    st = isinstance(t, int)
                    pe.wait_ge(S["xt_ready"], u + 1)
                    if not st or u >= 1:
                        pe.wait_ge(S["v_ev"], u)
                    if not st or t >= 3:
                        pe.wait_ge(S["h_read"], u - 2)
                    elif r:
                        pe.wait_ge(S["h_read"], base)
                    for g in range(2):
                        for k in range(2):
                            mm = nc.tensor.transpose(ps_v[0:GROWS, g, k * P:(k + 1) * P],
                                                     xt[:, par, k, g * GROWS:(g + 1) * GROWS], identh[:])
                    mm.then_inc(S["v_done"], 1)

                def turn_probs(t, par, g):
                    u = base + t
                    st = isinstance(t, int)
                    if st and t == 0:
                        pe.wait_ge(S["hc_ready"], 2 * r + g + 1)
                    if not st or u >= 1:
                        pe.wait_ge(S["pt_ev"], 2 * u + g - 1)
                    pe.wait_ge(S["norm_done"], 2 * u + g + 1)
                    for h in range(4):
                        mm = nc.tensor.transpose(ps_pt[0:GROWS, g, h * GROWS:(h + 1) * GROWS],
                                                 p_sb[0:GROWS, par, 4 * (h % 2) + 2 * g + h // 2, :],
                                                 ident[0:GROWS, 0:GROWS])
                    mm.then_inc(S["t_done"], 1)

                def attend(t, par):
                    u = base + t
                    st = isinstance(t, int)
                    pe.wait_ge(S["v_ev"], u + 1)
                    if not st or u >= 1:
                        pe.wait_ge(S["o_ev"], u)
                    for g in range(2):
                        pe.wait_ge(S["pt_ev"], 2 * u + g + 1)
                        for h in range(4):
                            q = 64 * (h % 2)
                            c0 = (h // 2) * BCOLS + g * GROWS
                            mm = nc.tensor.matmul(ps_o[q:q + 64, c0:c0 + GROWS], vs_sb[0:GROWS, par, g, 64 * h:64 * h + 64],
                                                  pt_sb[0:GROWS, par, 4 * g + h, :], start=True, stop=True)
                    mm.then_inc(S["pv_done"], 1)

                def project(t, par):
                    u = base + t
                    st = isinstance(t, int)
                    pe.wait_ge(S["o_ev"], u + 1)
                    pe.wait_ge(S["v_ev"], base + BODIES if st and t >= BODIES - 2 else u + 3)
                    if not st or u >= 1:
                        pe.wait_ge(S["h_read"], u)
                    for k in range(2):
                        mm = nc.tensor.matmul(ps_hg[0:O, :], wp[layer][:, k, :], o_sb[:, par, k, :],
                                              start=k == 0, stop=k == 1)
                    mm.then_inc(S["w_done"], 1)

                def batch_features(b):
                    pe.wait_ge(S["feat_ready"], b + 1)
                    pe.wait_ge(S["o_ev"], base)
                    for k in range(NBLK):
                        mm = nc.tensor.transpose(ps_o[:, k * 64:(k + 1) * 64], f0[0:64, k * P:(k + 1) * P], ident[0:64, 0:64])
                    mm.then_inc(S["fnT_ps"], 1)
                    pe.wait_ge(S["fnT_ev"], 3 + b)

                p0 = base % 2
                p1 = 1 - p0
                scores(0, p0)
                values(0, p0)
                centre_output(0)
                scores(1, p1)
                centre_output(1)

                def step(t, par, last=False):
                    turn_probs(t, par, 0)
                    if not isinstance(t, int) or t + 2 < BODIES:
                        scores(t + 2, par)
                    if last and r + 1 < RUNS:
                        sorted_transposes(pe, r + 1, 0)
                    if not last:
                        values(t + 1, 1 - par)
                    turn_probs(t, par, 1)
                    if last and r + 1 < RUNS:
                        sorted_transposes(pe, r + 1, 1)
                    if isinstance(t, int) and t == 0 and 0 < r <= B:
                        batch_features(r - 1)
                    if not isinstance(t, int) or t:
                        project(t - 1, 1 - par)
                    attend(t, par)

                step(0, p0)
                step(1, p1)
                step(2, p0)
                with pe.Fori(3, BODIES - 2, 2) as t:
                    step(t, p1)
                    step(t + 1, p0)
                step(BODIES - 2, p1)
                step(BODIES - 1, p0, last=True)
                project(BODIES - 1, p0)
            for b in range(B):
                pe.wait_ge(S["feat_ready"], B + b + 1)
                pe.wait_ge(g01_in[b], 32)
                pe.wait_ge(S["pt_ev"], 2 * BODIES * RUNS)
                for h in range(2):
                    cols = slice(512 * h, 512 * h + 512)
                    nc.tensor.matmul(ps_pt[64 * b:64 * b + 64, h, :], wconv3[:, 0, :], g01[b][:, cols], start=True, stop=False)
                    mm = nc.tensor.matmul(ps_pt[64 * b:64 * b + 64, h, :], wconv3[:, 1, :], f2[b][:, cols], start=False, stop=True)
                mm.then_inc(S["h3_ps"], 1)

            def transpose_tokens(n):
                pe.wait_ge(S["hn_ready"], n + 1)
                for h in range(2):
                    for k in range(4):
                        mm = nc.tensor.transpose(ps_pt[:, h, k * P:(k + 1) * P], hn[:, (4 * h + k) * P:(4 * h + k + 1) * P], ident[:])
                    mm.then_inc(S["hT_ps"], 1)
                pe.wait_ge(S["hT_ev"], 2 * n + 2)

            def bank_for(nm):
                g = PROJ.index(nm)
                if g >= 2:
                    pe.wait_ge(S["proj_ev"], g - 1)
                return proj_bank[g % 2]

            def project_tokens(nm):
                w = chunk(pe, nm)
                bank = bank_for(nm)
                for k in range(KT):
                    mm = nc.tensor.matmul(bank, hT[:, k, :], w[:, k, :], start=k == 0, stop=k == KT - 1)
                mm.then_inc(S["proj_ps"], 1)

            def small_product(nm, w, cols):
                bank = bank_for(nm)
                for k in range(KT):
                    mm = nc.tensor.matmul(bank[:, 0:cols], hT[:, k, :], w[:, k, :], start=k == 0, stop=k == KT - 1)
                mm.then_inc(S["proj_ps"], 1)

            def turn(nm, src):
                n = TURNS.index(nm)
                pe.wait_ge(S["proj_ev"] if nm[0] != "a" else S["rope_ready"],
                           PROJ.index(nm) + 1 if nm[0] != "a" else 1 + ("ak" in nm))
                if n >= 2:
                    pe.wait_ge(S["turn_ev"], n - 1)
                for k in range(4):
                    mm = nc.tensor.transpose(ps_pt[:, n % 2, k * P:(k + 1) * P], src[:, k * P:(k + 1) * P], ident[:])
                mm.then_inc(S["turn_ps"], 1)

            def group_scores(n):
                if n >= 2:
                    pe.wait_ge(S["g_masked"], n - 1)
                bank = ps_s[:, 0, n % 2]
                for i in range(4):
                    if n < AGROUPS:
                        q, t = slice(64 * (n % 2), 64 * (n % 2) + 64), 4 * (n // 2) + i
                        l, r = aqT[q, t, :], akT[q, t, :]
                    else:
                        l, r = sqT[:, 4 * (n - AGROUPS) + i, :], skT[:, n - AGROUPS, :]
                    mm = nc.tensor.matmul(bank[:, i * P:(i + 1) * P], l, r, start=True, stop=True)
                mm.then_inc(S["g_s"], 1)

            def group_turn(n):
                pe.wait_ge(S["g_norm"], n + 1)
                if n >= 2:
                    pe.wait_ge(S["g_tev"], n - 1)
                pr = (gp if n < AGROUPS else sp_)[:, n % 2]
                for i in range(4):
                    mm = nc.tensor.transpose(ps_pt[:, n % 2, i * P:(i + 1) * P], pr[:, i, :], ident[:])
                mm.then_inc(S["g_t"], 1)

            def group_outputs(n):
                pe.wait_ge(S["g_tev"], n + 1)
                if n >= 2:
                    pe.wait_ge(S["g_oev"], n - 1)
                bank = proj_bank[n % 2]
                if n < AGROUPS:
                    q = 64 * (n % 2)
                    for i in range(4):
                        c = (4 * (n // 2) + i) * P + q
                        mm = nc.tensor.matmul(bank[q:q + 64, i * P:(i + 1) * P], av[:, c:c + 64], gpT[:, n % 2, i, :],
                                              start=True, stop=True)
                else:
                    c = (n - AGROUPS) * P
                    mm = nc.tensor.matmul(bank, sv[:, c:c + P], spT[:, n % 2].rearrange("p h n -> p (h n)"), start=True, stop=True)
                mm.then_inc(S["g_pv"], 1)

            def groups(lo, hi):
                group_scores(lo)
                group_scores(lo + 1)
                for n in range(lo, hi):
                    group_turn(n)
                    if n + 2 < hi:
                        group_scores(n + 2)
                    group_outputs(n)

            def output_map(names, oT):
                for j, nm in enumerate(names):
                    w = chunk(pe, nm)
                    for k in range(4):
                        for h in range(2):
                            mm = nc.tensor.matmul(y_ps[h], oT[:, 4 * j + k, :], w[:, k, 512 * h:512 * h + 512],
                                                  start=(j, k) == (0, 0), stop=(j, k) == (len(names) - 1, 3),
                                                  skip_group_check=True)
                    mm.then_inc(S["y_ps"] if j == len(names) - 1 else S["w_used"], 1)

            transpose_tokens(0)
            for nm in ("aq0", "aq1", "ak0", "ak1", "av0", "av1"):
                project_tokens(nm)
            for nm, src in (("aq0", aq[:, 0:512]), ("aq1", aq[:, 512:N]), ("ak0", ak[:, 0:512]), ("ak1", ak[:, 512:N])):
                turn(nm, src)
            pe.wait_ge(S["turn_ev"], 4)
            pe.wait_ge(S["proj_ev"], 6)
            groups(0, AGROUPS)
            pe.wait_ge(S["g_oev"], AGROUPS)
            output_map(["ao0", "ao1"], aoT)
            transpose_tokens(1)
            pe.wait_ge(S["late_in"], LATE)
            small_product("gates", wgate, GATES)
            for h in range(2):
                w = chunk(pe, f"base{h}")
                for k in range(KT):
                    mm = nc.tensor.matmul(y_ps[h], hT[:, k, :], w[:, k, :], start=k == 0, stop=False, skip_group_check=True)
                mm.then_inc(S["w_used"], 1)
            pe.wait_ge(S["gate_ready"], 1)
            nc.tensor.transpose(ps_pt[:, 0, 0:P], lora, ident[:]).then_inc(S["gateT_ps"], 1)
            pe.wait_ge(S["gateT_ev"], 1)
            for h in range(2):
                mm = nc.tensor.matmul(y_ps[h], loraT, lora_b[:, 512 * h:512 * h + 512], start=False, stop=True, skip_group_check=True)
            mm.then_inc(S["y_ps"], 1)
            transpose_tokens(2)
            for i in range(8):
                project_tokens(f"xq{i}")
                if i:
                    turn(f"xq{i - 1}", sq[:, 512 * (i - 1):512 * i])
            turn("xq7", sq[:, 512 * 7:512 * 8])
            w = chunk(pe, "xk")
            bank = bank_for("xk")
            for h in range(4):
                for k in range(KT):
                    mm = nc.tensor.matmul(bank[:, h * P:(h + 1) * P], w[:, k, h * P:(h + 1) * P], hT[:, k, :], start=k == 0, stop=k == KT - 1)
            mm.then_inc(S["proj_ps"], 1)
            w = chunk(pe, "xv")
            for b in range(B):
                bank = bank_for(f"xv_b{b}")
                for k in range(KT):
                    mm = nc.tensor.matmul(bank[0:64, :], hT[:, k, 64 * b:64 * b + 64], w[:, k, :], start=k == 0, stop=k == KT - 1)
                mm.then_inc(S["proj_ps"], 1)
            pe.wait_ge(S["proj_ev"], PROJ.index("xv_b1") + 1)
            pe.wait_ge(S["turn_ev"], TURNS.index("xq7") + 1)

            def x_scores(n):
                b, h, g = n // 16, n // 4 % 4, n % 4
                if n >= 2:
                    pe.wait_ge(S["t_exp"], n - 1)
                else:
                    pe.wait_ge(S["x_ready"], 2)
                l = xqT[:, b, 8 * h + 2 * g:8 * h + 2 * g + 2, :].rearrange("p h n -> p (h n)")
                for c in range(2):
                    lo = b * KV + 512 * c
                    mm = nc.tensor.matmul(ps_s[:, n % 2, c], l, keysT[:, h, lo:lo + 512], start=True, stop=True)
                mm.then_inc(S["t_s"], 1)

            def tail_scores(c):
                if c >= 2:
                    pe.wait_ge(S["tail_ev"], c - 1)
                for n in range(8 * c, 8 * c + 8):
                    b, h, g = n // 16, n // 4 % 4, n % 4
                    l = xqT[:, b, 8 * h + 2 * g:8 * h + 2 * g + 2, :].rearrange("p h n -> p (h n)")
                    mm = nc.tensor.matmul(x_bank[c % 2][:, 64 * (n % 8):64 * (n % 8) + 64], l,
                                          keysT[:, h, b * KV + N:b * KV + KV], start=True, stop=True)
                mm.then_inc(S["tail_ps"], 1)

            def x_turn(n, js):
                pe.wait_ge(S["t_norm"], n + 1)
                for j in js:
                    m = 3 * n + j
                    if m >= 2:
                        pe.wait_ge(S["t_tev"], m - 1)
                    for k in range(4 * j, min(4 * j + 4, KVT)):
                        w = P if k < KVT - 1 else 64
                        mm = nc.tensor.transpose(ps_pt[0:w, m % 2, (k % 4) * P:(k % 4 + 1) * P], xp[:, n % 2, k * P:k * P + w], ident[:])
                    mm.then_inc(S["t_t"], 1)

            def x_outputs(n):
                b, h, g = n // 16, n // 4 % 4, n % 4
                pe.wait_ge(S["t_tev"], 3 * n + 3)
                if n >= 2:
                    pe.wait_ge(S["t_oev"], n - 1)
                for k in range(KVT):
                    if k < KVT - 1:
                        l, r = vals[:, NBLK * b + k, h * P:(h + 1) * P], xpT[:, n % 2, k, :]
                    else:
                        l, r = vlat[0:64, b, h * P:(h + 1) * P], xpT[0:64, n % 2, k, :]
                    mm = nc.tensor.matmul(x_bank[n % 2][:, 0:P], l, r, start=k == 0, stop=k == KVT - 1)
                mm.then_inc(S["t_pv"], 1)

            tail_scores(0)
            x_scores(0)
            x_scores(1)
            for c in range(1, 4):
                tail_scores(c)
            for n in range(XTILES):
                x_turn(n, (0, 1))
                if n + 2 < XTILES:
                    x_scores(n + 2)
                x_turn(n, (2,))
                x_outputs(n)
            pe.wait_ge(S["t_oev"], XTILES)
            output_map([f"xo{i}" for i in range(8)], soT)
            transpose_tokens(3)
            for i in range(8):
                project_tokens(f"sq{i}")
                if i:
                    turn(f"sq{i - 1}", sq[:, 512 * (i - 1):512 * i])
            turn("sq7", sq[:, 512 * 7:512 * 8])
            for nm in ("sk0", "sk1", "sv0", "sv1"):
                project_tokens(nm)
            turn("sk0", sk[:, 0:512])
            turn("sk1", sk[:, 512:N])
            pe.wait_ge(S["turn_ev"], len(TURNS))
            pe.wait_ge(S["proj_ev"], PROJ.index("sv1") + 1)
            groups(AGROUPS, AGROUPS + SGROUPS)
            pe.wait_ge(S["g_oev"], AGROUPS + SGROUPS)
            output_map([f"so{i}" for i in range(8)], soT)
            transpose_tokens(4)
            pe.wait_ge(S["late2_in"], LATE2)
            small_product("route", wroute, 64)
            pe.wait_ge(S["route_ready"], 1)
            nc.tensor.transpose(ps_pt[0:64, 0, 0:P], route[:, 4, :], ident[:]).then_inc(S["routeT_ps"], 1)
            pe.wait_ge(S["routeT_ev"], 1)
            for h in range(2):
                mm = nc.tensor.matmul(y_ps[h], rT[0:64, :], ebias[0:64, 512 * h:512 * h + 512], start=True, stop=True)
            mm.then_inc(S["y_ps"], 1)

        @block.scalar
        def _(act):
            for h in range(2):
                act.wait_ge(S["fnT_ps"], h + 1)
                nc.scalar.copy(fn[:, 4 * h:4 * h + 4, :], ps_f.rearrange("p (k c) -> p k c", k=4)).then_inc(S["fnT_ev"], 1)
            for g in range(32):
                c, j = divmod(g, 8)
                if g == 8:
                    act.wait_ge(S["keyT_ps"], 1)
                    nc.scalar.copy(keycol[:], ps_f[0:64, 0:P]).then_inc(S["keycol_ready"], 1)
                act.wait_ge(S["ctx_ps"], g + 1)
                bank = (ps_o[:], ps_h)[g % 2]
                if j < 4:
                    lo = (c // 2) * KV + (c % 2) * 512
                    dst = keysT[:, j, lo:lo + 512]
                else:
                    dst = vals[:, 4 * c + j - 4, :]
                nc.scalar.copy(dst, bank).then_inc(S["ctx_ev"], 1)
            act.wait_ge(S["wp_ps"], 1)
            for l in range(2):
                O = OUTC[l]
                for t in range(2):
                    nc.scalar.copy(wp[l][:, t, :], ps_s[:, 0, l, t * P:t * P + O])
                    nc.scalar.copy(wc[l][:, t, :], ps_pt[:, l, t * P:t * P + O])
                cp = nc.scalar.copy(cb[0:O, l:l + 1], ps_pt[0:O, l, 256:257])
            cp.then_inc(S["wp_ev"], 1)
            def regroup(r):
                act.wait_ge(S["fsr_in"], 16 * (r + 1))
                if r:
                    act.wait_ge(S["fsT_ps"], 4 * r)
                for m in range(METHODS):
                    cp = nc.scalar.copy(fsp.rearrange("p k (h m c) -> p m k h c", h=4, m=METHODS)[:, m],
                                        fsr.rearrange("p (m k) (h c) -> p m k h c", m=METHODS, h=4)[:, m])
                cp.then_inc(S["fsp_ready"], 1)

            def sorted_out(r, t):
                par = (BODIES * r + t) % 2
                if r:
                    act.wait_ge(S["xt_ready"], BODIES * r)
                for h in range(2):
                    act.wait_ge(S["fsT_ps"], 4 * r + 2 * t + h + 1)
                    nc.scalar.copy(fs[:, t, 5 + 512 * h:5 + 512 * h + 512], ps_s[:, par, h]).then_inc(S["fsT_ev"], 1)

            regroup(0)
            sorted_out(0, 0)
            sorted_out(0, 1)
            for r in range(RUNS):
                layer, b = divmod(r, B)
                O = OUTC[layer]
                base = BODIES * r

                def centre_out(h):
                    act.wait_ge(S["hc_ps"], 2 * r + h + 1)
                    if r:
                        act.wait_ge(S["h_read"], base)
                    nc.scalar.activation(hc[0:O, 512 * h:512 * h + 512], ps_pt[0:O, h], ACT.Identity,
                                         bias=cb[0:O, layer:layer + 1]).then_inc(S["hc_ready"], 1)

                def values_out(t, par):
                    u = base + t
                    st = isinstance(t, int)
                    act.wait_ge(S["v_done"], u + 1)
                    if not st or u >= 2:
                        act.wait_ge(S["pv_done"], u - 1)
                    nc.scalar.copy(vs_sb[0:GROWS, par, :, :], ps_v[0:GROWS, :, 0:256]).then_inc(S["v_ev"], 1)

                def exponentials(t, par, g):
                    u = base + t
                    st = isinstance(t, int)
                    act.wait_ge(S["negmax_ready"], u + 1)
                    if not st or u >= 2:
                        act.wait_ge(S["t_done"], 2 * u - 3 + g)
                    for n in (2 * g, 2 * g + 1, 4 + 2 * g, 5 + 2 * g):
                        e = nc.scalar.activation(p_sb[0:GROWS, par, n, :],
                                                 ps_s[0:GROWS, par, n // 4, (n % 4) * GROWS:(n % 4 + 1) * GROWS], ACT.Exp,
                                                 bias=negmax[0:GROWS, par, 1, n:n + 1], scale=0.125,
                                                 accum_out=rsum[0:GROWS, par, 0, n:n + 1])
                    e.then_inc(S["exp_done"], 1)

                def outputs_out(t, par):
                    u = base + t
                    st = isinstance(t, int)
                    act.wait_ge(S["pv_done"], u + 1)
                    if not st or u >= 2:
                        act.wait_ge(S["w_done"], u - 1)
                    nc.scalar.copy(o_sb[:, par, :, :], ps_o[:, 0:2 * BCOLS].rearrange("p (t n) -> p t n", t=2))\
                        .then_inc(S["o_ev"], 1)

                p0 = base % 2
                p1 = 1 - p0
                values_out(0, p0)
                exponentials(0, p0, 0)
                centre_out(0)
                exponentials(0, p0, 1)
                centre_out(1)

                def step(t, par, last=False):
                    if last and r + 1 < RUNS:
                        sorted_out(r + 1, 0)
                    if not last:
                        exponentials(t + 1, 1 - par, 0)
                    if not isinstance(t, int) or t:
                        outputs_out(t - 1, 1 - par)
                    if last and r + 1 < RUNS:
                        sorted_out(r + 1, 1)
                    if not last:
                        values_out(t + 1, 1 - par)
                        exponentials(t + 1, 1 - par, 1)

                step(0, p0)
                step(1, p1)
                step(2, p0)
                with act.Fori(3, BODIES - 2, 2) as t:
                    step(t, p1)
                    step(t + 1, p0)
                if r + 1 < RUNS:
                    regroup(r + 1)
                step(BODIES - 2, p1)
                step(BODIES - 1, p0, last=True)
                outputs_out(BODIES - 1, p0)
            def tokens_out(n):
                for h in range(2):
                    act.wait_ge(S["hT_ps"], 2 * n + h + 1)
                    nc.scalar.copy(hT[:, 4 * h:4 * h + 4, :], heads(ps_pt[:, h], P)).then_inc(S["hT_ev"], 1)

            def proj_out(nm, dst, rows=P):
                g = PROJ.index(nm)
                act.wait_ge(S["proj_ps"], g + 1)
                w = dst.shape[-1] if len(dst.shape) == 2 else 512
                src = proj_bank[g % 2][0:rows, 0:w]
                if len(dst.shape) == 4:
                    src = src.rearrange("p (h b n) -> p h b n", h=dst.shape[1], b=dst.shape[2])
                nc.scalar.copy(dst, src).then_inc(S["proj_ev"], 1)

            def turn_out(nm, dst):
                n = TURNS.index(nm)
                act.wait_ge(S["turn_ps"], n + 1)
                src = ps_pt[:, n % 2]
                src = src.rearrange("p (h b n) -> p h b n", h=4, b=B) if len(dst.shape) == 4 else heads(src, P)
                nc.scalar.copy(dst, src).then_inc(S["turn_ev"], 1)

            def group_exp(n, scale):
                act.wait_ge(S["g_negmax"], n + 1)
                pr = (gp if n < AGROUPS else sp_)[:, n % 2]
                for i in range(4):
                    act_ = nc.scalar.activation(pr[:, i, :], pr[:, i, :], ACT.Exp, bias=gsum[:, n % 2, 1, i:i + 1], scale=scale,
                                                accum_out=gsum[:, n % 2, 2, i:i + 1])
                act_.then_inc(S["g_exp"], 1)

            def group_turn_out(n):
                act.wait_ge(S["g_t"], n + 1)
                if n >= 2:
                    act.wait_ge(S["g_pv"], n - 1)
                nc.scalar.copy((gpT if n < AGROUPS else spT)[:, n % 2], heads(ps_pt[:, n % 2], P)).then_inc(S["g_tev"], 1)

            def group_out(n):
                act.wait_ge(S["g_pv"], n + 1)
                if n < AGROUPS:
                    q = slice(64 * (n % 2), 64 * (n % 2) + 64)
                    dst = aoT[q, 4 * (n // 2):4 * (n // 2) + 4, :]
                    src = heads(proj_bank[n % 2][q, :], P)
                else:
                    dst = soT[:, 4 * (n - AGROUPS):4 * (n - AGROUPS) + 4, :]
                    src = heads(proj_bank[n % 2], P)
                nc.scalar.copy(dst, src).then_inc(S["g_oev"], 1)

            def groups(lo, hi, scale):
                group_exp(lo, scale)
                for n in range(lo, hi):
                    if n + 1 < hi:
                        group_exp(n + 1, scale)
                    group_turn_out(n)
                    group_out(n)

            tokens_out(0)
            for nm, dst in (("aq", aq), ("ak", ak), ("av", av)):
                proj_out(nm + "0", dst[:, 0:512])
                proj_out(nm + "1", dst[:, 512:N])
            for nm, dst in (("aq", aqT), ("ak", akT)):
                turn_out(nm + "0", dst[:, 0:4, :])
                turn_out(nm + "1", dst[:, 4:8, :])
            groups(0, AGROUPS, 0.125)
            tokens_out(1)
            proj_out("gates", gates[:, 0:GATES])
            act.wait_ge(S["gate_max"], 1)
            nc.scalar.activation(tiny[:, 8:16], gates[:, 128:136], ACT.Exp, bias=tiny[:, 1:2], accum_out=tiny[:, 2:3])
            nc.scalar.activation(tiny[:, 4:5], tiny[:, 3:4], ACT.Exp, scale=-1.0).then_inc(S["gate_exp"], 1)
            act.wait_ge(S["gateT_ps"], 1)
            nc.scalar.copy(loraT, ps_pt[:, 0, 0:P]).then_inc(S["gateT_ev"], 1)
            tokens_out(2)
            for i in range(8):
                proj_out(f"xq{i}", sq[:, 512 * i:512 * i + 512])
                if i:
                    turn_out(f"xq{i - 1}", xqT[:, :, 4 * (i - 1):4 * i, :].rearrange("p b h n -> p h b n"))
            turn_out("xq7", xqT[:, :, 28:32, :].rearrange("p b h n -> p h b n"))
            proj_out("xk", keysT[:].rearrange("p h (b n) -> p h b n", b=B)[:, :, :, N:KV])
            for b in range(B):
                proj_out(f"xv_b{b}", vlat[0:64, b, :], 64)
            root = float(P) ** -0.5

            def x_exp(n):
                act.wait_ge(S["t_max"], n + 1)
                if n >= 2:
                    act.wait_ge(S["t_t"], 3 * n - 3)
                k = n % 2
                nc.scalar.activation(xp[:, k, 0:N], ps_s[:, k].rearrange("p g n -> p (g n)"), ACT.Exp, bias=xsum[:, k, 3:4],
                                     scale=root, accum_out=xsum[:, k, 4:5])
                nc.scalar.activation(xp[:, k, N:KV], xtail[:, n, :], ACT.Exp, bias=xsum[:, k, 3:4],
                                     scale=root, accum_out=xsum[:, k, 5:6]).then_inc(S["t_exp"], 1)

            def x_turn_out(n):
                for j in range(3):
                    m = 3 * n + j
                    if j == 0 and n >= 2:
                        act.wait_ge(S["t_pv"], n - 1)
                    act.wait_ge(S["t_t"], m + 1)
                    if j < 2:
                        nc.scalar.copy(xpT[:, n % 2, 4 * j:4 * j + 4, :], heads(ps_pt[:, m % 2], P)).then_inc(S["t_tev"], 1)
                    else:
                        nc.scalar.copy(xpT[0:64, n % 2, 8, :], ps_pt[0:64, m % 2, 0:P]).then_inc(S["t_tev"], 1)

            def x_out(n):
                b, h, g = n // 16, n // 4 % 4, n % 4
                act.wait_ge(S["t_pv"], n + 1)
                h0 = 8 * h + 2 * g
                nc.scalar.copy(soT[:, h0:h0 + 2, 64 * b:64 * b + 64], heads(x_bank[n % 2][:, 0:P], 64)).then_inc(S["t_oev"], 1)

            def tail_out(c):
                act.wait_ge(S["tail_ps"], c + 1)
                nc.scalar.copy(xtail[:, 8 * c:8 * c + 8, :], heads(x_bank[c % 2][:], 64)).then_inc(S["tail_ev"], 1)

            tail_out(0)
            x_exp(0)
            for c in range(1, 4):
                tail_out(c)
            act.wait_ge(S["tail_ev"], 4)
            for n in range(XTILES):
                if n + 1 < XTILES:
                    x_exp(n + 1)
                x_turn_out(n)
                x_out(n)
            tokens_out(3)
            for i in range(8):
                proj_out(f"sq{i}", sq[:, 512 * i:512 * i + 512])
                if i:
                    turn_out(f"sq{i - 1}", sqT[:, 4 * (i - 1):4 * i, :])
            turn_out("sq7", sqT[:, 28:32, :])
            for nm, dst in (("sk", sk), ("sv", sv)):
                proj_out(nm + "0", dst[:, 0:512])
                proj_out(nm + "1", dst[:, 512:N])
            turn_out("sk0", skT[:, 0:4, :])
            turn_out("sk1", skT[:, 4:8, :])
            groups(AGROUPS, AGROUPS + SGROUPS, root)
            tokens_out(4)
            proj_out("route", route[:, 0, :])
            act.wait_ge(S["route_max"], 1)
            nc.scalar.activation(route[:, 1, :], route[:, 1, :], ACT.Exp, bias=tiny[:, 1:2], accum_out=tiny[:, 2:3])\
                .then_inc(S["route_exp"], 1)
            act.wait_ge(S["routeT_ps"], 1)
            nc.scalar.copy(rT[0:64, :], ps_pt[0:64, 0, 0:P]).then_inc(S["routeT_ev"], 1)

        @block.vector
        def _(dve):
            chain = [0]

            def link(ins):
                chain[0] += 1
                ins.then_inc(S["vchain"], 1)
                dve.wait_ge(S["vchain"], chain[0])

            V = nc.vector

            pows = [0]

            def begin_stats(rows, stats):
                pows[0] += 1
                link(V.bn_aggr(small[0:rows, 0:2], stats))
                V.tensor_scalar(small[0:rows, 1:2], small[0:rows, 1:2], EPS, None, ALU.add).then_inc(S["pow_ready"], 1)

            def end_stats():
                dve.wait_ge(S["pow_done"], pows[0])

            def norm_stats(rows, stats):
                begin_stats(rows, stats)
                end_stats()

            V.memset(small[:, 8:9], -0.5)
            V.memset(small[:, 9:10], 0.0)
            V.memset(cnt[:], 0.0)
            link(V.memset(expo[:], 0x20000000))
            dve.wait_ge(S["coord_in"], 16)
            cv = coord.rearrange("p i (b k) -> p (i b) k", b=B)
            link(V.tensor_reduce(ext[:, 0, :], cv, AX.X, ALU.max))
            V.tensor_reduce(ext[:, 1, :], cv, AX.X, ALU.min, negate=True).then_inc(S["minmax_ready"], 1)
            dve.wait_ge(S["x_in"], 16)
            link(V.bn_stats(bstat[:, 0, :], x[:, 0:512]))
            link(V.bn_stats(bstat[:, 1, :], x[:, 512:1024]))
            norm_stats(P, bstat[:, 0:2, :])
            V.tensor_scalar(f0, x[:], small[:, 0:1], small[:, 2:3], ALU.subtract, ALU.mult).then_inc(S["ln_ready"], 1)
            dve.wait_ge(S["minmax_all"], 1)
            link(V.tensor_tensor(ext[:, 0, :], ext[:, 2, :], ext[:, 3, :], ALU.add))
            link(V.tensor_scalar(ext[:, 0, :], ext[:, 0, :], 1e-6, None, ALU.add))
            link(V.reciprocal(ext[:, 1, :], ext[:, 0, :]))
            link(V.tensor_scalar(ext[:, 1, :], ext[:, 1, :], 1023.0, None, ALU.mult))
            qv = quant.rearrange("p i (b k) -> p (i b) k", b=B)
            link(V.tensor_tensor(qv, cv, ext[:, 3, :].unsqueeze(2).broadcast_to([P, 6, NBLK]), ALU.add))
            link(V.tensor_tensor(qv, qv, ext[:, 1, :].unsqueeze(2).broadcast_to([P, 6, NBLK]), ALU.mult))
            link(V.tensor_copy(qint, quant))
            link(V.tensor_copy(qtmp, qint))
            link(V.tensor_tensor(coord, qtmp, quant, ALU.is_gt))
            link(V.tensor_tensor(qtmp, qtmp, coord, ALU.subtract))
            link(V.tensor_scalar(qtmp, qtmp, 0.0, 1023.0, ALU.max, ALU.min))
            link(V.tensor_copy(qint, qtmp))
            for m in range(METHODS):
                for i in range(3):
                    j = (0, 1, 2)[i] if m % 2 == 0 else (1, 0, 2)[i]
                    ins = V.tensor_copy(bits[:, i, m, :], qint[:, j, :])
            link(ins)
            h3 = [bits[:, i, 2:4, :].rearrange("p m n -> p (m n)") for i in range(3)]
            m_, t_, n_, s_, a_ = (bt[:, i, :] for i in range(5))
            for bit in range(9, 0, -1):
                low = (1 << bit) - 1
                for i in range(3):
                    if i:
                        V.tensor_tensor(t_, h3[0], h3[i], ALU.bitwise_xor)
                    link(V.tensor_scalar(m_, h3[i], 31 - bit, 31, ALU.logical_shift_left, ALU.arith_shift_right))
                    if i == 0:
                        link(V.scalar_tensor_tensor(h3[0], m_, low, h3[0], ALU.bitwise_and, ALU.bitwise_xor))
                        continue
                    V.scalar_tensor_tensor(a_, m_, low, h3[0], ALU.bitwise_and, ALU.bitwise_xor)
                    link(V.tensor_scalar(n_, m_, -1, None, ALU.bitwise_xor))
                    link(V.scalar_tensor_tensor(s_, t_, low, n_, ALU.bitwise_and, ALU.bitwise_and))
                    V.tensor_tensor(h3[0], a_, s_, ALU.bitwise_xor)
                    link(V.tensor_tensor(h3[i], h3[i], s_, ALU.bitwise_xor))
            link(V.tensor_tensor(h3[1], h3[1], h3[0], ALU.bitwise_xor))
            link(V.tensor_tensor(h3[2], h3[2], h3[1], ALU.bitwise_xor))
            link(V.tensor_scalar(t_, h3[2], 1, None, ALU.logical_shift_right))
            for sh in (1, 2, 4, 8):
                link(V.scalar_tensor_tensor(m_ if sh in (1, 4) else t_, t_ if sh in (1, 4) else m_, sh,
                                            t_ if sh in (1, 4) else m_, ALU.logical_shift_right, ALU.bitwise_xor))
            for i in range(3):
                ins = V.tensor_tensor(h3[i], h3[i], t_, ALU.bitwise_xor)
            link(ins)
            bv = bits.rearrange("p i m n -> p (i m n)")
            sv = spread.rearrange("p i m n -> p (i m n)")
            for sh, mask in ((16, 0x030000FF), (8, 0x0300F00F), (4, 0x030C30C3), (2, 0x09249249)):
                link(V.scalar_tensor_tensor(sv, bv, sh, bv, ALU.logical_shift_left, ALU.bitwise_or))
                link(V.tensor_scalar(bv, sv, mask, None, ALU.bitwise_and))
            b3 = [bits[:, i, :, :].rearrange("p m n -> p (m n)") for i in range(3)]
            link(V.scalar_tensor_tensor(key[:], b3[0], 1, b3[1], ALU.logical_shift_left, ALU.bitwise_or))
            link(V.scalar_tensor_tensor(spread[:, 0, :, :].rearrange("p m n -> p (m n)"), key[:], 1, b3[2],
                                        ALU.logical_shift_left, ALU.bitwise_or))
            V.tensor_tensor(key[:], spread[:, 0, :, :].rearrange("p m n -> p (m n)"), expo[:], ALU.add)\
                .then_inc(S["key_ready"], 1)
            dve.wait_ge(S["key_ready"], 1)
            keyf = key[:].bitcast(F32)
            dve.wait_ge(S["const_in"], CONSTS)
            ncount = [0]

            def spare(n):
                if ncount[0] >= 2:
                    dve.wait_ge(S["counted"], ncount[0] - 1)
                return junk[:, ncount[0] % 2, 0:n]

            def counted(ins):
                ncount[0] += 1
                ins.then_inc(S["counted"], 1)

            for b in range(B):
                dve.wait_ge(S["keyrow_in"], 16 * (b + 1))
                for m in range(METHODS):
                    for k in range(NBLK):
                        col = (m * B + b) * NBLK + k
                        mine = keyf[:, col:col + 1]
                        if k:
                            counted(V.tensor_scalar(spare(P * k), keyrow[:, m, 0:P * k], mine, 0.0, ALU.is_le, ALU.add,
                                                    accum_out=cnt[:, 0, col:col + 1]))
                        counted(V.tensor_scalar(spare(N - P * k), keyrow[:, m, P * k:N], mine, 0.0, ALU.is_lt, ALU.add,
                                                accum_out=cnt[:, 1, col:col + 1]))
                        counted(V.scalar_tensor_tensor(spare(P), keyrow[:, m, P * k:P * k + P], mine, lower[:],
                                                       ALU.is_equal, ALU.mult, accum_out=cnt[:, 2, col:col + 1]))
                dve.wait_ge(S["counted"], ncount[0])
                V.tensor_copy(small[:, 24:25], small[:, 8:9]).then_inc(S["keyrow_free"], 1)
                dve.wait_ge(S["keyrow_free"], b + 1)
                bc = [cnt[:, i, :].rearrange("p (m b k) -> p b m k", m=METHODS, b=B)[:, b] for i in range(3)]
                rk = ranks[:].rearrange("p (m b k) -> p b m k", m=METHODS, b=B)[:, b]
                ro = rankoff[:].rearrange("p (m b k) -> p b m k", m=METHODS, b=B)[:, b]
                ri = rowidx[:].rearrange("p (m b k) -> p b m k", m=METHODS, b=B)[:, b]
                link(V.tensor_tensor(rk, bc[0], bc[1], ALU.add))
                link(V.tensor_tensor(rk, rk, bc[2], ALU.add))
                link(V.tensor_tensor(rk, rk, ro, ALU.add))
                V.tensor_copy(ri, rk).then_inc(S["rank_ready"], 1)
            def centres(r):
                dve.wait_ge(S["fc_in"], 64 * (r + 1))
                dve.wait_ge(S["hc_ps"] if r else S["ctx_ps"], 2 * r if r else 32)
                V.tensor_copy(c16, fc.rearrange("p t n -> p (t n)")).then_inc(S["c16_ready"], 1)
                dve.wait_ge(S["c16_ready"], r + 1)
                V.tensor_copy(c32, c16).then_inc(S["c32_ready"], 1)

            def first_windows(r):
                dve.wait_ge(S["fsT_ev"], 4 * (r + 1))
                for n in range(5):
                    V.tensor_copy(fh[:, :, n, 0:n + 6], fs[:, :, 5:n + 11])
                    if n < 4:
                        V.tensor_copy(fh[:, :, n, n + 6:KW], fs[:, :, n + 10:n + 11].broadcast_to([P, 2, 4 - n]))
                V.tensor_copy(fs[:, :, N + 5:N + 9], fs[:, :, N + 4:N + 5].broadcast_to([P, 2, 4])).then_inc(S["fh_ready"], 1)

            def run_statistics(r):
                dve.wait_ge(S["stats_ready"], r + 1)
                begin_stats(OUTC[r // B], bstat[0:OUTC[r // B], :, :])

            def run_output(r):
                layer, b = divmod(r, B)
                O = OUTC[layer]
                end_stats()
                link(V.tensor_scalar(mx[0:O, :], mx[0:O, :], small[0:O, 0:1], small[0:O, 2:3], ALU.subtract, ALU.mult))
                if layer == 0:
                    dve.wait_ge(S["fnT_ps"], 2 + b)
                    dve.wait_ge(S["feat_out"] if b else S["feat_out0"], 16)
                    dst = f0[0:64, :]
                else:
                    dve.wait_ge(S["fsp_ready"], RUNS if b else 1)
                    dst = f2[b]
                V.scalar_tensor_tensor(dst, mx[0:O, :], 0.2, mx[0:O, :], ALU.mult, ALU.max).then_inc(S["feat_ready"], 1)

            centres(0)
            first_windows(0)
            for r in range(RUNS):
                layer, b = divmod(r, B)
                O = OUTC[layer]
                base = BODIES * r

                def row_max(t, par):
                    u = base + t
                    st = isinstance(t, int)
                    dve.wait_ge(S["s_done"], u + 1)
                    if not st or u >= 2:
                        dve.wait_ge(S["exp_done"], 2 * u - 2)
                    V.tensor_reduce(negmax[0:GROWS, par, 0, :],
                                    ps_s[0:GROWS, par, :, 0:4 * GROWS].rearrange("p g (h n) -> p g h n", h=4),
                                    AX.X, ALU.max).then_inc(S["rowmax"], 1)
                    dve.wait_ge(S["rowmax"], u + 1)
                    V.tensor_scalar(negmax[0:GROWS, par, 1, :], negmax[0:GROWS, par, 0, :], -0.125, None, ALU.mult)\
                        .then_inc(S["negmax_ready"], 1)

                def sums(t, par, g):
                    u = base + t
                    st = isinstance(t, int)
                    if not st or u >= 2:
                        dve.wait_ge(S["norm_done"], 2 * u - 3 + g)
                    dve.wait_ge(S["exp_done"], 2 * u + g + 1)
                    i, o = (rsum[0:GROWS, par, w].rearrange("p (f g k) -> p f g k", f=2, g=2)[:, :, g] for w in range(2))
                    V.reciprocal(o, i).then_inc(S["recip_ready"], 1)

                def probs_out(t, par, g):
                    u = base + t
                    st = isinstance(t, int)
                    if not st or u >= 2:
                        dve.wait_ge(S["pv_done"], u - 1)
                    dve.wait_ge(S["t_done"], 2 * u + g + 1)
                    V.tensor_copy(pt_sb[0:GROWS, par, 4 * g:4 * g + 4, :],
                                  ps_pt[0:GROWS, g, 0:4 * GROWS].rearrange("p (h n) -> p h n", h=4)).then_inc(S["pt_ev"], 1)

                def add_centre(t, par):
                    u = base + t
                    n0 = n0_of(t)
                    dve.wait_ge(S["w_done"], u + 1)
                    if isinstance(t, int) and t == 0:
                        dve.wait_ge(S["hc_ready"], 2 * r + 2)
                    hcw = bass.AP(tensor=arena, offset=hc_off + n0, ap=[[ARENA, O], [1, BP], [0, KW]])
                    hv = hs[0:O, par, :].rearrange("p (n k) -> p n k", k=KW)
                    V.tensor_tensor(hv, ps_hg[0:O, :].rearrange("p (n k) -> p n k", k=KW), hcw, ALU.add)\
                        .then_inc(S["h_read"], 1)

                def statistics(t, par):
                    u = base + t
                    n0 = n0_of(t)
                    hv = hs[0:O, par, :].rearrange("p (n k) -> p n k", k=KW)
                    dve.wait_ge(S["h_read"], u + 1)
                    tail = isinstance(t, int) and t == BODIES - 1
                    lo = BCOLS - TAIL_NEW * KW if tail else 0
                    ti = t if isinstance(t, int) else t
                    V.bn_stats(bass.AP(tensor=bstat, offset=ti * 6, ap=[[BODIES * 6, O], [1, 6]]), hs[0:O, par, lo:BCOLS])
                    last = V.tensor_reduce(bass.AP(tensor=arena, offset=mx_off + n0, ap=[[ARENA, O], [1, BP]]), hv,
                                           AX.X, ALU.max)
                    if tail:
                        last.then_inc(S["stats_ready"], 1)

                p0 = base % 2
                p1 = 1 - p0
                row_max(0, p0)
                if r:
                    run_output(r - 1)
                row_max(1, p1)
                sums(0, p0, 0)

                def step(t, par, last=False):
                    st = isinstance(t, int)
                    sums(t, par, 1)
                    if not last:
                        sums(t + 1, 1 - par, 0)
                    probs_out(t, par, 0)
                    if not st or t + 2 < BODIES:
                        row_max(t + 2, par)
                    probs_out(t, par, 1)
                    if st and t == 0 and 0 < r <= B:
                        dve.wait_ge(S["fnT_ps"], 2 + r)
                        dve.wait_ge(scattered[r - 1], 16 * METHODS * NBLK)
                        q = slice(64 * (r - 1), 64 * r)
                        V.tensor_copy(fn[:, :, q], ps_o[:].rearrange("p (k c) -> p k c", k=NBLK)).then_inc(S["fnT_ev"], 1)
                    if not st or t >= 1:
                        add_centre(t - 1, 1 - par)
                    if not st or t >= 1:
                        statistics(t - 1, 1 - par)

                step(0, p0)
                step(1, p1)
                step(2, p0)
                with dve.Fori(3, BODIES - 2, 2) as t:
                    step(t, p1)
                    step(t + 1, p0)
                step(BODIES - 2, p1)
                step(BODIES - 1, p0, last=True)
                if r + 1 < RUNS:
                    centres(r + 1)
                    first_windows(r + 1)
                add_centre(BODIES - 1, p0)
                statistics(BODIES - 1, p0)
                run_statistics(r)
            run_output(RUNS - 1)
            for b in range(B):
                dve.wait_ge(S["h3_ps"], b + 1)
                dve.wait_ge(S["feat_out"], 32)
                q = slice(64 * b, 64 * b + 64)
                V.tensor_copy(f0[q, :], ps_pt[q].rearrange("p h n -> p (h n)")).then_inc(S["h3_out"], 1)
            dve.wait_ge(S["h3_out"], 2)
            for h in range(2):
                link(V.bn_stats(bstat[:, h, :], f0[:, 512 * h:512 * h + 512]))
            norm_stats(P, bstat[:, 0:2, :])
            link(V.tensor_scalar(mx, f0, small[:, 0:1], small[:, 2:3], ALU.subtract, ALU.mult))
            link(V.scalar_tensor_tensor(mx, mx, 0.2, mx, ALU.mult, ALU.max))
            V.tensor_tensor(x[:], x[:], mx, ALU.add).then_inc(S["x1_ready"], 1)
            def layer_norm(n):
                dve.wait_ge(S["x1_ready"] if n == 0 else S["x_ready"], max(n, 1))
                if n:
                    dve.wait_ge(S["hT_ps"], 2 * n)
                link(V.bn_stats(bstat[:, 0, :], x[:, 0:512]))
                link(V.bn_stats(bstat[:, 1, :], x[:, 512:N]))
                norm_stats(P, bstat[:, 0:2, :])
                V.tensor_scalar(hn, x[:], small[:, 0:1], small[:, 2:3], ALU.subtract, ALU.mult).then_inc(S["hn_ready"], 1)

            def group_max(n, mask, scale):
                k = n % 2
                pr = (gp if n < AGROUPS else sp_)[:, k]
                dve.wait_ge(S["g_s"], n + 1)
                if n >= 2:
                    dve.wait_ge(S["g_t"], n - 1)
                V.tensor_tensor(pr, heads(ps_s[:, 0, k], P), mask.unsqueeze(1).broadcast_to([P, 4, P]), ALU.add)\
                    .then_inc(S["g_masked"], 1)
                dve.wait_ge(S["g_masked"], n + 1)
                V.tensor_reduce(gsum[:, k, 0, :], pr, AX.X, ALU.max).then_inc(S["g_max"], 1)
                dve.wait_ge(S["g_max"], n + 1)
                V.tensor_scalar(gsum[:, k, 1, :], gsum[:, k, 0, :], -scale, None, ALU.mult).then_inc(S["g_negmax"], 1)

            def group_recip(n):
                dve.wait_ge(S["g_exp"], n + 1)
                V.reciprocal(gsum[:, n % 2, 3, :], gsum[:, n % 2, 2, :]).then_inc(S["g_recip"], 1)

            def groups(lo, hi, mask, scale):
                group_max(lo, mask, scale)
                for n in range(lo, hi):
                    if n + 1 < hi:
                        group_max(n + 1, mask, scale)
                    group_recip(n)

            def residual(n):
                dve.wait_ge(S["y_ps"], n)
                V.tensor_tensor(x[:, 0:512], x[:, 0:512], y_ps[0], ALU.add)
                V.tensor_tensor(x[:, 512:N], x[:, 512:N], y_ps[1], ALU.add).then_inc(S["x_ready"], 1)

            layer_norm(0)
            dve.wait_ge(S["late_in"], LATE)
            for i, v in enumerate((aq, ak)):
                dve.wait_ge(S["proj_ev"], 2 * i + 2)
                v4 = v.rearrange("p (h n t) -> p h n t", h=16, t=2)
                r4 = rot.rearrange("p (h n t) -> p h n t", h=16, t=2)
                s4 = sinn.rearrange("p (n t) -> p n t", t=2)
                for e in range(2):
                    last = V.tensor_tensor(r4[:, :, :, e], v4[:, :, :, 1 - e], s4[:, :, e].unsqueeze(1).broadcast_to([P, 16, 32]), ALU.mult)
                link(last)
                v3, r3 = heads(v, 64), heads(rot, 64)
                link(V.tensor_tensor(v3, v3, cosn.unsqueeze(1).broadcast_to([P, 16, 64]), ALU.mult))
                V.tensor_tensor(v3, v3, r3, ALU.add).then_inc(S["rope_ready"], 1)
                dve.wait_ge(S["rope_ready"], i + 1)
            groups(0, AGROUPS, causal, 0.125)
            residual(1)
            layer_norm(1)
            link(V.tensor_tensor(x[:], x[:], bbase, ALU.add))
            dve.wait_ge(S["proj_ev"], PROJ.index("gates") + 1)
            link(V.tensor_reduce(tiny[:, 0:1], gates[:, 128:136], AX.X, ALU.max))
            link(V.tensor_scalar(tiny[:, 1:2], tiny[:, 0:1], -1.0, None, ALU.mult))
            V.tensor_tensor(tiny[:, 3:4], gates[:, 136:137], bthr, ALU.add).then_inc(S["gate_max"], 1)
            dve.wait_ge(S["gate_exp"], 1)
            link(V.reciprocal(tiny[:, 5:6], tiny[:, 2:3]))
            link(V.tensor_scalar(tiny[:, 6:7], tiny[:, 4:5], 1.0, None, ALU.add))
            link(V.reciprocal(tiny[:, 7:8], tiny[:, 6:7]))
            link(V.tensor_scalar(tiny[:, 7:8], tiny[:, 7:8], 0.125, None, ALU.mult))
            link(V.tensor_scalar(tiny[:, 8:16], tiny[:, 8:16], tiny[:, 5:6], tiny[:, 7:8], ALU.mult, ALU.subtract))
            link(V.tensor_scalar(tiny[:, 8:16], tiny[:, 8:16], 0.0, None, ALU.max))
            link(V.tensor_reduce(tiny[:, 16:17], tiny[:, 8:16], AX.X, ALU.add))
            link(V.tensor_scalar(tiny[:, 17:18], tiny[:, 16:17], 0.0, None, ALU.is_equal))
            link(V.tensor_tensor(tiny[:, 18:19], tiny[:, 16:17], tiny[:, 17:18], ALU.add))
            link(V.reciprocal(tiny[:, 19:20], tiny[:, 18:19]))
            link(V.tensor_scalar(tiny[:, 24:32], tiny[:, 8:16], tiny[:, 19:20], 2.0, ALU.mult, ALU.mult))
            V.tensor_tensor(heads(lora, 16), heads(gates[:, 0:128], 16), tiny[:, 24:32].unsqueeze(2).broadcast_to([P, 8, 16]),
                            ALU.mult).then_inc(S["gate_ready"], 1)
            residual(2)
            layer_norm(2)
            root = float(P) ** -0.5

            def x_max(n):
                k = n % 2
                dve.wait_ge(S["t_s"], n + 1)
                link(V.tensor_reduce(xsum[:, k, 0:1], ps_s[:, k].rearrange("p g n -> p (g n)"), AX.X, ALU.max))
                V.tensor_scalar(xsum[:, k, 3:4], xsum[:, k, 0:1], tailmax[:, n:n + 1], -root, ALU.max, ALU.mult)\
                    .then_inc(S["t_max"], 1)

            def tail_max(c):
                dve.wait_ge(S["tail_ev"], c + 1)
                V.tensor_reduce(tailmax[:, 8 * c:8 * c + 8], xtail[:, 8 * c:8 * c + 8, :], AX.X, ALU.max)\
                    .then_inc(S["tail_max"], 1)

            def x_norm(n):
                k = n % 2
                dve.wait_ge(S["t_exp"], n + 1)
                link(V.tensor_tensor(xsum[:, k, 6:7], xsum[:, k, 4:5], xsum[:, k, 5:6], ALU.add))
                link(V.reciprocal(xsum[:, k, 7:8], xsum[:, k, 6:7]))
                V.tensor_scalar(xp[:, k, :], xp[:, k, :], xsum[:, k, 7:8], None, ALU.mult).then_inc(S["t_norm"], 1)

            tail_max(0)
            dve.wait_ge(S["tail_max"], 1)
            x_max(0)
            for c in range(1, 4):
                tail_max(c)
            dve.wait_ge(S["tail_max"], 4)
            x_max(1)
            for n in range(XTILES):
                x_norm(n)
                if n + 2 < XTILES:
                    x_max(n + 2)
            residual(3)
            layer_norm(3)
            dve.wait_ge(S["late2_in"], LATE2)
            groups(AGROUPS, AGROUPS + SGROUPS, samebatch, root)
            residual(4)
            layer_norm(4)
            dve.wait_ge(S["proj_ev"], PROJ.index("route") + 1)
            link(V.tensor_tensor(route[:, 1, :], route[:, 0, :], rbias, ALU.add))
            link(V.tensor_reduce(tiny[:, 0:1], route[:, 1, :], AX.X, ALU.max))
            V.tensor_scalar(tiny[:, 1:2], tiny[:, 0:1], -1.0, None, ALU.mult).then_inc(S["route_max"], 1)
            dve.wait_ge(S["route_exp"], 1)
            link(V.reciprocal(tiny[:, 3:4], tiny[:, 2:3]))
            link(V.tensor_scalar(route[:, 2, :], route[:, 1, :], tiny[:, 3:4], None, ALU.mult))
            link(V.max(tiny[:, 8:16], route[:, 2, :]))
            link(V.match_replace(route[:, 3, :], tiny[:, 8:16], route[:, 2, :], -1.0))
            link(V.tensor_reduce(tiny[:, 16:17], tiny[:, 8:16], AX.X, ALU.add))
            V.scalar_tensor_tensor(route[:, 4, :], route[:, 3, :], 0.0, route[:, 2, :], ALU.is_lt, ALU.mult)\
                .then_inc(S["route_ready"], 1)
            dve.wait_ge(S["y_ps"], 5)
            for h in range(2):
                c = slice(512 * h, 512 * h + 512)
                last = V.scalar_tensor_tensor(hn[:, c], hn[:, c], tiny[:, 16:17], y_ps[h], ALU.mult, ALU.add)
            link(last)
            V.tensor_tensor(x[:], x[:], hn, ALU.add).then_inc(S["x_ready"], 1)


def host(inputs):
    import numpy as np
    g = {k: np.asarray(v) for k, v in inputs.items()}
    a = {}
    a["x"] = g["x"].reshape(P, N)
    ctx = g["ctx_4096"]
    a["coords"] = ctx[:, 0:3, :].reshape(B, 3, NBLK, P).transpose(3, 1, 0, 2).reshape(P, 3, 16)
    a["ident"] = np.eye(P, dtype=np.float32)
    a["identh"] = np.eye(P, dtype=np.float16)
    a["lower"] = np.tril(np.ones((P, P), np.float32), -1)
    a["rankoff"] = np.tile(np.repeat(np.arange(METHODS) * N, 16)[None].astype(np.float32), (P, 1))
    own = np.arange(GROWS) // KW == np.arange(GP)[:, None]
    root = BIG ** 0.5
    ml = np.full((GP + 1, GROWS), root, np.float16)
    ml[:GP] = own * root
    mr = np.full((GP + 1, GROWS), -root, np.float16)
    mr[:GP] = own * root
    ml, mr = (np.tile(np.pad(m, ((0, 64 - GP - 1), (0, 0))), (2, 1)) for m in (ml, mr))
    a["maskl"] = ml
    a["maskr"] = np.tile(mr, (1, 4))
    perms = ([2, 0, 3, 1], [1, 3, 0, 2])

    def lin(w, perm, lo):
        w = w.reshape(P, 2 * C, METHODS)[:, lo:lo + C, :]
        w = w[:, :, [perm.index(m) for m in range(METHODS)]]
        return w.reshape(P, 2, 2, 16, METHODS).transpose(0, 1, 2, 4, 3).reshape(P, 256)

    ws = [g["L0_xattn_W_lin1"], g["L0_xattn_W_lin2"]]
    a["wlin_n"] = np.stack([lin(w, p, C) for w, p in zip(ws, perms)], 1)
    a["wlin_c"] = np.stack([lin(w, p, 0) for w, p in zip(ws, perms)], 1)
    a["blin"] = np.stack([g["L0_xattn_b_lin1"], g["L0_xattn_b_lin2"]], 1)
    a["wconv0"] = g["L0_xattn_W_conv1"].T
    a["wconv1"] = g["L0_xattn_W_conv2"].T
    a["wconv3"] = g["L0_xattn_W_conv3"].T.reshape(2, P, 64).transpose(1, 0, 2)

    def wide(w):
        n = w.shape[1]
        return w.reshape(KT, P, n // 512, 512).transpose(2, 1, 0, 3).reshape(n // 512, P, CHUNK)

    def tall(w):
        return w.reshape(-1, 4, P, N).transpose(0, 2, 1, 3).reshape(-1, P, CHUNK)

    cx = ctx.reshape(B * N, N)
    chunks = [wide(g["L1_xattn_Wk"]), wide(g["L1_xattn_Wv"]), wide(cx.T),
              wide(g["L0_attn_wq"].T), wide(g["L0_attn_wk"].T), wide(g["L0_attn_wv"].T), tall(g["L0_attn_wo"].T),
              wide(g["L0_ffn_W_base"].T), wide(g["L1_xattn_Wq"]), tall(g["L1_xattn_Wo"]),
              wide(g["L1_attn_wq"].T), wide(g["L1_attn_wk"].T), wide(g["L1_attn_wv"].T), tall(g["L1_attn_wo"].T)]
    freq = (1.0 / np.float32(10000.0) ** (np.arange(0, 64, 2, dtype=np.float32) / np.float32(64))).astype(np.float32)
    ang = np.arange(C, dtype=np.float32)[:, None] * freq[None]
    a["cosn"] = np.tile(np.repeat(np.cos(ang), 2, axis=1), (B, 1))
    a["sinn"] = np.tile(np.repeat(np.sin(ang), 2, axis=1) * np.tile(np.array([-1, 1], np.float32), 32), (B, 1))
    tok = np.arange(P)
    same = tok[:, None] // C == tok[None] // C
    a["samebatch"] = np.where(same, 0, -BIG).astype(np.float32)
    a["causal"] = np.where(same & (tok[:, None] >= tok[None]), 0, -BIG).astype(np.float32)
    wg = np.concatenate([g["L0_ffn_A_w"].reshape(P, N), g["L0_ffn_W_gate"], g["L0_ffn_W_thr"][None]], 0)
    a["wgate"] = wg.T.reshape(KT, P, GATES).transpose(1, 0, 2)
    a["lora_b"] = g["L0_ffn_B_w"].transpose(0, 2, 1).reshape(P, N)
    a["bbase"] = g["L0_ffn_b_base"]
    a["bthr"] = g["L0_ffn_b_thr"]
    a["wroute"] = g["L1_ffn_router_weight"].T.reshape(KT, P, 64).transpose(1, 0, 2)
    a["rbias"] = g["L1_ffn_router_bias"]
    a["ebias"] = g["L1_ffn_expert_bias"]
    a["wstream"] = np.concatenate(chunks, 0)
    return {k: np.ascontiguousarray(v) for k, v in a.items()}


def kernel(**inputs):
    import numpy as _np
    import concourse.bacc as _bacc
    from concourse.bass_utils import run_bass_kernel_spmd as _run

    nc = _bacc.Bacc("TRN2", target_bir_lowering=False, num_devices=1)
    arrays = host(inputs)
    args = {n: nc.dram_tensor(f"in_{n}", v.shape, mybir.dt.from_np(v.dtype), kind="ExternalInput").ap()
            for n, v in arrays.items()}
    out = nc.dram_tensor("out_0", (P, N), F32, kind="ExternalOutput").ap()
    build(nc, args, out)
    r = _run(nc, [{f"in_{n}": v for n, v in arrays.items()}], core_ids=[0])
    return r.results[0]["out_0"].reshape(B, C, N)
```

```python
from contextlib import ExitStack

import concourse.bass as bass
from concourse import mybir

F32 = mybir.dt.float32
F16 = mybir.dt.float16
I32 = mybir.dt.int32
U32 = mybir.dt.uint32
ALU = mybir.AluOpType
ACT = mybir.ActivationFunctionType
AX = mybir.AxisListType

P = 128
B, C, N = 2, 64, 1024
NBLK = N // P
METHODS = 4
KW = 10
GP = 12
GROWS = GP * KW
BP = 2 * GP
BCOLS = BP * KW
BODIES = -(-N // BP)
TAIL_NEW = N - (BODIES - 1) * BP
RUNS = 2 * B
OUTC = (64, 128)
BIG = 2.0 ** 30
EPS = 1e-5
KT = N // P
KV = N + C
CHUNK = 4096
SLOTS = 3
CTX_OPEN = 28
ARENA = 18960


WEIGHTS = (["aq0", "aq1", "ak0", "ak1", "av0", "av1", "ao0", "ao1", "base0", "base1"]
           + [f"xq{i}" for i in range(8)] + ["xk", "xv"] + [f"xo{i}" for i in range(8)]
           + [f"sq{i}" for i in range(8)] + ["sk0", "sk1", "sv0", "sv1"] + [f"so{i}" for i in range(8)])
PROJ = (["aq0", "aq1", "ak0", "ak1", "av0", "av1", "gates"] + [f"xq{i}" for i in range(8)] + ["xk", "xv_b0", "xv_b1"]
        + [f"sq{i}" for i in range(8)] + ["sk0", "sk1", "sv0", "sv1", "route"])
GATES = 128 + 8 + 1
TURNS = (["aq0", "aq1", "ak0", "ak1"] + [f"xq{i}" for i in range(8)] + [f"sq{i}" for i in range(8)] + ["sk0", "sk1"])
AGROUPS = 4
SGROUPS = 8
XTILES = 32
KVT = 9


def build(nc, a, out):
    ctx = ExitStack()
    with ctx:
        def sb(name, shape, dt):
            return ctx.enter_context(nc.sbuf_tensor(name, shape, dt))

        def sem(name):
            return ctx.enter_context(nc.semaphore(name))

        def dram(name, shape, dt=F32):
            return nc.dram_tensor(name, shape, dt, kind="Internal").ap()

        x = sb("x", [P, N], F32)
        ident = sb("ident", [P, P], F32)
        identh = sb("identh", [P, P], F16)
        ring = sb("ring", [P, SLOTS, CHUNK], F32)
        keysT = sb("keysT", [P, 4, B * KV], F32)
        vals = sb("vals", [P, B * NBLK, 512], F32)
        small = sb("small", [P, 64], F32)
        bstat = sb("bstat", [P, BODIES, 6], F32)
        arena = sb("arena", [P, ARENA], F32)
        used = [0]

        def take(n, dt=F32):
            lo = used[0]
            used[0] += n
            assert used[0] <= ARENA, used[0]
            return arena[:, lo:lo + n]

        FSW = N + 12
        p_all = take(2 * 8 * GROWS)
        pt_all = take(2 * 8 * GROWS)
        vs_all = take(2 * 2 * 256)
        keyrow = arena[:, 0:4 * N].rearrange("p (m n) -> p m n", m=4)
        p_sb = p_all.rearrange("p (k g n) -> p k g n", k=2, g=8)
        pt_sb = pt_all.rearrange("p (k g n) -> p k g n", k=2, g=8)
        vs_sb = vs_all.rearrange("p (k g n) -> p k g n", k=2, g=2)
        o_off = used[0]
        o_sb = take(2 * 2 * BCOLS).rearrange("p (k t n) -> p k t n", k=2, t=2)
        hs = take(2 * BCOLS).rearrange("p (k n) -> p k n", k=2)
        xt = take(2 * BCOLS).bitcast(F16).rearrange("p (k t n) -> p k t n", k=2, t=2)
        fs_off = used[0]
        fs = take(2 * FSW).rearrange("p (t n) -> p t n", t=2)
        fc_off = used[0]
        fc = take(2 * N).rearrange("p (t n) -> p t n", t=2)
        fsr_off = used[0]
        fsr = take(NBLK * METHODS * C).rearrange("p (k c) -> p k c", c=C)
        fn = take(NBLK * P).rearrange("p (k c) -> p k c", k=NBLK)
        f0 = take(N)
        hc_off = used[0]
        hc = take(N)
        mx_off = used[0]
        mx = take(N)
        fsp = [ap.rearrange("p (k n) -> p k n", k=NBLK) for ap in (arena[:, 0:2 * N],) + 3 * (ring[:, 2, 0:2 * N],)]
        c32 = (arena[:, 2 * N:4 * N],) + 3 * (ring[:, 1, 2 * N:4 * N],)
        fh = take(2 * 5 * KW).rearrange("p (t n k) -> p t n k", t=2, n=5)
        junk = take(N).bitcast(F16).rearrange("p (k n) -> p k n", k=2)
        c16 = junk.rearrange("p k n -> p (k n)")
        flat = fsr.rearrange("p k c -> p (k c)")
        f2 = (ring[:, 1, 0:N], flat[:, 0:N])
        g01 = (ring[:, 1, N:2 * N], flat[:, N:2 * N])

        def scratch(lo, n, dt=F32):
            return arena[:, o_off + lo:o_off + lo + n].bitcast(dt)

        spot = [0]

        def place(n, *dims):
            lo = spot[0]
            spot[0] += n
            assert spot[0] <= ARENA, spot[0]
            return arena[:, lo:lo + n]

        def heads(ap, n):
            return ap.rearrange("p (h n) -> p h n", n=n)

        hn = place(N)
        hT = heads(place(N), P)
        common = spot[0]
        aq, ak, av, rot = place(N), place(N), place(N), place(N)
        aqT, akT, aoT = heads(place(N), P), heads(place(N), P), heads(place(N), P)
        gp = place(2 * 512).rearrange("p (k h n) -> p k h n", k=2, h=4)
        gpT = place(2 * 512).rearrange("p (k h n) -> p k h n", k=2, h=4)
        cosn, sinn, causal = place(64), place(64), place(P)
        wgate = place(KT * GATES).rearrange("p (k n) -> p k n", k=KT)
        lora_b, bbase = place(N), place(N)
        gates, lora, loraT, bthr = place(GATES + 1), place(P), place(P), place(1)
        spot[0] = common
        sq = place(4 * N)
        soT = heads(sq, P)
        xqT = place(4 * N).rearrange("p (b h n) -> p b h n", b=B, h=32)
        sqT = heads(arena[:, common + 4 * N:common + 8 * N], P)
        shared = spot[0]
        vlat = place(2 * 512).rearrange("p (b n) -> p b n", b=B)
        xp = place(2 * KV).rearrange("p (k n) -> p k n", k=2)
        xpT = place(2 * KVT * P).rearrange("p (k t n) -> p k t n", k=2, t=KVT)
        xtail = heads(place(XTILES * 64), 64)
        tailmax = place(XTILES)
        spot[0] = shared
        sk, sv, skT = place(N), place(N), heads(place(N), P)
        sp_ = place(2 * 512).rearrange("p (k h n) -> p k h n", k=2, h=4)
        spT = place(2 * 512).rearrange("p (k h n) -> p k h n", k=2, h=4)
        samebatch = place(P)
        wroute = place(KT * 64).rearrange("p (k n) -> p k n", k=KT)
        ebias, rbias = place(N), place(64)
        route = place(5 * 64).rearrange("p (k n) -> p k n", k=5)
        rT = place(P)
        gsum = sb("gsum", [P, 2, 4, 4], F32)
        xsum = sb("xsum", [P, 2, 8], F32)
        tiny = sb("tiny", [P, 40], F32)

        coord, quant, qtmp = (scratch(48 * i, 48).rearrange("p (i n) -> p i n", i=3) for i in range(3))
        qint = scratch(144, 48, I32).rearrange("p (i n) -> p i n", i=3)
        bits = scratch(192, 192, I32).rearrange("p (i m n) -> p i m n", i=3, m=METHODS)
        spread = scratch(384, 192, I32).rearrange("p (i m n) -> p i m n", i=3, m=METHODS)
        bt = scratch(576, 160, I32).rearrange("p (i n) -> p i n", i=5)
        key = sb("key", [P, 64], I32)
        expo = sb("expo", [P, 64], I32)
        ext = sb("ext", [P, 4, 6], F32)
        keycol = sb("keycol", [64, P], F32)
        cnt = sb("cnt", [P, 3, 64], F32)
        ranks = sb("ranks", [P, 64], F32)
        rankoff = sb("rankoff", [P, 64], F32)
        rowidx = sb("rowidx", [P, 64], U32)
        lower = sb("lower", [P, P], F32)
        maskl = sb("maskl", [P, GROWS], F16)
        maskr = sb("maskr", [P, 4 * GROWS], F16)
        wlin_n = sb("wlin_n", [P, 2, 256], F32)
        wlin_c = sb("wlin_c", [P, 2, 256], F32)
        blin = sb("blin", [P, 2], F32)
        wconv = [sb(f"wconv{l}", [P, OUTC[l]], F32) for l in range(2)]
        wconv3 = sb("wconv3", [P, 2, 64], F32)
        wp = [sb(f"wp{l}", [P, 2, OUTC[l]], F32) for l in range(2)]
        wc = [sb(f"wc{l}", [P, 2, OUTC[l]], F32) for l in range(2)]
        cb = sb("cb", [P, 2], F32)
        negmax = sb("negmax", [P, 2, 2, 8], F32)
        rsum = sb("rsum", [P, 2, 2, 8], F32)

        ps_s = ctx.enter_context(nc.psum_tensor("ps_s", [P, 2, 2, 512], F32))
        ps_pt = ctx.enter_context(nc.psum_tensor("ps_pt", [P, 2, 512], F32))
        ps_o = ctx.enter_context(nc.psum_tensor("ps_o", [P, 512], F32))
        ps_vh = ctx.enter_context(nc.psum_tensor("ps_vh", [P, 512], F32))
        ps_v = ps_vh[:, 0:256].bitcast(F16).rearrange("p (g n) -> p g n", g=2)
        ps_hg = ps_vh[:, 256:256 + BCOLS]
        ps_h, ps_f = ps_s[:, 1, 0], ps_s[:, 1, 1]
        y_ps = (ps_vh[:], ps_f)
        x_bank = (ps_o, ps_vh)
        proj_bank = (ps_o[:], ps_h)

        keys_d = dram("keys_d", (64, P))
        feat_d = [dram(f"feat_d{l}", (P, N)) for l in range(2)]
        sorted_d = [dram(f"sorted_d{r}", (METHODS * N, C)) for r in range(RUNS)]

        names = ("xk_lo xk_hi ctx0_lo ctx0_hi xv_in ctx1_in ctx2_in ctx3_in x_in ident_in coord_in const_in vchain minmax_ready minmax_all pow_ready pow_done ln_ready feat_out0 "
                 "keyT_ps keycol_ready keys_out keyrow_in keyrow_free rank_ready fnT_ps fnT_ev "
                 "fsr_in fsT_ps fsT_ev fc_in fh_ready wp_ps wp_ev c16_ready c32_ready hc_ps hc_ready "
                 "counted key_ready fsp_ready stats_ready ctx_ps ctx_ev "
                 "xt_ready s_done v_done t_done pv_done w_done rowmax negmax_ready exp_done recip_ready norm_done "
                 "v_ev pt_ev o_ev h_read feat_ready feat_out h3_ps x1_ready x_ready out_done "
                 "late_in late2_in hn_ready hT_ps hT_ev scaled hi_done lo_done w_used proj_ps proj_ev rope_ready turn_ps turn_ev "
                 "g_s g_masked g_max g_negmax g_exp g_recip g_norm g_t g_tev g_pv g_oev tail_ps tail_ev tail_max "
                 "t_s t_max t_exp t_norm t_t t_tev t_pv t_oev y0_ps y_ps x_half gate_max gate_exp gate_ready gateT_ps gateT_ev "
                 "route_max route_exp route_ready routeT_ps routeT_ev dchain").split()
        S = {n: sem(n) for n in names}
        scattered = [sem(f"scattered{r}") for r in range(RUNS)]
        g01_in = [sem(f"g01_in{b}") for b in range(B)]
        slot_in = [sem(f"slot_in{i}") for i in range(SLOTS)]

        ctx_place = {"xk": ring[:, 0, :], "ctx0": ring[:, 2, :], "xv": ring[:, 1, :],
                     "ctx1": vals[:, NBLK:2 * NBLK, :].rearrange("p k n -> p (k n)"),
                     "ctx2": arena[:, fs_off:fs_off + CHUNK], "ctx3": ring[:, 2, :]}
        SPLITS = ["xk", "ctx1", "xv", "ctx2", "ctx3"]
        spare_at = {"xk": hc_off, "xv": mx_off, "ctx1": fsr_off, "ctx2": fsr_off + N, "ctx3": o_off}
        WSCALE = 256.0

        def raw_tile(nm, k):
            return ctx_place[nm][:, 512 * k:512 * k + 512]

        def pair(nm, k):
            ap = raw_tile(nm, k - 2) if k >= 2 else arena[:, spare_at[nm] + 512 * k:spare_at[nm] + 512 * (k + 1)]
            ap = ap.bitcast(F16)
            return ap[:, 0:512], ap[:, 512:1024]

        FIRST = ["xk", "ctx0", "xv", "ctx1", "ctx2", "ctx3"]
        stream_row = {nm: i for i, nm in enumerate(["xk", "xv", "ctx0", "ctx1", "ctx2", "ctx3"]
                                                   + [n for n in WEIGHTS if n not in ("xk", "xv")])}
        loads = {nm: (i % SLOTS, 16 * (i // SLOTS + 1)) for i, nm in enumerate(WEIGHTS)}

        summed = [nm for nm in WEIGHTS if nm[:2] in ("ao", "ba", "xo", "so") and nm not in ("ao1", "xo7", "so7")]

        def used_at(nm):
            if nm in summed:
                return S["w_used"], summed.index(nm) + 1
            if nm in ("ao1", "xo7", "so7"):
                return S["y_ps"], {"ao1": 1, "xo7": 3, "so7": 4}[nm]
            return S["proj_ps"], PROJ.index("xv_b1" if nm == "xv" else nm) + 1

        def chunk(eng, nm):
            s, v = loads[nm]
            eng.wait_ge(slot_in[s], v)
            return ring[:, s, :].rearrange("p (k n) -> p k n", n=N if nm[:2] in ("ao", "xo", "so") else 512)

        block = ctx.enter_context(nc.Block())

        @block.sync
        def _(sp):
            def first_parts(part):
                for nm in FIRST[0:2]:
                    c = slice(CHUNK // 2 * part, CHUNK // 2 * (part + 1))
                    sp.dma_start(ctx_place[nm][:, c], a["wstream"][stream_row[nm]][:, c]).then_inc(S[f"{nm}_{('lo', 'hi')[part]}"], 16)

            sp.dma_start(coord, a["coords"]).then_inc(S["coord_in"], 16)
            sp.dma_start(x[:], a["x"]).then_inc(S["x_in"], 16)
            sp.dma_start(ident[:], a["ident"]).then_inc(S["ident_in"], 16)
            first_parts(0)
            for dst, src in ((identh[:], "identh"), (lower[:], "lower"),
                             (rankoff[:], "rankoff"), (maskl[:], "maskl"), (maskr[:], "maskr"),
                             (wlin_n[:], "wlin_n"), (wlin_c[:], "wlin_c"), (blin[:], "blin"),
                             (wconv[0][:], "wconv0"), (wconv[1][:], "wconv1"), (wconv3[:], "wconv3")):
                sp.dma_start(dst, a[src]).then_inc(S["const_in"], 16)
            def stream(lo, hi):
                for i in range(lo, hi):
                    if i >= SLOTS:
                        sp.wait_ge(*used_at(WEIGHTS[i - SLOTS]))
                    else:
                        sp.wait_ge(S["ctx_ps"], 32)
                    sp.dma_start(ring[:, i % SLOTS, :], a["wstream"][stream_row[WEIGHTS[i]]]).then_inc(slot_in[i % SLOTS], 16)

            def sorted_in(r):
                sp.wait_ge(scattered[r], 16 * METHODS * NBLK)
                if r:
                    sp.wait_ge(S["fsp_ready"], r)
                sp.dma_start(fsr, sorted_d[r].rearrange("(k q) c -> q k c", q=P)).then_inc(S["fsr_in"], 16)

            def centres_in(r):
                layer, b = divmod(r, B)
                if layer == 0:
                    sp.wait_ge(S["feat_out0"], 16)
                else:
                    sp.wait_ge(S["feat_out"], 16 * (b + 1))
                if r:
                    sp.wait_ge(S["xt_ready"], BODIES * r)
                    sp.wait_ge(S["c16_ready"], r)
                for t in range(2):
                    for h in range(2):
                        src = feat_d[layer]
                        sp.dma_start(fc[64 * h:64 * h + 64, t, :],
                                     bass.AP(tensor=src.tensor, offset=(64 * b + 32 * t + 16 * h) * N,
                                             ap=[[0, METHODS], [N, 16], [1, N]])).then_inc(S["fc_in"], 16)

            def earlier_in(b):
                sp.wait_ge(S["feat_out"], 16 * (b + 1))
                if b:
                    sp.wait_ge(S["fsp_ready"], RUNS)
                for l in range(2):
                    sp.dma_start(g01[b][64 * l:64 * l + 64, :], feat_d[l][64 * b:64 * b + 64, :]).then_inc(g01_in[b], 16)

            first_parts(1)
            for nm in FIRST[2:]:
                if nm == "ctx3":
                    sp.wait_ge(S["ctx_ps"], 8)
                sp.dma_start(ctx_place[nm], a["wstream"][stream_row[nm]]).then_inc(S[nm + "_in"], 16)
            sp.wait_ge(S["ctx_ps"], 24)
            centres_in(0)
            sorted_in(0)
            stream(0, 1)
            for r in range(1, RUNS):
                sorted_in(r)
                centres_in(r)
                if r - 1 < B:
                    sp.wait_ge(S["feat_ready"], r)
                    sp.dma_start(feat_d[1][64 * (r - 1):64 * r, :], f0[0:64, :]).then_inc(S["feat_out"], 16)
            earlier_in(0)
            earlier_in(1)
            sp.wait_ge(S["fsT_ps"], 4 * RUNS)
            sp.wait_ge(S["c32_ready"], RUNS)
            stream(2, 3)
            sp.wait_ge(S["h3_ps"], B)
            stream(1, 2)
            sp.wait_ge(S["x1_ready"], 1)
            for dst, src in ((cosn, a["cosn"]), (sinn, a["sinn"]), (causal, a["causal"]), (wgate, a["wgate"]),
                             (lora_b, a["lora_b"]), (bbase, a["bbase"].partition_broadcast(P)),
                             (bthr, a["bthr"].partition_broadcast(P))):
                sp.dma_start(dst, src).then_inc(S["late_in"], 16)
            stream(SLOTS, WEIGHTS.index("sq0") + 3)
            sp.wait_ge(S["x_ready"], 3)
            for dst, src in ((samebatch, a["samebatch"]), (wroute, a["wroute"]), (ebias[0:64, :], a["ebias"]),
                             (rbias, a["rbias"].partition_broadcast(P))):
                sp.dma_start(dst, src).then_inc(S["late2_in"], 16)
            stream(WEIGHTS.index("sq0") + 3, len(WEIGHTS))
            sp.wait_ge(S["x_ready"], 5)
            sp.dma_start(out, x[:]).then_inc(S["out_done"], 16)
            sp.wait_ge(S["out_done"], 16)

        CONSTS = 16 * 11
        LATE, LATE2 = 16 * 7, 16 * 4

        def scatter(pool, r, j):
            layer, b = divmod(r, B)
            m, k = divmod(j, NBLK)
            if j == 0 and layer == 0:
                pool.wait_ge(S["rank_ready"], b + 1)
                pool.wait_ge(S["fnT_ev"], 2)
            elif j == 0:
                pool.wait_ge(S["fnT_ev"], 3 + b)
            col = (m * B + b) * NBLK + k
            pool.indirect_dma_start(
                out=sorted_d[r], out_offset=bass.IndirectOffsetOnAxis(ap=rowidx[:, col:col + 1], axis=0),
                in_=fn[:, k, 64 * b:64 * b + 64], in_offset=None).then_inc(scattered[r], 16)

        def n0_of(t):
            return t * BP if not isinstance(t, int) or t < BODIES - 1 else N - BP

        def win(t, lo, cnt):
            return bass.AP(tensor=arena, offset=fs_off + lo, ap=[[ARENA, P], [FSW, 2], [1, cnt], [1, KW]])

        def centre(lo, cnt):
            return bass.AP(tensor=arena, offset=fc_off + lo, ap=[[ARENA, P], [N, 2], [1, cnt], [0, KW]])

        def xt_body(pool, base, t, par):
            u = base + t
            par = par if not isinstance(t, int) else u % 2
            if not isinstance(t, int) or u >= 2:
                pool.wait_ge(S["v_done"], u - 1)
            dst = xt[:, par, :, :].rearrange("p t (n k) -> p t n k", k=KW)
            if isinstance(t, int) and t == 0:
                nc.gpsimd.tensor_tensor(dst[:, :, 0:5, :], fh, centre(0, 5), ALU.subtract)
                nc.gpsimd.tensor_tensor(dst[:, :, 5:BP, :], win(t, 5, BP - 5), centre(5, BP - 5), ALU.subtract)\
                    .then_inc(S["xt_ready"], 1)
            else:
                n0 = n0_of(t)
                nc.gpsimd.tensor_tensor(dst, win(t, n0, BP), centre(n0, BP), ALU.subtract).then_inc(S["xt_ready"], 1)

        def norm_half(pool, base, t, par, g):
            u = base + t
            par = par if not isinstance(t, int) else u % 2
            if True:
                pool.wait_ge(S["recip_ready"], 2 * u + g + 1)
                pr = p_sb[0:GROWS, par].rearrange("p (f g k) n -> p f g k n", f=2, g=2)[:, :, g]
                sums = rsum[0:GROWS, par, 1].rearrange("p (f g k) -> p f g k", f=2, g=2)[:, :, g]
                nc.gpsimd.tensor_tensor(pr, pr, sums.unsqueeze(3).broadcast_to([GROWS, 2, 2, GROWS]), ALU.mult)\
                    .then_inc(S["norm_done"], 1)

        @block.gpsimd
        def _(pool):
            pool.wait_ge(S["minmax_ready"], 1)
            nc.gpsimd.partition_all_reduce(ext[:, 2:4, :], ext[:, 0:2, :], P, bass.bass_isa.ReduceOp.max)\
                .then_inc(S["minmax_all"], 1)

            def powers(n, rows=P):
                pool.wait_ge(S["pow_ready"], n)
                nc.gpsimd.tensor_tensor(small[0:rows, 2:3], small[0:rows, 1:2], small[0:rows, 8:9], ALU.pow)\
                    .then_inc(S["pow_done"], 1)

            powers(1)
            pool.wait_ge(S["ln_ready"], 1)
            pool.dma_start(feat_d[0], f0).then_inc(S["feat_out0"], 16)
            def low_parts(lo, hi):
                for n in range(lo, hi):
                    nm, k = SPLITS[n // KT], n % KT
                    pool.wait_ge(S["hi_done"], n + 1)
                    h, l = pair(nm, k)
                    nc.gpsimd.tensor_tensor(l, raw_tile(nm, k), h, ALU.subtract).then_inc(S["lo_done"], 1)

            low_parts(0, 4)
            pool.wait_ge(S["keycol_ready"], 1)
            pool.dma_start(keys_d, keycol[:]).then_inc(S["keys_out"], 16)
            pool.wait_ge(S["keys_out"], 16)
            kd = keys_d.rearrange("(m b k) q -> b m (k q)", m=METHODS, b=B)
            pool.dma_start(keyrow, kd[0].partition_broadcast(P)).then_inc(S["keyrow_in"], 16)
            low_parts(4, KT * len(SPLITS))
            pool.wait_ge(S["keyrow_free"], 1)
            pool.dma_start(keyrow, kd[1].partition_broadcast(P)).then_inc(S["keyrow_in"], 16)
            for j in range(METHODS * NBLK):
                scatter(pool, 0, j)
            for r in range(RUNS):
                layer, b = divmod(r, B)
                pool.wait_ge(S["fsT_ev"], 4 * (r + 1))
                pool.wait_ge(S["fh_ready"], r + 1)
                pool.wait_ge(S["fc_in"], 64 * (r + 1))
                base = BODIES * r
                p0 = base % 2
                p1 = 1 - p0
                xt_body(pool, base, 0, p0)
                if r:
                    powers(1 + r, OUTC[(r - 1) // B])
                xt_body(pool, base, 1, p1)
                xt_body(pool, base, 2, p0)
                norm_half(pool, base, 0, p0, 0)

                def step(t, par):
                    norm_half(pool, base, t, par, 1)
                    if not isinstance(t, int) or t + 3 < BODIES:
                        xt_body(pool, base, t + 3, 1 - par)
                    if not isinstance(t, int) or t + 1 < BODIES:
                        norm_half(pool, base, t + 1, 1 - par, 0)

                if r + 1 < RUNS:
                    for t in range(BODIES):
                        step(t, (base + t) % 2)
                        if 0 <= t - 3 < METHODS * NBLK:
                            scatter(pool, r + 1, t - 3)
                else:
                    step(0, p0)
                    with pool.Fori(1, BODIES - 4, 2) as t:
                        step(t, p1)
                        step(t + 1, p0)
                    for t in range(BODIES - 4, BODIES):
                        step(t, (base + t) % 2)
            powers(1 + RUNS, OUTC[1])
            powers(2 + RUNS)
            def normalise(n):
                pool.wait_ge(S["g_recip"], n + 1)
                pr = (gp if n < AGROUPS else sp_)[:, n % 2]
                nc.gpsimd.tensor_tensor(pr, pr, gsum[:, n % 2, 3, :].unsqueeze(2).broadcast_to([P, 4, P]), ALU.mult)\
                    .then_inc(S["g_norm"], 1)

            powers(3 + RUNS)
            for n in range(AGROUPS):
                normalise(n)
            powers(4 + RUNS)
            powers(5 + RUNS)
            powers(6 + RUNS)
            for n in range(AGROUPS, AGROUPS + SGROUPS):
                normalise(n)
            powers(7 + RUNS)

        def ctx_bank(g):
            return (ps_vh[:], ps_o[:], ps_pt[:, 0], ps_pt[:, 1])[g] if g < 4 else (ps_vh[:], ps_o[:])[g % 2]

        def map_out(which, l, t):
            lo = P * l + OUTC[l] * t
            return ps_s[:, 0, which, lo:lo + OUTC[l]]

        def ctx_group(pe, g, ks):
            c, j = divmod(g, 8)
            cx = ctx_place[f"ctx{c}"].rearrange("p (k n) -> p k n", k=KT)
            wk = ring[:, 0, :].rearrange("p (k n) -> p k n", k=KT)
            wv = ring[:, 1, :].rearrange("p (k n) -> p k n", k=KT)
            if g >= 4:
                pe.wait_ge(S["ctx_ev"], g - 1)
            q = j % 4
            blk = slice(q * P, (q + 1) * P)
            for k in ks:
                if c == 0:
                    l, r = (wk[:, k, blk], cx[:, k, :]) if j < 4 else (cx[:, k, blk], wv[:, k, :])
                    mm = nc.tensor.matmul(ctx_bank(g), l, r, start=k == 0, stop=k == KT - 1)
                    continue
                names = ("xk", f"ctx{c}") if j < 4 else (f"ctx{c}", "xv")
                if j % 4 == 0:
                    for nm in names:
                        pe.wait_ge(S["lo_done"], KT * SPLITS.index(nm) + k + 1)
                (lh, ll), (rh, rl) = (pair(nm, k) for nm in names)
                for i, (l, r) in enumerate(((lh, rh), (lh, rl), (ll, rh))):
                    mm = nc.tensor.matmul(ctx_bank(g), l[:, blk], r, start=(k, i) == (0, 0), stop=(k, i) == (KT - 1, 2))
            if ks[-1] == KT - 1:
                mm.then_inc(S["ctx_ps"], 1)

        def ctx_groups(pe, lo, hi):
            for g in range(lo, hi):
                if g == 4:
                    pe.wait_ge(S["xv_in"], 16)
                ctx_group(pe, g, range(KT))

        def sorted_transposes(pe, r, t):
            pe.wait_ge(S["fsp_ready"], r + 1)
            par = (BODIES * r + t) % 2
            if r:
                pe.wait_ge(S["exp_done"], 2 * (BODIES * r - 1 + t))
            for h in range(2):
                for k in range(4):
                    src = fsp[r][:, 4 * h + k, 128 * t:128 * t + 128]
                    mm = nc.tensor.transpose(ps_s[:, par, h, k * P:(k + 1) * P], src, ident[:])
                mm.then_inc(S["fsT_ps"], 1)

        @block.tensor
        def _(pe):
            pe.wait_ge(S["ident_in"], 16)
            pe.wait_ge(S["ln_ready"], 1)
            for h in range(2):
                if h:
                    pe.wait_ge(S["fnT_ev"], h)
                for k in range(4):
                    mm = nc.tensor.transpose(ps_f[:, k * P:(k + 1) * P], f0[:, (4 * h + k) * P:(4 * h + k + 1) * P], ident[:])
                mm.then_inc(S["fnT_ps"], 1)
            for half in range(2):
                for nm in ("xk", "ctx0"):
                    pe.wait_ge(S[f"{nm}_{('lo', 'hi')[half]}"], 16)
                for g in range(4):
                    ctx_group(pe, g, range(4 * half, 4 * half + 4))
            ctx_groups(pe, 4, 5)
            pe.wait_ge(S["key_ready"], 1)
            pe.wait_ge(S["fnT_ev"], 2)
            nc.tensor.transpose(ps_f[0:64, 0:P], key[:].bitcast(F32), ident[:]).then_inc(S["keyT_ps"], 1)
            pe.wait_ge(S["const_in"], CONSTS)
            for l in range(2):
                for which, w in enumerate((wlin_n, wlin_c)):
                    for t in range(2):
                        nc.tensor.matmul(map_out(which, l, t), w[:, l, t * P:(t + 1) * P], wconv[l][:], start=True, stop=True)
                mm = nc.tensor.matmul(ps_s[0:OUTC[l], 0, 1, 384 + l:385 + l], wconv[l][:], blin[:, l:l + 1], start=True, stop=True)
            mm.then_inc(S["wp_ps"], 1)
            ctx_groups(pe, 5, CTX_OPEN)
            pe.wait_ge(S["keycol_ready"], 1)
            pe.wait_ge(S["wp_ev"], 1)
            for t in range(2):
                sorted_transposes(pe, 0, t)
            ctx_groups(pe, CTX_OPEN, 31)
            for r in range(RUNS):
                layer, b = divmod(r, B)
                O = OUTC[layer]
                base = BODIES * r

                def centre_output(h):
                    pe.wait_ge(S["c32_ready"], r + 1)
                    if r:
                        pe.wait_ge(S["pt_ev"], 2 * base)
                    for t in range(2):
                        mm = nc.tensor.matmul(ps_pt[0:O, h, :], wc[layer][:, t, :], c32[r][:, N * t + 512 * h:N * t + 512 * h + 512],
                                              start=t == 0, stop=t == 1)
                    mm.then_inc(S["hc_ps"], 1)

                def scores(t, par):
                    u = base + t
                    st = isinstance(t, int)
                    pe.wait_ge(S["xt_ready"], u + 1)
                    if not st or u >= 2:
                        pe.wait_ge(S["exp_done"], 2 * u - 2)
                    for half in range(2):
                        q = slice(64 * half, 64 * half + 64)
                        nc.tensor.matmul(ps_s[0:GROWS, par, half, 0:4 * GROWS], maskl[q, :], maskr[q, :], start=True, stop=False,
                                         skip_group_check=True)
                        for g in range(2):
                            for k in range(2):
                                c0 = (2 * g + k) * GROWS
                                xs = xt[q, par, k, g * GROWS:(g + 1) * GROWS]
                                mm = nc.tensor.matmul(ps_s[0:GROWS, par, half, c0:c0 + GROWS], xs, xs, start=False,
                                                      stop=(g, k) == (1, 1), skip_group_check=True)
                    mm.then_inc(S["s_done"], 1)

                def values(t, par):
                    u = base + t
                    st = isinstance(t, int)
                    pe.wait_ge(S["xt_ready"], u + 1)
                    if not st or u >= 1:
                        pe.wait_ge(S["v_ev"], u)
                    else:
                        pe.wait_ge(S["ctx_ev"], 31)
                    if not st or t >= 3:
                        pe.wait_ge(S["h_read"], u - 2)
                    elif r:
                        pe.wait_ge(S["h_read"], base)
                    for g in range(2):
                        for k in range(2):
                            mm = nc.tensor.transpose(ps_v[0:GROWS, g, k * P:(k + 1) * P],
                                                     xt[:, par, k, g * GROWS:(g + 1) * GROWS], identh[:])
                    mm.then_inc(S["v_done"], 1)

                def turn_probs(t, par, g):
                    u = base + t
                    st = isinstance(t, int)
                    if st and t == 0:
                        pe.wait_ge(S["hc_ready"], 2 * r + g + 1)
                    if not st or u >= 1:
                        pe.wait_ge(S["pt_ev"], 2 * u + g - 1)
                    pe.wait_ge(S["norm_done"], 2 * u + g + 1)
                    for h in range(4):
                        mm = nc.tensor.transpose(ps_pt[0:GROWS, g, h * GROWS:(h + 1) * GROWS],
                                                 p_sb[0:GROWS, par, 4 * (h % 2) + 2 * g + h // 2, :],
                                                 ident[0:GROWS, 0:GROWS])
                    mm.then_inc(S["t_done"], 1)

                def attend(t, par):
                    u = base + t
                    st = isinstance(t, int)
                    pe.wait_ge(S["v_ev"], u + 1)
                    if not st or u >= 1:
                        pe.wait_ge(S["o_ev"], u)
                    else:
                        pe.wait_ge(S["ctx_ev"], 32)
                    for g in range(2):
                        pe.wait_ge(S["pt_ev"], 2 * u + g + 1)
                        for h in range(4):
                            q = 64 * (h % 2)
                            c0 = (h // 2) * BCOLS + g * GROWS
                            mm = nc.tensor.matmul(ps_o[q:q + 64, c0:c0 + GROWS], vs_sb[0:GROWS, par, g, 64 * h:64 * h + 64],
                                                  pt_sb[0:GROWS, par, 4 * g + h, :], start=True, stop=True)
                    mm.then_inc(S["pv_done"], 1)

                def project(t, par):
                    u = base + t
                    st = isinstance(t, int)
                    pe.wait_ge(S["o_ev"], u + 1)
                    pe.wait_ge(S["v_ev"], base + BODIES if st and t >= BODIES - 2 else u + 3)
                    if not st or u >= 1:
                        pe.wait_ge(S["h_read"], u)
                    for k in range(2):
                        mm = nc.tensor.matmul(ps_hg[0:O, :], wp[layer][:, k, :], o_sb[:, par, k, :],
                                              start=k == 0, stop=k == 1)
                    mm.then_inc(S["w_done"], 1)

                def batch_features(b):
                    pe.wait_ge(S["feat_ready"], b + 1)
                    pe.wait_ge(S["o_ev"], base)
                    for k in range(NBLK):
                        mm = nc.tensor.transpose(ps_o[:, k * 64:(k + 1) * 64], f0[0:64, k * P:(k + 1) * P], ident[0:64, 0:64])
                    mm.then_inc(S["fnT_ps"], 1)
                    pe.wait_ge(S["fnT_ev"], 3 + b)

                p0 = base % 2
                p1 = 1 - p0
                scores(0, p0)
                if r:
                    values(0, p0)
                centre_output(0)
                scores(1, p1)
                centre_output(1)
                if r == 0:
                    ctx_groups(pe, 31, 32)
                    values(0, p0)

                def step(t, par, last=False):
                    turn_probs(t, par, 0)
                    if not isinstance(t, int) or t + 2 < BODIES:
                        scores(t + 2, par)
                    if last and r + 1 < RUNS:
                        sorted_transposes(pe, r + 1, 0)
                    if not last:
                        values(t + 1, 1 - par)
                    turn_probs(t, par, 1)
                    if last and r + 1 < RUNS:
                        sorted_transposes(pe, r + 1, 1)
                    if isinstance(t, int) and t == 0 and 0 < r <= B:
                        batch_features(r - 1)
                    if not isinstance(t, int) or t:
                        project(t - 1, 1 - par)
                    attend(t, par)

                step(0, p0)
                step(1, p1)
                step(2, p0)
                with pe.Fori(3, BODIES - 2, 2) as t:
                    step(t, p1)
                    step(t + 1, p0)
                step(BODIES - 2, p1)
                step(BODIES - 1, p0, last=True)
                project(BODIES - 1, p0)
            for b in range(B):
                pe.wait_ge(S["feat_ready"], B + b + 1)
                pe.wait_ge(g01_in[b], 32)
                pe.wait_ge(S["pt_ev"], 2 * BODIES * RUNS)
                for h in range(2):
                    cols = slice(512 * h, 512 * h + 512)
                    nc.tensor.matmul(ps_pt[64 * b:64 * b + 64, h, :], wconv3[:, 0, :], g01[b][:, cols], start=True, stop=False)
                    mm = nc.tensor.matmul(ps_pt[64 * b:64 * b + 64, h, :], wconv3[:, 1, :], f2[b][:, cols], start=False, stop=True)
                mm.then_inc(S["h3_ps"], 1)

            norms = [0]

            def transpose_tokens(n):
                for h in range(2):
                    pe.wait_ge(S["hn_ready"], 2 * n + h + 1)
                    for k in range(4):
                        mm = nc.tensor.transpose(ps_pt[:, h, k * P:(k + 1) * P], hn[:, (4 * h + k) * P:(4 * h + k + 1) * P], ident[:])
                    mm.then_inc(S["hT_ps"], 1)
                norms[0] = n

            def token_tiles():
                for k in range(KT):
                    if k % 4 == 0:
                        pe.wait_ge(S["hT_ev"], 2 * norms[0] + k // 4 + 1)
                    yield k

            def bank_for(nm):
                g = PROJ.index(nm)
                if g >= 2:
                    pe.wait_ge(S["proj_ev"], g - 1)
                return proj_bank[g % 2]

            def project_tokens(nm):
                w = chunk(pe, nm)
                bank = bank_for(nm)
                for k in token_tiles():
                    mm = nc.tensor.matmul(bank, hT[:, k, :], w[:, k, :], start=k == 0, stop=k == KT - 1)
                mm.then_inc(S["proj_ps"], 1)

            def small_product(nm, w, cols):
                bank = bank_for(nm)
                for k in token_tiles():
                    mm = nc.tensor.matmul(bank[:, 0:cols], hT[:, k, :], w[:, k, :], start=k == 0, stop=k == KT - 1)
                mm.then_inc(S["proj_ps"], 1)

            def turn(nm, src):
                n = TURNS.index(nm)
                pe.wait_ge(S["proj_ev"] if nm[0] != "a" else S["rope_ready"],
                           PROJ.index(nm) + 1 if nm[0] != "a" else 1 + ("ak" in nm))
                if n >= 2:
                    pe.wait_ge(S["turn_ev"], n - 1)
                for k in range(4):
                    mm = nc.tensor.transpose(ps_pt[:, n % 2, k * P:(k + 1) * P], src[:, k * P:(k + 1) * P], ident[:])
                mm.then_inc(S["turn_ps"], 1)

            def group_scores(n):
                if n >= 2:
                    pe.wait_ge(S["g_masked"], n - 1)
                bank = ps_s[:, 0, n % 2]
                for i in range(4):
                    if n < AGROUPS:
                        q, t = slice(64 * (n % 2), 64 * (n % 2) + 64), 4 * (n // 2) + i
                        l, r = aqT[q, t, :], akT[q, t, :]
                    else:
                        l, r = sqT[:, 4 * (n - AGROUPS) + i, :], skT[:, n - AGROUPS, :]
                    mm = nc.tensor.matmul(bank[:, i * P:(i + 1) * P], l, r, start=True, stop=True)
                mm.then_inc(S["g_s"], 1)

            def group_turn(n):
                pe.wait_ge(S["g_norm"], n + 1)
                if n >= 2:
                    pe.wait_ge(S["g_tev"], n - 1)
                pr = (gp if n < AGROUPS else sp_)[:, n % 2]
                for i in range(4):
                    mm = nc.tensor.transpose(ps_pt[:, n % 2, i * P:(i + 1) * P], pr[:, i, :], ident[:])
                mm.then_inc(S["g_t"], 1)

            def group_outputs(n):
                pe.wait_ge(S["g_tev"], n + 1)
                if n >= 2:
                    pe.wait_ge(S["g_oev"], n - 1)
                bank = proj_bank[n % 2]
                if n < AGROUPS:
                    q = 64 * (n % 2)
                    for i in range(4):
                        c = (4 * (n // 2) + i) * P + q
                        mm = nc.tensor.matmul(bank[q:q + 64, i * P:(i + 1) * P], av[:, c:c + 64], gpT[:, n % 2, i, :],
                                              start=True, stop=True)
                else:
                    c = (n - AGROUPS) * P
                    mm = nc.tensor.matmul(bank, sv[:, c:c + P], spT[:, n % 2].rearrange("p h n -> p (h n)"), start=True, stop=True)
                mm.then_inc(S["g_pv"], 1)

            def output_chunk(names, j, oT):
                w = chunk(pe, names[j])
                last = j == len(names) - 1
                for h, k in [(h, k) for h in range(2) for k in range(4)] if last else [(h, k) for k in range(4) for h in range(2)]:
                    mm = nc.tensor.matmul(y_ps[h], oT[:, 4 * j + k, :], w[:, k, 512 * h:512 * h + 512],
                                          start=(j, k) == (0, 0), stop=(j, k) == (len(names) - 1, 3),
                                          skip_group_check=True)
                    if last and (h, k) == (0, 3):
                        mm.then_inc(S["y0_ps"], 1)
                mm.then_inc(S["y_ps"] if last else S["w_used"], 1)

            def groups(lo, hi, names, oT, values):
                per = (hi - lo) // len(names)

                def map_chunk(n):
                    if n >= lo and (n - lo) % per == per - 1:
                        pe.wait_ge(S["g_oev"], n + 1)
                        output_chunk(names, (n - lo) // per, oT)

                group_scores(lo)
                group_scores(lo + 1)
                project_tokens(values)
                pe.wait_ge(S["proj_ev"], PROJ.index(values) + 1)
                for n in range(lo, hi):
                    if n + 2 < hi:
                        group_scores(n + 2)
                    if n > lo:
                        group_outputs(n - 1)
                    group_turn(n)
                    map_chunk(n - 2)
                group_outputs(hi - 1)
                map_chunk(hi - 2)
                map_chunk(hi - 1)

            transpose_tokens(0)
            for nm in ("aq0", "aq1", "ak0", "ak1", "av0"):
                project_tokens(nm)
            for nm, src in (("aq0", aq[:, 0:512]), ("aq1", aq[:, 512:N]), ("ak0", ak[:, 0:512]), ("ak1", ak[:, 512:N])):
                turn(nm, src)
            pe.wait_ge(S["turn_ev"], 4)
            groups(0, AGROUPS, ["ao0", "ao1"], aoT, "av1")
            transpose_tokens(1)
            pe.wait_ge(S["late_in"], LATE)
            small_product("gates", wgate, GATES)
            for h in range(2):
                w = chunk(pe, f"base{h}")
                for k in range(KT):
                    mm = nc.tensor.matmul(y_ps[h], hT[:, k, :], w[:, k, :], start=k == 0, stop=False, skip_group_check=True)
                mm.then_inc(S["w_used"], 1)
            pe.wait_ge(S["gate_ready"], 1)
            nc.tensor.transpose(ps_pt[:, 0, 0:P], lora, ident[:]).then_inc(S["gateT_ps"], 1)
            pe.wait_ge(S["gateT_ev"], 1)
            for h in range(2):
                nc.tensor.matmul(y_ps[h], loraT, lora_b[:, 512 * h:512 * h + 512], start=False, stop=True, skip_group_check=True)\
                    .then_inc(S["y_ps"] if h else S["y0_ps"], 1)
            transpose_tokens(2)
            for i in range(8):
                project_tokens(f"xq{i}")
                if i:
                    turn(f"xq{i - 1}", sq[:, 512 * (i - 1):512 * i])
            turn("xq7", sq[:, 512 * 7:512 * 8])
            w = chunk(pe, "xk")
            bank = bank_for("xk")
            for h in range(4):
                for k in range(KT):
                    mm = nc.tensor.matmul(bank[:, h * P:(h + 1) * P], w[:, k, h * P:(h + 1) * P], hT[:, k, :], start=k == 0, stop=k == KT - 1)
            mm.then_inc(S["proj_ps"], 1)
            w = chunk(pe, "xv")
            for b in range(B):
                bank = bank_for(f"xv_b{b}")
                for k in range(KT):
                    mm = nc.tensor.matmul(bank[0:64, :], hT[:, k, 64 * b:64 * b + 64], w[:, k, :], start=k == 0, stop=k == KT - 1)
                mm.then_inc(S["proj_ps"], 1)
            pe.wait_ge(S["proj_ev"], PROJ.index("xv_b1") + 1)
            pe.wait_ge(S["turn_ev"], TURNS.index("xq7") + 1)

            def x_scores(n):
                b, h, g = n // 16, n // 4 % 4, n % 4
                if n >= 2:
                    pe.wait_ge(S["t_exp"], n - 1)
                else:
                    pe.wait_ge(S["x_ready"], 2)
                l = xqT[:, b, 8 * h + 2 * g:8 * h + 2 * g + 2, :].rearrange("p h n -> p (h n)")
                for c in range(2):
                    lo = b * KV + 512 * c
                    mm = nc.tensor.matmul(ps_s[:, n % 2, c], l, keysT[:, h, lo:lo + 512], start=True, stop=True)
                mm.then_inc(S["t_s"], 1)

            def tail_scores(c):
                if c >= 2:
                    pe.wait_ge(S["tail_ev"], c - 1)
                for n in range(8 * c, 8 * c + 8):
                    b, h, g = n // 16, n // 4 % 4, n % 4
                    l = xqT[:, b, 8 * h + 2 * g:8 * h + 2 * g + 2, :].rearrange("p h n -> p (h n)")
                    mm = nc.tensor.matmul(x_bank[c % 2][:, 64 * (n % 8):64 * (n % 8) + 64], l,
                                          keysT[:, h, b * KV + N:b * KV + KV], start=True, stop=True)
                mm.then_inc(S["tail_ps"], 1)

            def x_turn(n):
                pe.wait_ge(S["t_norm"], n + 1)
                for j in range(3):
                    if n:
                        pe.wait_ge(S["t_tev"], 3 * n - 2 + j)
                    if j == 2 and n >= 2:
                        pe.wait_ge(S["t_oev"], n - 1)
                    for k in range(4 * j, min(4 * j + 4, KVT)):
                        w = P if k < KVT - 1 else 64
                        dst = ps_pt[:, j, (k % 4) * P:(k % 4 + 1) * P] if j < 2 else x_bank[n % 2][0:64, P:2 * P]
                        mm = nc.tensor.transpose(dst, xp[:, n % 2, k * P:k * P + w], ident[:])
                    mm.then_inc(S["t_t"], 1)

            def x_outputs(n):
                b, h, g = n // 16, n // 4 % 4, n % 4
                pe.wait_ge(S["t_tev"], 3 * n + 3)
                for k in range(KVT):
                    if k < KVT - 1:
                        l, r = vals[:, NBLK * b + k, h * P:(h + 1) * P], xpT[:, n % 2, k, :]
                    else:
                        l, r = vlat[0:64, b, h * P:(h + 1) * P], xpT[0:64, n % 2, k, :]
                    mm = nc.tensor.matmul(x_bank[n % 2][:, 0:P], l, r, start=k == 0, stop=k == KVT - 1)
                mm.then_inc(S["t_pv"], 1)

            tail_scores(0)
            x_scores(0)
            x_scores(1)
            for c in range(1, 4):
                tail_scores(c)
            for n in range(XTILES):
                x_turn(n)
                if n + 2 < XTILES:
                    x_scores(n + 2)
                x_outputs(n)
            pe.wait_ge(S["t_oev"], XTILES)
            for j in range(8):
                output_chunk([f"xo{i}" for i in range(8)], j, soT)
            transpose_tokens(3)
            for i in range(8):
                project_tokens(f"sq{i}")
                if i:
                    turn(f"sq{i - 1}", sq[:, 512 * (i - 1):512 * i])
            turn("sq7", sq[:, 512 * 7:512 * 8])
            for nm in ("sk0", "sk1", "sv0"):
                project_tokens(nm)
            turn("sk0", sk[:, 0:512])
            turn("sk1", sk[:, 512:N])
            pe.wait_ge(S["turn_ev"], len(TURNS))
            groups(AGROUPS, AGROUPS + SGROUPS, [f"so{i}" for i in range(8)], soT, "sv1")
            transpose_tokens(4)
            pe.wait_ge(S["late2_in"], LATE2)
            small_product("route", wroute, 64)
            pe.wait_ge(S["route_ready"], 1)
            nc.tensor.transpose(ps_pt[0:64, 0, 0:P], route[:, 4, :], ident[:]).then_inc(S["routeT_ps"], 1)
            pe.wait_ge(S["routeT_ev"], 1)
            for h in range(2):
                mm = nc.tensor.matmul(y_ps[h], rT[0:64, :], ebias[0:64, 512 * h:512 * h + 512], start=True, stop=True)
            mm.then_inc(S["y_ps"], 1)

        @block.scalar
        def _(act):
            for h in range(2):
                act.wait_ge(S["fnT_ps"], h + 1)
                nc.scalar.copy(fn[:, 4 * h:4 * h + 4, :], ps_f.rearrange("p (k c) -> p k c", k=4)).then_inc(S["fnT_ev"], 1)
            def ctx_out(lo, hi):
                for g in range(lo, hi):
                    c, j = divmod(g, 8)
                    act.wait_ge(S["ctx_ps"], g + 1)
                    if j < 4:
                        lo_ = (c // 2) * KV + (c % 2) * 512
                        dst = keysT[:, j, lo_:lo_ + 512]
                    else:
                        dst = vals[:, 4 * c + j - 4, :]
                    if c == 0:
                        nc.scalar.copy(dst, ctx_bank(g)).then_inc(S["ctx_ev"], 1)
                    else:
                        nc.scalar.activation(dst, ctx_bank(g), ACT.Copy, scale=1.0 / WSCALE).then_inc(S["ctx_ev"], 1)

            def regroup(r):
                act.wait_ge(S["fsr_in"], 16 * (r + 1))
                if r:
                    act.wait_ge(S["fsT_ps"], 4 * r)
                for m in range(METHODS):
                    cp = nc.scalar.copy(fsp[r].rearrange("p k (h m c) -> p m k h c", h=4, m=METHODS)[:, m],
                                        fsr.rearrange("p (m k) (h c) -> p m k h c", m=METHODS, h=4)[:, m])
                cp.then_inc(S["fsp_ready"], 1)

            def sorted_out(r, t):
                par = (BODIES * r + t) % 2
                if r:
                    act.wait_ge(S["xt_ready"], BODIES * r)
                for h in range(2):
                    act.wait_ge(S["fsT_ps"], 4 * r + 2 * t + h + 1)
                    nc.scalar.copy(fs[:, t, 5 + 512 * h:5 + 512 * h + 512], ps_s[:, par, h]).then_inc(S["fsT_ev"], 1)

            def high_parts(lo, hi):
                for n in range(lo, hi):
                    nm, k = SPLITS[n // KT], n % KT
                    if k == 0:
                        if nm[0] == "c":
                            act.wait_ge(S[nm + "_in"], 16)
                        act.wait_ge(S["ctx_ps"], 4 if nm == "xk" else 8 if nm == "xv" else 1)
                        if nm == "ctx3":
                            act.wait_ge(S["keyT_ps"], 1)
                        if nm[0] == "x":
                            w = ctx_place[nm]
                            nc.scalar.activation(w, w, ACT.Copy, scale=WSCALE).then_inc(S["scaled"], 1)
                            act.wait_ge(S["scaled"], 1 + (nm == "xv"))
                    if k >= 2:
                        act.wait_ge(S["lo_done"], n - 1)
                    nc.scalar.copy(pair(nm, k)[0], raw_tile(nm, k)).then_inc(S["hi_done"], 1)

            done = 0
            for g in range(CTX_OPEN - 1):
                ctx_out(g, g + 1)
                if g == 4:
                    act.wait_ge(S["keyT_ps"], 1)
                    nc.scalar.copy(keycol[:], ps_f[0:64, 0:P]).then_inc(S["keycol_ready"], 1)
                    act.wait_ge(S["wp_ps"], 1)
                    for l in range(2):
                        O = OUTC[l]
                        for t in range(2):
                            nc.scalar.copy(wp[l][:, t, :], map_out(0, l, t))
                            nc.scalar.copy(wc[l][:, t, :], map_out(1, l, t))
                        cp = nc.scalar.copy(cb[0:O, l:l + 1], ps_s[0:O, 0, 1, 384 + l:385 + l])
                    cp.then_inc(S["wp_ev"], 1)
                if g >= 3:
                    hi = min(done + (4 if g < 5 else 4 if g < 8 else 4), KT * len(SPLITS))
                    high_parts(done, hi)
                    done = hi
            act.wait_ge(S["rank_ready"], 2)
            regroup(0)
            ctx_out(CTX_OPEN - 1, CTX_OPEN)
            sorted_out(0, 0)
            sorted_out(0, 1)
            ctx_out(CTX_OPEN, 31)
            for r in range(RUNS):
                layer, b = divmod(r, B)
                O = OUTC[layer]
                base = BODIES * r

                def centre_out(h):
                    act.wait_ge(S["hc_ps"], 2 * r + h + 1)
                    if r:
                        act.wait_ge(S["h_read"], base)
                    nc.scalar.activation(hc[0:O, 512 * h:512 * h + 512], ps_pt[0:O, h], ACT.Identity,
                                         bias=cb[0:O, layer:layer + 1]).then_inc(S["hc_ready"], 1)

                def values_out(t, par):
                    u = base + t
                    st = isinstance(t, int)
                    act.wait_ge(S["v_done"], u + 1)
                    if not st or u >= 2:
                        act.wait_ge(S["pv_done"], u - 1)
                    nc.scalar.copy(vs_sb[0:GROWS, par, :, :], ps_v[0:GROWS, :, 0:256]).then_inc(S["v_ev"], 1)

                def exponentials(t, par, g):
                    u = base + t
                    st = isinstance(t, int)
                    act.wait_ge(S["negmax_ready"], u + 1)
                    if not st or u >= 2:
                        act.wait_ge(S["t_done"], 2 * u - 3 + g)
                    for n in (2 * g, 2 * g + 1, 4 + 2 * g, 5 + 2 * g):
                        e = nc.scalar.activation(p_sb[0:GROWS, par, n, :],
                                                 ps_s[0:GROWS, par, n // 4, (n % 4) * GROWS:(n % 4 + 1) * GROWS], ACT.Exp,
                                                 bias=negmax[0:GROWS, par, 1, n:n + 1], scale=0.125,
                                                 accum_out=rsum[0:GROWS, par, 0, n:n + 1])
                    e.then_inc(S["exp_done"], 1)

                def outputs_out(t, par):
                    u = base + t
                    st = isinstance(t, int)
                    act.wait_ge(S["pv_done"], u + 1)
                    if not st or u >= 2:
                        act.wait_ge(S["w_done"], u - 1)
                    nc.scalar.copy(o_sb[:, par, :, :], ps_o[:, 0:2 * BCOLS].rearrange("p (t n) -> p t n", t=2))\
                        .then_inc(S["o_ev"], 1)

                p0 = base % 2
                p1 = 1 - p0
                if r:
                    values_out(0, p0)
                exponentials(0, p0, 0)
                centre_out(0)
                exponentials(0, p0, 1)
                centre_out(1)
                if r == 0:
                    ctx_out(31, 32)
                    values_out(0, p0)

                def step(t, par, last=False):
                    if last and r + 1 < RUNS:
                        sorted_out(r + 1, 0)
                    if not last:
                        exponentials(t + 1, 1 - par, 0)
                    if not isinstance(t, int) or t:
                        outputs_out(t - 1, 1 - par)
                    if last and r + 1 < RUNS:
                        sorted_out(r + 1, 1)
                    if not last:
                        values_out(t + 1, 1 - par)
                        exponentials(t + 1, 1 - par, 1)

                step(0, p0)
                step(1, p1)
                step(2, p0)
                with act.Fori(3, BODIES - 2, 2) as t:
                    step(t, p1)
                    step(t + 1, p0)
                if r + 1 < RUNS:
                    regroup(r + 1)
                step(BODIES - 2, p1)
                step(BODIES - 1, p0, last=True)
                outputs_out(BODIES - 1, p0)
            def tokens_out(n):
                for h in range(2):
                    act.wait_ge(S["hT_ps"], 2 * n + h + 1)
                    nc.scalar.copy(hT[:, 4 * h:4 * h + 4, :], heads(ps_pt[:, h], P)).then_inc(S["hT_ev"], 1)

            def proj_out(nm, dst, rows=P):
                g = PROJ.index(nm)
                act.wait_ge(S["proj_ps"], g + 1)
                w = dst.shape[-1] if len(dst.shape) == 2 else 512
                src = proj_bank[g % 2][0:rows, 0:w]
                if len(dst.shape) == 4:
                    src = src.rearrange("p (h b n) -> p h b n", h=dst.shape[1], b=dst.shape[2])
                nc.scalar.copy(dst, src).then_inc(S["proj_ev"], 1)

            def turn_out(nm, dst):
                n = TURNS.index(nm)
                act.wait_ge(S["turn_ps"], n + 1)
                src = ps_pt[:, n % 2]
                src = src.rearrange("p (h b n) -> p h b n", h=4, b=B) if len(dst.shape) == 4 else heads(src, P)
                nc.scalar.copy(dst, src).then_inc(S["turn_ev"], 1)

            def group_exp(n, scale):
                act.wait_ge(S["g_negmax"], n + 1)
                pr = (gp if n < AGROUPS else sp_)[:, n % 2]
                for i in range(4):
                    act_ = nc.scalar.activation(pr[:, i, :], pr[:, i, :], ACT.Exp, bias=gsum[:, n % 2, 1, i:i + 1], scale=scale,
                                                accum_out=gsum[:, n % 2, 2, i:i + 1])
                act_.then_inc(S["g_exp"], 1)

            def group_turn_out(n):
                act.wait_ge(S["g_t"], n + 1)
                if n >= 2:
                    act.wait_ge(S["g_pv"], n - 1)
                nc.scalar.copy((gpT if n < AGROUPS else spT)[:, n % 2], heads(ps_pt[:, n % 2], P)).then_inc(S["g_tev"], 1)

            def group_out(n):
                act.wait_ge(S["g_pv"], n + 1)
                if n < AGROUPS:
                    q = slice(64 * (n % 2), 64 * (n % 2) + 64)
                    dst = aoT[q, 4 * (n // 2):4 * (n // 2) + 4, :]
                    src = heads(proj_bank[n % 2][q, :], P)
                else:
                    dst = soT[:, 4 * (n - AGROUPS):4 * (n - AGROUPS) + 4, :]
                    src = heads(proj_bank[n % 2], P)
                nc.scalar.copy(dst, src).then_inc(S["g_oev"], 1)

            def groups(lo, hi, scale, name, values):
                group_exp(lo, scale)
                proj_out(name, values)
                for n in range(lo, hi):
                    if n + 1 < hi:
                        group_exp(n + 1, scale)
                    if n > lo:
                        group_out(n - 1)
                    group_turn_out(n)
                group_out(hi - 1)

            tokens_out(0)
            for nm, dst in (("aq", aq), ("ak", ak)):
                proj_out(nm + "0", dst[:, 0:512])
                proj_out(nm + "1", dst[:, 512:N])
            proj_out("av0", av[:, 0:512])
            for nm, dst in (("aq", aqT), ("ak", akT)):
                turn_out(nm + "0", dst[:, 0:4, :])
                turn_out(nm + "1", dst[:, 4:8, :])
            groups(0, AGROUPS, 0.125, "av1", av[:, 512:N])
            tokens_out(1)
            proj_out("gates", gates[:, 0:GATES])
            act.wait_ge(S["gate_max"], 1)
            nc.scalar.activation(tiny[:, 8:16], gates[:, 128:136], ACT.Exp, bias=tiny[:, 1:2], accum_out=tiny[:, 2:3])
            nc.scalar.activation(tiny[:, 4:5], tiny[:, 3:4], ACT.Exp, scale=-1.0).then_inc(S["gate_exp"], 1)
            act.wait_ge(S["gateT_ps"], 1)
            nc.scalar.copy(loraT, ps_pt[:, 0, 0:P]).then_inc(S["gateT_ev"], 1)
            tokens_out(2)
            for i in range(8):
                proj_out(f"xq{i}", sq[:, 512 * i:512 * i + 512])
                if i:
                    turn_out(f"xq{i - 1}", xqT[:, :, 4 * (i - 1):4 * i, :].rearrange("p b h n -> p h b n"))
            turn_out("xq7", xqT[:, :, 28:32, :].rearrange("p b h n -> p h b n"))
            proj_out("xk", keysT[:].rearrange("p h (b n) -> p h b n", b=B)[:, :, :, N:KV])
            for b in range(B):
                proj_out(f"xv_b{b}", vlat[0:64, b, :], 64)
            root = float(P) ** -0.5

            def x_exp(n):
                act.wait_ge(S["t_max"], n + 1)
                if n >= 2:
                    act.wait_ge(S["t_t"], 3 * n - 3)
                k = n % 2
                nc.scalar.activation(xp[:, k, 0:N], ps_s[:, k].rearrange("p g n -> p (g n)"), ACT.Exp, bias=xsum[:, k, 3:4],
                                     scale=root, accum_out=xsum[:, k, 4:5])
                nc.scalar.activation(xp[:, k, N:KV], xtail[:, n, :], ACT.Exp, bias=xsum[:, k, 3:4],
                                     scale=root, accum_out=xsum[:, k, 5:6]).then_inc(S["t_exp"], 1)

            def x_turn_out(n):
                for j in range(3):
                    m = 3 * n + j
                    if j == 0 and n >= 2:
                        act.wait_ge(S["t_pv"], n - 1)
                    act.wait_ge(S["t_t"], m + 1)
                    if j < 2:
                        nc.scalar.copy(xpT[:, n % 2, 4 * j:4 * j + 4, :], heads(ps_pt[:, j], P)).then_inc(S["t_tev"], 1)
                    else:
                        nc.scalar.copy(xpT[0:64, n % 2, 8, :], x_bank[n % 2][0:64, P:2 * P]).then_inc(S["t_tev"], 1)

            def x_out(n):
                b, h, g = n // 16, n // 4 % 4, n % 4
                act.wait_ge(S["t_pv"], n + 1)
                h0 = 8 * h + 2 * g
                nc.scalar.copy(soT[:, h0:h0 + 2, 64 * b:64 * b + 64], heads(x_bank[n % 2][:, 0:P], 64)).then_inc(S["t_oev"], 1)

            def tail_out(c):
                act.wait_ge(S["tail_ps"], c + 1)
                nc.scalar.copy(xtail[:, 8 * c:8 * c + 8, :], heads(x_bank[c % 2][:], 64)).then_inc(S["tail_ev"], 1)

            tail_out(0)
            x_exp(0)
            for c in range(1, 4):
                tail_out(c)
            act.wait_ge(S["tail_ev"], 4)
            for n in range(XTILES):
                x_turn_out(n)
                if n + 1 < XTILES:
                    x_exp(n + 1)
                x_out(n)
            tokens_out(3)
            for i in range(8):
                proj_out(f"sq{i}", sq[:, 512 * i:512 * i + 512])
                if i:
                    turn_out(f"sq{i - 1}", sqT[:, 4 * (i - 1):4 * i, :])
            turn_out("sq7", sqT[:, 28:32, :])
            proj_out("sk0", sk[:, 0:512])
            proj_out("sk1", sk[:, 512:N])
            proj_out("sv0", sv[:, 0:512])
            turn_out("sk0", skT[:, 0:4, :])
            turn_out("sk1", skT[:, 4:8, :])
            groups(AGROUPS, AGROUPS + SGROUPS, root, "sv1", sv[:, 512:N])
            tokens_out(4)
            proj_out("route", route[:, 0, :])
            act.wait_ge(S["route_max"], 1)
            nc.scalar.activation(route[:, 1, :], route[:, 1, :], ACT.Exp, bias=tiny[:, 1:2], accum_out=tiny[:, 2:3])\
                .then_inc(S["route_exp"], 1)
            act.wait_ge(S["routeT_ps"], 1)
            nc.scalar.copy(rT[0:64, :], ps_pt[0:64, 0, 0:P]).then_inc(S["routeT_ev"], 1)

        @block.vector
        def _(dve):
            chain = [0]

            def link(ins):
                chain[0] += 1
                ins.then_inc(S["vchain"], 1)
                dve.wait_ge(S["vchain"], chain[0])

            V = nc.vector

            pows = [0]

            def begin_stats(rows, stats):
                pows[0] += 1
                link(V.bn_aggr(small[0:rows, 0:2], stats))
                V.tensor_scalar(small[0:rows, 1:2], small[0:rows, 1:2], EPS, None, ALU.add).then_inc(S["pow_ready"], 1)

            def end_stats():
                dve.wait_ge(S["pow_done"], pows[0])

            def norm_stats(rows, stats):
                begin_stats(rows, stats)
                end_stats()

            V.memset(small[:, 8:9], -0.5)
            V.memset(small[:, 9:10], 0.0)
            V.memset(cnt[:], 0.0)
            link(V.memset(expo[:], 0x20000000))
            dve.wait_ge(S["coord_in"], 16)
            cv = coord.rearrange("p i (b k) -> p (i b) k", b=B)
            link(V.tensor_reduce(ext[:, 0, :], cv, AX.X, ALU.max))
            V.tensor_reduce(ext[:, 1, :], cv, AX.X, ALU.min, negate=True).then_inc(S["minmax_ready"], 1)
            dve.wait_ge(S["x_in"], 16)
            link(V.bn_stats(bstat[:, 0, :], x[:, 0:512]))
            link(V.bn_stats(bstat[:, 1, :], x[:, 512:1024]))
            norm_stats(P, bstat[:, 0:2, :])
            V.tensor_scalar(f0, x[:], small[:, 0:1], small[:, 2:3], ALU.subtract, ALU.mult).then_inc(S["ln_ready"], 1)
            dve.wait_ge(S["minmax_all"], 1)
            link(V.tensor_tensor(ext[:, 0, :], ext[:, 2, :], ext[:, 3, :], ALU.add))
            link(V.tensor_scalar(ext[:, 0, :], ext[:, 0, :], 1e-6, None, ALU.add))
            link(V.reciprocal(ext[:, 1, :], ext[:, 0, :]))
            link(V.tensor_scalar(ext[:, 1, :], ext[:, 1, :], 1023.0, None, ALU.mult))
            qv = quant.rearrange("p i (b k) -> p (i b) k", b=B)
            link(V.tensor_tensor(qv, cv, ext[:, 3, :].unsqueeze(2).broadcast_to([P, 6, NBLK]), ALU.add))
            link(V.tensor_tensor(qv, qv, ext[:, 1, :].unsqueeze(2).broadcast_to([P, 6, NBLK]), ALU.mult))
            link(V.tensor_copy(qint, quant))
            link(V.tensor_copy(qtmp, qint))
            link(V.tensor_tensor(coord, qtmp, quant, ALU.is_gt))
            link(V.tensor_tensor(qtmp, qtmp, coord, ALU.subtract))
            link(V.tensor_scalar(qtmp, qtmp, 0.0, 1023.0, ALU.max, ALU.min))
            link(V.tensor_copy(qint, qtmp))
            for m in range(METHODS):
                for i in range(3):
                    j = (0, 1, 2)[i] if m % 2 == 0 else (1, 0, 2)[i]
                    ins = V.tensor_copy(bits[:, i, m, :], qint[:, j, :])
            link(ins)
            h3 = [bits[:, i, 2:4, :].rearrange("p m n -> p (m n)") for i in range(3)]
            m_, t_, n_, s_, a_ = (bt[:, i, :] for i in range(5))
            for bit in range(9, 0, -1):
                low = (1 << bit) - 1
                for i in range(3):
                    if i:
                        V.tensor_tensor(t_, h3[0], h3[i], ALU.bitwise_xor)
                    link(V.tensor_scalar(m_, h3[i], 31 - bit, 31, ALU.logical_shift_left, ALU.arith_shift_right))
                    if i == 0:
                        link(V.scalar_tensor_tensor(h3[0], m_, low, h3[0], ALU.bitwise_and, ALU.bitwise_xor))
                        continue
                    V.scalar_tensor_tensor(a_, m_, low, h3[0], ALU.bitwise_and, ALU.bitwise_xor)
                    link(V.tensor_scalar(n_, m_, -1, None, ALU.bitwise_xor))
                    link(V.scalar_tensor_tensor(s_, t_, low, n_, ALU.bitwise_and, ALU.bitwise_and))
                    V.tensor_tensor(h3[0], a_, s_, ALU.bitwise_xor)
                    link(V.tensor_tensor(h3[i], h3[i], s_, ALU.bitwise_xor))
            link(V.tensor_tensor(h3[1], h3[1], h3[0], ALU.bitwise_xor))
            link(V.tensor_tensor(h3[2], h3[2], h3[1], ALU.bitwise_xor))
            link(V.tensor_scalar(t_, h3[2], 1, None, ALU.logical_shift_right))
            for sh in (1, 2, 4, 8):
                link(V.scalar_tensor_tensor(m_ if sh in (1, 4) else t_, t_ if sh in (1, 4) else m_, sh,
                                            t_ if sh in (1, 4) else m_, ALU.logical_shift_right, ALU.bitwise_xor))
            for i in range(3):
                ins = V.tensor_tensor(h3[i], h3[i], t_, ALU.bitwise_xor)
            link(ins)
            bv = bits.rearrange("p i m n -> p (i m n)")
            sv = spread.rearrange("p i m n -> p (i m n)")
            for sh, mask in ((16, 0x030000FF), (8, 0x0300F00F), (4, 0x030C30C3), (2, 0x09249249)):
                link(V.scalar_tensor_tensor(sv, bv, sh, bv, ALU.logical_shift_left, ALU.bitwise_or))
                link(V.tensor_scalar(bv, sv, mask, None, ALU.bitwise_and))
            b3 = [bits[:, i, :, :].rearrange("p m n -> p (m n)") for i in range(3)]
            link(V.scalar_tensor_tensor(key[:], b3[0], 1, b3[1], ALU.logical_shift_left, ALU.bitwise_or))
            link(V.scalar_tensor_tensor(spread[:, 0, :, :].rearrange("p m n -> p (m n)"), key[:], 1, b3[2],
                                        ALU.logical_shift_left, ALU.bitwise_or))
            V.tensor_tensor(key[:], spread[:, 0, :, :].rearrange("p m n -> p (m n)"), expo[:], ALU.add)\
                .then_inc(S["key_ready"], 1)
            dve.wait_ge(S["key_ready"], 1)
            keyf = key[:].bitcast(F32)
            dve.wait_ge(S["const_in"], CONSTS)
            ncount = [0]

            def spare(n):
                if ncount[0] >= 2:
                    dve.wait_ge(S["counted"], ncount[0] - 1)
                return junk[:, ncount[0] % 2, 0:n]

            def counted(ins):
                ncount[0] += 1
                ins.then_inc(S["counted"], 1)

            for b in range(B):
                dve.wait_ge(S["keyrow_in"], 16 * (b + 1))
                for m in range(METHODS):
                    for k in range(NBLK):
                        col = (m * B + b) * NBLK + k
                        mine = keyf[:, col:col + 1]
                        if k:
                            counted(V.tensor_scalar(spare(P * k), keyrow[:, m, 0:P * k], mine, 0.0, ALU.is_le, ALU.add,
                                                    accum_out=cnt[:, 0, col:col + 1]))
                        counted(V.tensor_scalar(spare(N - P * k), keyrow[:, m, P * k:N], mine, 0.0, ALU.is_lt, ALU.add,
                                                accum_out=cnt[:, 1, col:col + 1]))
                        counted(V.scalar_tensor_tensor(spare(P), keyrow[:, m, P * k:P * k + P], mine, lower[:],
                                                       ALU.is_equal, ALU.mult, accum_out=cnt[:, 2, col:col + 1]))
                dve.wait_ge(S["counted"], ncount[0])
                V.tensor_copy(small[:, 24:25], small[:, 8:9]).then_inc(S["keyrow_free"], 1)
                dve.wait_ge(S["keyrow_free"], b + 1)
                bc = [cnt[:, i, :].rearrange("p (m b k) -> p b m k", m=METHODS, b=B)[:, b] for i in range(3)]
                rk = ranks[:].rearrange("p (m b k) -> p b m k", m=METHODS, b=B)[:, b]
                ro = rankoff[:].rearrange("p (m b k) -> p b m k", m=METHODS, b=B)[:, b]
                ri = rowidx[:].rearrange("p (m b k) -> p b m k", m=METHODS, b=B)[:, b]
                link(V.tensor_tensor(rk, bc[0], bc[1], ALU.add))
                link(V.tensor_tensor(rk, rk, bc[2], ALU.add))
                link(V.tensor_tensor(rk, rk, ro, ALU.add))
                V.tensor_copy(ri, rk).then_inc(S["rank_ready"], 1)
            def centres(r):
                dve.wait_ge(S["fc_in"], 64 * (r + 1))
                if r:
                    dve.wait_ge(S["hc_ps"], 2 * r)
                    dve.wait_ge(S["ctx_ps"], 32)
                else:
                    dve.wait_ge(S["counted"], ncount[0])
                V.tensor_copy(c16, fc.rearrange("p t n -> p (t n)")).then_inc(S["c16_ready"], 1)
                dve.wait_ge(S["c16_ready"], r + 1)
                V.tensor_copy(c32[r], c16).then_inc(S["c32_ready"], 1)

            def first_windows(r):
                dve.wait_ge(S["fsT_ev"], 4 * (r + 1))
                for n in range(5):
                    V.tensor_copy(fh[:, :, n, 0:n + 6], fs[:, :, 5:n + 11])
                    if n < 4:
                        V.tensor_copy(fh[:, :, n, n + 6:KW], fs[:, :, n + 10:n + 11].broadcast_to([P, 2, 4 - n]))
                V.tensor_copy(fs[:, :, N + 5:N + 9], fs[:, :, N + 4:N + 5].broadcast_to([P, 2, 4])).then_inc(S["fh_ready"], 1)

            def run_statistics(r):
                dve.wait_ge(S["stats_ready"], r + 1)
                begin_stats(OUTC[r // B], bstat[0:OUTC[r // B], :, :])

            def run_output(r):
                layer, b = divmod(r, B)
                O = OUTC[layer]
                end_stats()
                link(V.tensor_scalar(mx[0:O, :], mx[0:O, :], small[0:O, 0:1], small[0:O, 2:3], ALU.subtract, ALU.mult))
                if layer == 0:
                    dve.wait_ge(S["fnT_ps"], 2 + b)
                    dve.wait_ge(S["feat_out"] if b else S["feat_out0"], 16)
                    dst = f0[0:64, :]
                else:
                    dve.wait_ge(S["fsp_ready"], RUNS if b else 1)
                    dst = f2[b]
                V.scalar_tensor_tensor(dst, mx[0:O, :], 0.2, mx[0:O, :], ALU.mult, ALU.max).then_inc(S["feat_ready"], 1)

            centres(0)
            first_windows(0)
            for r in range(RUNS):
                layer, b = divmod(r, B)
                O = OUTC[layer]
                base = BODIES * r

                def row_max(t, par):
                    u = base + t
                    st = isinstance(t, int)
                    dve.wait_ge(S["s_done"], u + 1)
                    if not st or u >= 2:
                        dve.wait_ge(S["exp_done"], 2 * u - 2)
                    V.tensor_reduce(negmax[0:GROWS, par, 0, :],
                                    ps_s[0:GROWS, par, :, 0:4 * GROWS].rearrange("p g (h n) -> p g h n", h=4),
                                    AX.X, ALU.max).then_inc(S["rowmax"], 1)
                    dve.wait_ge(S["rowmax"], u + 1)
                    V.tensor_scalar(negmax[0:GROWS, par, 1, :], negmax[0:GROWS, par, 0, :], -0.125, None, ALU.mult)\
                        .then_inc(S["negmax_ready"], 1)

                def sums(t, par, g):
                    u = base + t
                    st = isinstance(t, int)
                    if not st or u >= 2:
                        dve.wait_ge(S["norm_done"], 2 * u - 3 + g)
                    dve.wait_ge(S["exp_done"], 2 * u + g + 1)
                    i, o = (rsum[0:GROWS, par, w].rearrange("p (f g k) -> p f g k", f=2, g=2)[:, :, g] for w in range(2))
                    V.reciprocal(o, i).then_inc(S["recip_ready"], 1)

                def probs_out(t, par, g):
                    u = base + t
                    st = isinstance(t, int)
                    if not st or u >= 2:
                        dve.wait_ge(S["pv_done"], u - 1)
                    dve.wait_ge(S["t_done"], 2 * u + g + 1)
                    V.tensor_copy(pt_sb[0:GROWS, par, 4 * g:4 * g + 4, :],
                                  ps_pt[0:GROWS, g, 0:4 * GROWS].rearrange("p (h n) -> p h n", h=4)).then_inc(S["pt_ev"], 1)

                def add_centre(t, par):
                    u = base + t
                    n0 = n0_of(t)
                    dve.wait_ge(S["w_done"], u + 1)
                    if isinstance(t, int) and t == 0:
                        dve.wait_ge(S["hc_ready"], 2 * r + 2)
                    hcw = bass.AP(tensor=arena, offset=hc_off + n0, ap=[[ARENA, O], [1, BP], [0, KW]])
                    hv = hs[0:O, par, :].rearrange("p (n k) -> p n k", k=KW)
                    V.tensor_tensor(hv, ps_hg[0:O, :].rearrange("p (n k) -> p n k", k=KW), hcw, ALU.add)\
                        .then_inc(S["h_read"], 1)

                def statistics(t, par):
                    u = base + t
                    n0 = n0_of(t)
                    hv = hs[0:O, par, :].rearrange("p (n k) -> p n k", k=KW)
                    dve.wait_ge(S["h_read"], u + 1)
                    tail = isinstance(t, int) and t == BODIES - 1
                    lo = BCOLS - TAIL_NEW * KW if tail else 0
                    ti = t if isinstance(t, int) else t
                    V.bn_stats(bass.AP(tensor=bstat, offset=ti * 6, ap=[[BODIES * 6, O], [1, 6]]), hs[0:O, par, lo:BCOLS])
                    last = V.tensor_reduce(bass.AP(tensor=arena, offset=mx_off + n0, ap=[[ARENA, O], [1, BP]]), hv,
                                           AX.X, ALU.max)
                    if tail:
                        last.then_inc(S["stats_ready"], 1)

                p0 = base % 2
                p1 = 1 - p0
                row_max(0, p0)
                if r:
                    run_output(r - 1)
                row_max(1, p1)
                sums(0, p0, 0)
                sums(0, p0, 1)

                def step(t, par, last=False):
                    st = isinstance(t, int)
                    if not last:
                        sums(t + 1, 1 - par, 0)
                    probs_out(t, par, 0)
                    if not st or t + 2 < BODIES:
                        row_max(t + 2, par)
                    probs_out(t, par, 1)
                    if st and t == 0 and 0 < r <= B:
                        dve.wait_ge(S["fnT_ps"], 2 + r)
                        dve.wait_ge(scattered[r - 1], 16 * METHODS * NBLK)
                        q = slice(64 * (r - 1), 64 * r)
                        V.tensor_copy(fn[:, :, q], ps_o[:].rearrange("p (k c) -> p k c", k=NBLK)).then_inc(S["fnT_ev"], 1)
                    if not st or t >= 1:
                        add_centre(t - 1, 1 - par)
                    if not last:
                        sums(t + 1, 1 - par, 1)
                    if not st or t >= 1:
                        statistics(t - 1, 1 - par)

                step(0, p0)
                step(1, p1)
                step(2, p0)
                with dve.Fori(3, BODIES - 2, 2) as t:
                    step(t, p1)
                    step(t + 1, p0)
                step(BODIES - 2, p1)
                step(BODIES - 1, p0, last=True)
                if r + 1 < RUNS:
                    centres(r + 1)
                    first_windows(r + 1)
                add_centre(BODIES - 1, p0)
                statistics(BODIES - 1, p0)
                run_statistics(r)
            run_output(RUNS - 1)
            dve.wait_ge(S["h3_ps"], B)
            for h in range(2):
                link(V.bn_stats(bstat[:, h, :], ps_pt[:, h]))
            norm_stats(P, bstat[:, 0:2, :])
            link(V.tensor_scalar(mx, ps_pt[:].rearrange("p h n -> p (h n)"), small[:, 0:1], small[:, 2:3], ALU.subtract, ALU.mult))
            link(V.scalar_tensor_tensor(mx, mx, 0.2, mx, ALU.mult, ALU.max))
            V.tensor_tensor(x[:], x[:], mx, ALU.add).then_inc(S["x1_ready"], 1)
            def layer_norm(n):
                for h in range(2):
                    c = slice(512 * h, 512 * h + 512)
                    if n:
                        dve.wait_ge(S["y_ps"] if h else S["y0_ps"], n)
                        V.tensor_tensor(x[:, c], x[:, c], y_ps[h], ALU.add).then_inc(S["x_ready"] if h else S["x_half"], 1)
                        dve.wait_ge(S["x_ready"] if h else S["x_half"], n)
                    else:
                        dve.wait_ge(S["x1_ready"], 1)
                    link(V.bn_stats(bstat[:, h, :], x[:, c]))
                norm_stats(P, bstat[:, 0:2, :])
                if n:
                    dve.wait_ge(S["hT_ps"], 2 * n)
                for h in range(2):
                    c = slice(512 * h, 512 * h + 512)
                    V.tensor_scalar(hn[:, c], x[:, c], small[:, 0:1], small[:, 2:3], ALU.subtract, ALU.mult)\
                        .then_inc(S["hn_ready"], 1)

            def group_max(n, mask, scale):
                k = n % 2
                pr = (gp if n < AGROUPS else sp_)[:, k]
                dve.wait_ge(S["g_s"], n + 1)
                if n >= 2:
                    dve.wait_ge(S["g_t"], n - 1)
                V.tensor_tensor(pr, heads(ps_s[:, 0, k], P), mask.unsqueeze(1).broadcast_to([P, 4, P]), ALU.add)\
                    .then_inc(S["g_masked"], 1)
                dve.wait_ge(S["g_masked"], n + 1)
                V.tensor_reduce(gsum[:, k, 0, :], pr, AX.X, ALU.max).then_inc(S["g_max"], 1)
                dve.wait_ge(S["g_max"], n + 1)
                V.tensor_scalar(gsum[:, k, 1, :], gsum[:, k, 0, :], -scale, None, ALU.mult).then_inc(S["g_negmax"], 1)

            def group_recip(n):
                dve.wait_ge(S["g_exp"], n + 1)
                V.reciprocal(gsum[:, n % 2, 3, :], gsum[:, n % 2, 2, :]).then_inc(S["g_recip"], 1)

            def groups(lo, hi, mask, scale):
                group_max(lo, mask, scale)
                group_max(lo + 1, mask, scale)
                group_recip(lo)
                for n in range(lo + 1, hi):
                    group_recip(n)
                    if n + 1 < hi:
                        group_max(n + 1, mask, scale)

            layer_norm(0)
            dve.wait_ge(S["late_in"], LATE)
            for i, v in enumerate((aq, ak)):
                dve.wait_ge(S["proj_ev"], 2 * i + 2)
                v4 = v.rearrange("p (h n t) -> p h n t", h=16, t=2)
                r4 = rot.rearrange("p (h n t) -> p h n t", h=16, t=2)
                s4 = sinn.rearrange("p (n t) -> p n t", t=2)
                for e in range(2):
                    last = V.tensor_tensor(r4[:, :, :, e], v4[:, :, :, 1 - e], s4[:, :, e].unsqueeze(1).broadcast_to([P, 16, 32]), ALU.mult)
                link(last)
                v3, r3 = heads(v, 64), heads(rot, 64)
                link(V.tensor_tensor(v3, v3, cosn.unsqueeze(1).broadcast_to([P, 16, 64]), ALU.mult))
                V.tensor_tensor(v3, v3, r3, ALU.add).then_inc(S["rope_ready"], 1)
                dve.wait_ge(S["rope_ready"], i + 1)
            groups(0, AGROUPS, causal, 0.125)
            layer_norm(1)
            dve.wait_ge(S["hn_ready"], 4)
            link(V.tensor_tensor(x[:], x[:], bbase, ALU.add))
            dve.wait_ge(S["proj_ev"], PROJ.index("gates") + 1)
            link(V.tensor_reduce(tiny[:, 0:1], gates[:, 128:136], AX.X, ALU.max))
            link(V.tensor_scalar(tiny[:, 1:2], tiny[:, 0:1], -1.0, None, ALU.mult))
            V.tensor_tensor(tiny[:, 3:4], gates[:, 136:137], bthr, ALU.add).then_inc(S["gate_max"], 1)
            dve.wait_ge(S["gate_exp"], 1)
            link(V.reciprocal(tiny[:, 5:6], tiny[:, 2:3]))
            link(V.tensor_scalar(tiny[:, 6:7], tiny[:, 4:5], 1.0, None, ALU.add))
            link(V.reciprocal(tiny[:, 7:8], tiny[:, 6:7]))
            link(V.tensor_scalar(tiny[:, 7:8], tiny[:, 7:8], 0.125, None, ALU.mult))
            link(V.tensor_scalar(tiny[:, 8:16], tiny[:, 8:16], tiny[:, 5:6], tiny[:, 7:8], ALU.mult, ALU.subtract))
            link(V.tensor_scalar(tiny[:, 8:16], tiny[:, 8:16], 0.0, None, ALU.max))
            link(V.tensor_reduce(tiny[:, 16:17], tiny[:, 8:16], AX.X, ALU.add))
            link(V.tensor_scalar(tiny[:, 17:18], tiny[:, 16:17], 0.0, None, ALU.is_equal))
            link(V.tensor_tensor(tiny[:, 18:19], tiny[:, 16:17], tiny[:, 17:18], ALU.add))
            link(V.reciprocal(tiny[:, 19:20], tiny[:, 18:19]))
            link(V.tensor_scalar(tiny[:, 24:32], tiny[:, 8:16], tiny[:, 19:20], 2.0, ALU.mult, ALU.mult))
            V.tensor_tensor(heads(lora, 16), heads(gates[:, 0:128], 16), tiny[:, 24:32].unsqueeze(2).broadcast_to([P, 8, 16]),
                            ALU.mult).then_inc(S["gate_ready"], 1)
            layer_norm(2)
            root = float(P) ** -0.5

            def x_max(n):
                k = n % 2
                dve.wait_ge(S["t_s"], n + 1)
                link(V.tensor_reduce(xsum[:, k, 0:1], ps_s[:, k].rearrange("p g n -> p (g n)"), AX.X, ALU.max))
                V.tensor_scalar(xsum[:, k, 3:4], xsum[:, k, 0:1], tailmax[:, n:n + 1], -root, ALU.max, ALU.mult)\
                    .then_inc(S["t_max"], 1)

            def tail_max(c):
                dve.wait_ge(S["tail_ev"], c + 1)
                V.tensor_reduce(tailmax[:, 8 * c:8 * c + 8], xtail[:, 8 * c:8 * c + 8, :], AX.X, ALU.max)\
                    .then_inc(S["tail_max"], 1)

            def x_norm(n):
                k = n % 2
                dve.wait_ge(S["t_exp"], n + 1)
                link(V.tensor_tensor(xsum[:, k, 6:7], xsum[:, k, 4:5], xsum[:, k, 5:6], ALU.add))
                link(V.reciprocal(xsum[:, k, 7:8], xsum[:, k, 6:7]))
                V.tensor_scalar(xp[:, k, :], xp[:, k, :], xsum[:, k, 7:8], None, ALU.mult).then_inc(S["t_norm"], 1)

            tail_max(0)
            dve.wait_ge(S["tail_max"], 1)
            x_max(0)
            for c in range(1, 4):
                tail_max(c)
            dve.wait_ge(S["tail_max"], 4)
            x_max(1)
            x_norm(0)
            for n in range(1, XTILES):
                x_norm(n)
                if n + 1 < XTILES:
                    x_max(n + 1)
            layer_norm(3)
            dve.wait_ge(S["late2_in"], LATE2)
            groups(AGROUPS, AGROUPS + SGROUPS, samebatch, root)
            layer_norm(4)
            dve.wait_ge(S["proj_ev"], PROJ.index("route") + 1)
            link(V.tensor_tensor(route[:, 1, :], route[:, 0, :], rbias, ALU.add))
            link(V.tensor_reduce(tiny[:, 0:1], route[:, 1, :], AX.X, ALU.max))
            V.tensor_scalar(tiny[:, 1:2], tiny[:, 0:1], -1.0, None, ALU.mult).then_inc(S["route_max"], 1)
            dve.wait_ge(S["route_exp"], 1)
            link(V.reciprocal(tiny[:, 3:4], tiny[:, 2:3]))
            link(V.tensor_scalar(route[:, 2, :], route[:, 1, :], tiny[:, 3:4], None, ALU.mult))
            link(V.max(tiny[:, 8:16], route[:, 2, :]))
            link(V.match_replace(route[:, 3, :], tiny[:, 8:16], route[:, 2, :], -1.0))
            link(V.tensor_reduce(tiny[:, 16:17], tiny[:, 8:16], AX.X, ALU.add))
            V.scalar_tensor_tensor(route[:, 4, :], route[:, 3, :], 0.0, route[:, 2, :], ALU.is_lt, ALU.mult)\
                .then_inc(S["route_ready"], 1)
            dve.wait_ge(S["y_ps"], 5)
            for h in range(2):
                c = slice(512 * h, 512 * h + 512)
                last = V.scalar_tensor_tensor(hn[:, c], hn[:, c], tiny[:, 16:17], y_ps[h], ALU.mult, ALU.add)
            link(last)
            V.tensor_tensor(x[:], x[:], hn, ALU.add).then_inc(S["x_ready"], 1)


def host(inputs):
    import numpy as np
    g = {k: np.asarray(v) for k, v in inputs.items()}
    a = {}
    a["x"] = g["x"].reshape(P, N)
    ctx = g["ctx_4096"]
    a["coords"] = ctx[:, 0:3, :].reshape(B, 3, NBLK, P).transpose(3, 1, 0, 2).reshape(P, 3, 16)
    a["ident"] = np.eye(P, dtype=np.float32)
    a["identh"] = np.eye(P, dtype=np.float16)
    a["lower"] = np.tril(np.ones((P, P), np.float32), -1)
    a["rankoff"] = np.tile(np.repeat(np.arange(METHODS) * N, 16)[None].astype(np.float32), (P, 1))
    own = np.arange(GROWS) // KW == np.arange(GP)[:, None]
    root = BIG ** 0.5
    ml = np.full((GP + 1, GROWS), root, np.float16)
    ml[:GP] = own * root
    mr = np.full((GP + 1, GROWS), -root, np.float16)
    mr[:GP] = own * root
    ml, mr = (np.tile(np.pad(m, ((0, 64 - GP - 1), (0, 0))), (2, 1)) for m in (ml, mr))
    a["maskl"] = ml
    a["maskr"] = np.tile(mr, (1, 4))
    perms = ([2, 0, 3, 1], [1, 3, 0, 2])

    def lin(w, perm, lo):
        w = w.reshape(P, 2 * C, METHODS)[:, lo:lo + C, :]
        w = w[:, :, [perm.index(m) for m in range(METHODS)]]
        return w.reshape(P, 2, 2, 16, METHODS).transpose(0, 1, 2, 4, 3).reshape(P, 256)

    ws = [g["L0_xattn_W_lin1"], g["L0_xattn_W_lin2"]]
    a["wlin_n"] = np.stack([lin(w, p, C) for w, p in zip(ws, perms)], 1)
    a["wlin_c"] = np.stack([lin(w, p, 0) for w, p in zip(ws, perms)], 1)
    a["blin"] = np.stack([g["L0_xattn_b_lin1"], g["L0_xattn_b_lin2"]], 1)
    a["wconv0"] = g["L0_xattn_W_conv1"].T
    a["wconv1"] = g["L0_xattn_W_conv2"].T
    a["wconv3"] = g["L0_xattn_W_conv3"].T.reshape(2, P, 64).transpose(1, 0, 2)

    def wide(w):
        n = w.shape[1]
        return w.reshape(KT, P, n // 512, 512).transpose(2, 1, 0, 3).reshape(n // 512, P, CHUNK)

    def tall(w):
        return w.reshape(-1, 4, P, N).transpose(0, 2, 1, 3).reshape(-1, P, CHUNK)

    cx = ctx.reshape(B * N, N)
    chunks = [wide(g["L1_xattn_Wk"]), wide(g["L1_xattn_Wv"]), wide(cx.T),
              wide(g["L0_attn_wq"].T), wide(g["L0_attn_wk"].T), wide(g["L0_attn_wv"].T), tall(g["L0_attn_wo"].T),
              wide(g["L0_ffn_W_base"].T), wide(g["L1_xattn_Wq"]), tall(g["L1_xattn_Wo"]),
              wide(g["L1_attn_wq"].T), wide(g["L1_attn_wk"].T), wide(g["L1_attn_wv"].T), tall(g["L1_attn_wo"].T)]
    freq = (1.0 / np.float32(10000.0) ** (np.arange(0, 64, 2, dtype=np.float32) / np.float32(64))).astype(np.float32)
    ang = np.arange(C, dtype=np.float32)[:, None] * freq[None]
    a["cosn"] = np.tile(np.repeat(np.cos(ang), 2, axis=1), (B, 1))
    a["sinn"] = np.tile(np.repeat(np.sin(ang), 2, axis=1) * np.tile(np.array([-1, 1], np.float32), 32), (B, 1))
    tok = np.arange(P)
    same = tok[:, None] // C == tok[None] // C
    a["samebatch"] = np.where(same, 0, -BIG).astype(np.float32)
    a["causal"] = np.where(same & (tok[:, None] >= tok[None]), 0, -BIG).astype(np.float32)
    wg = np.concatenate([g["L0_ffn_A_w"].reshape(P, N), g["L0_ffn_W_gate"], g["L0_ffn_W_thr"][None]], 0)
    a["wgate"] = wg.T.reshape(KT, P, GATES).transpose(1, 0, 2)
    a["lora_b"] = g["L0_ffn_B_w"].transpose(0, 2, 1).reshape(P, N)
    a["bbase"] = g["L0_ffn_b_base"]
    a["bthr"] = g["L0_ffn_b_thr"]
    a["wroute"] = g["L1_ffn_router_weight"].T.reshape(KT, P, 64).transpose(1, 0, 2)
    a["rbias"] = g["L1_ffn_router_bias"]
    a["ebias"] = g["L1_ffn_expert_bias"]
    a["wstream"] = np.concatenate(chunks, 0)
    return {k: np.ascontiguousarray(v) for k, v in a.items()}


def kernel(**inputs):
    import numpy as _np
    import concourse.bacc as _bacc
    from concourse.bass_utils import run_bass_kernel_spmd as _run

    nc = _bacc.Bacc("TRN2", target_bir_lowering=False, num_devices=1)
    arrays = host(inputs)
    args = {n: nc.dram_tensor(f"in_{n}", v.shape, mybir.dt.from_np(v.dtype), kind="ExternalInput").ap()
            for n, v in arrays.items()}
    out = nc.dram_tensor("out_0", (P, N), F32, kind="ExternalOutput").ap()
    build(nc, args, out)
    r = _run(nc, [{f"in_{n}": v for n, v in arrays.items()}], core_ids=[0])
    return r.results[0]["out_0"].reshape(B, C, N)
```
